# Optimizing a Trainium2 kernel written in Bass

```python
import numpy as np
import jax
import jax.numpy as jnp

def _softmax(x, axis=-1):
    return jax.nn.softmax(x, axis=axis)

def _gelu(x):
    return jax.nn.gelu(x, approximate=True)

def _silu(x):
    return jax.nn.silu(x)

def _sigmoid(x):
    return jax.nn.sigmoid(x)

def _layernorm(x, axis=-1, eps=1e-05):
    m = jnp.mean(x, axis=axis, keepdims=True)
    v = jnp.var(x, axis=axis, keepdims=True)
    return (x - m) / jnp.sqrt(v + eps)

def _scatter_add(tgt, idx, src, axis=0):
    return tgt.at[idx].add(src)

def _segment_sum(src, seg, n):
    return jax.ops.segment_sum(src, seg, n)
kernel_name = 'mk_xattn_seq_d4_seqx_r4_2c7375'

def setup_inputs(seed: int=0):
    np.random.seed(seed)
    _w = jnp.asarray

    def _rec_inputs():
        import jax
        import jax.numpy as jnp
        _rk = jax.random.key(seed)
        x = -0.0002928 + 1 * jax.random.normal(jax.random.fold_in(_rk, 1), (4, 1024, 256), jnp.float32)
        _lenS = 1024 - jax.random.randint(jax.random.fold_in(_rk, 7), (4,), 0, max(1, 1024 // 4) + 1, jnp.int32)
        _lenS2 = 64 - jax.random.randint(jax.random.fold_in(_rk, 8), (4,), 0, max(1, 64 // 4) + 1, jnp.int32)
        _ctx_1024P = jax.random.normal(jax.random.fold_in(_rk, 11), (4, 16, 256), jnp.float32)
        _ctx_1024c = jax.random.dirichlet(jax.random.fold_in(_rk, 511), 0.3 * jnp.ones((16,), jnp.float32), (4, 64))
        _ctx_1024t = jnp.einsum('bsk,bkd->bsd', _ctx_1024c, _ctx_1024P)
        _ctx_1024t = _ctx_1024t * jax.lax.rsqrt(jnp.mean(jnp.square(_ctx_1024t)) + 1e-12) * 0.953939
        ctx_1024 = -1.39393e-06 + 0.999914 * (_ctx_1024t + 0.3 * jax.random.normal(jax.random.fold_in(_rk, 611), (4, 64, 256), jnp.float32))
        return (x, ctx_1024)
    x, ctx_1024 = _rec_inputs()

    def _L0_xattn_setup():
        import jax, jax.numpy as jnp
        import numpy as np
        D_MODEL = 256
        N_HEADS = 16
        D_K = D_MODEL // N_HEADS
        LN_EPS = 1e-05

        def _attention(query, key_value, W_qkv, b_qkv, W_o, b_o, ln_gamma, ln_beta):
            B, Sq, _ = query.shape
            Skv = key_value.shape[1]
            Wq, Wk, Wv = (W_qkv[:D_MODEL], W_qkv[D_MODEL:2 * D_MODEL], W_qkv[2 * D_MODEL:])
            bq, bk, bv = (b_qkv[:D_MODEL], b_qkv[D_MODEL:2 * D_MODEL], b_qkv[2 * D_MODEL:])
            Q = (query @ Wq.T + bq).reshape(B, Sq, N_HEADS, D_K).transpose(0, 2, 1, 3)
            K = (key_value @ Wk.T + bk).reshape(B, Skv, N_HEADS, D_K).transpose(0, 2, 1, 3)
            V = (key_value @ Wv.T + bv).reshape(B, Skv, N_HEADS, D_K).transpose(0, 2, 1, 3)
            scores = jnp.einsum('bhqd,bhkd->bhqk', Q.astype(jnp.float32), K.astype(jnp.float32))
            scores = scores / np.sqrt(D_K)
            attn = jax.nn.softmax(scores, axis=-1)
            context = jnp.einsum('bhqk,bhkd->bhqd', attn, V.astype(jnp.float32)).astype(query.dtype)
            context = context.transpose(0, 2, 1, 3).reshape(B, Sq, D_MODEL)
            output = context @ W_o.T + b_o
            x = output + query
            mu = jnp.mean(x, axis=-1, keepdims=True)
            var = jnp.mean(jnp.square(x - mu), axis=-1, keepdims=True)
            return (x - mu) / jnp.sqrt(var + LN_EPS) * ln_gamma + ln_beta
        key = jax.random.key(seed)
        ks = jax.random.split(key, 8)
        B, Sq, Skv = (2, 512, 512)
        scale = 1.0 / np.sqrt(D_MODEL)
        return {'query': jax.random.normal(ks[0], (B, Sq, D_MODEL), dtype=jnp.float32), 'key_value': jax.random.normal(ks[1], (B, Skv, D_MODEL), dtype=jnp.float32), 'W_qkv': jax.random.normal(ks[2], (3 * D_MODEL, D_MODEL), dtype=jnp.float32) * scale, 'b_qkv': jax.random.normal(ks[3], (3 * D_MODEL,), dtype=jnp.float32) * 0.01, 'W_o': jax.random.normal(ks[4], (D_MODEL, D_MODEL), dtype=jnp.float32) * scale, 'b_o': jax.random.normal(ks[5], (D_MODEL,), dtype=jnp.float32) * 0.01, 'ln_gamma': jnp.ones((D_MODEL,), dtype=jnp.float32), 'ln_beta': jnp.zeros((D_MODEL,), dtype=jnp.float32)}
    _L0_xattn_all = _L0_xattn_setup()
    _L0_xattn_in = {k: v for k, v in _L0_xattn_all.items() if k in ('W_qkv', 'b_qkv', 'W_o', 'b_o', 'ln_gamma', 'ln_beta')}
    del _L0_xattn_all

    def _L1_xattn_setup():
        import jax, jax.numpy as jnp
        import numpy as np
        D, H, E, K, DFF = (256, 16, 8, 2, 1024)
        B, L, T = (4, 128, 512)
        EPS = 1e-05

        def _xavier(key, shape):
            fan_in, fan_out = (shape[-1], shape[-2])
            a = jnp.sqrt(6.0 / (fan_in + fan_out))
            return jax.random.uniform(key, shape, jnp.float32, -a, a)

        def _ln(x, g, b):
            m = x.mean(-1, keepdims=True)
            v = ((x - m) ** 2).mean(-1, keepdims=True)
            return (x - m) / jnp.sqrt(v + EPS) * g + b

        def _mha(q_in, kv_in, in_w, in_b, out_w, out_b):
            wq, wk, wv = jnp.split(in_w, 3, axis=0)
            bq, bk, bv = jnp.split(in_b, 3, axis=0)
            dh = D // H

            def heads(x, w, b):
                y = x @ w.T + b
                return y.reshape(x.shape[0], x.shape[1], H, dh).transpose(0, 2, 1, 3)
            q = heads(q_in, wq, bq)
            k = heads(kv_in, wk, bk)
            v = heads(kv_in, wv, bv)
            scores = jnp.einsum('bhqd,bhkd->bhqk', q, k) / jnp.sqrt(jnp.float32(dh))
            attn = jax.nn.softmax(scores, axis=-1)
            out = jnp.einsum('bhqk,bhkd->bhqd', attn, v)
            out = out.transpose(0, 2, 1, 3).reshape(q_in.shape[0], q_in.shape[1], D)
            return out @ out_w.T + out_b

        def _fuse_moe(x, ln_g, ln_b, rw, rb, fc1_w, fc1_b, fc2_w, fc2_b):
            h = _ln(x, ln_g, ln_b)
            logits = h @ rw.T + rb
            vals, idx = jax.lax.top_k(logits, K)
            gates = jax.nn.softmax(vals, axis=-1)
            N = x.shape[0] * x.shape[1]
            hf = h.reshape(N, D)
            h1 = jax.nn.gelu(jnp.einsum('nd,efd->enf', hf, fc1_w) + fc1_b[:, None, :], approximate=False)
            eo = jnp.einsum('enf,edf->end', h1, fc2_w) + fc2_b[:, None, :]
            idx_f = idx.reshape(N, K)
            gates_f = gates.reshape(N, K)
            gathered = eo[idx_f, jnp.arange(N)[:, None], :]
            mixed = (gathered * gates_f[..., None]).sum(axis=1).reshape(x.shape)
            return x + mixed
        key = jax.random.key(seed)
        ks = jax.random.split(key, 16)
        inp = {'latents': jax.random.normal(ks[0], (B, L, D), jnp.float32), 'tokens': jax.random.normal(ks[1], (B, T, D), jnp.float32), 'sa_ln_g': jnp.ones((D,)), 'sa_ln_b': jnp.zeros((D,)), 'sa_in_w': _xavier(ks[2], (3 * D, D)), 'sa_in_b': jnp.zeros((3 * D,)), 'sa_out_w': _xavier(ks[3], (D, D)), 'sa_out_b': jnp.zeros((D,)), 'ca_q_ln_g': jnp.ones((D,)), 'ca_q_ln_b': jnp.zeros((D,)), 'ca_kv_ln_g': jnp.ones((D,)), 'ca_kv_ln_b': jnp.zeros((D,)), 'ca_in_w': _xavier(ks[4], (3 * D, D)), 'ca_in_b': jnp.zeros((3 * D,)), 'ca_out_w': _xavier(ks[5], (D, D)), 'ca_out_b': jnp.zeros((D,)), 'moe_ln_g': jnp.ones((D,)), 'moe_ln_b': jnp.zeros((D,)), 'router_w': _xavier(ks[6], (E, D)), 'router_b': jnp.zeros((E,)), 'e_fc1_w': jax.vmap(lambda k: _xavier(k, (DFF, D)))(jax.random.split(ks[7], E)), 'e_fc1_b': jnp.zeros((E, DFF)), 'e_fc2_w': jax.vmap(lambda k: _xavier(k, (D, DFF)))(jax.random.split(ks[8], E)), 'e_fc2_b': jnp.zeros((E, D))}
        return inp
    _L1_xattn_all = _L1_xattn_setup()
    _L1_xattn_in = {k: v for k, v in _L1_xattn_all.items() if k in ('sa_ln_g', 'sa_ln_b', 'sa_in_w', 'sa_in_b', 'sa_out_w', 'sa_out_b', 'ca_q_ln_g', 'ca_q_ln_b', 'ca_kv_ln_g', 'ca_kv_ln_b', 'ca_in_w', 'ca_in_b', 'ca_out_w', 'ca_out_b', 'moe_ln_g', 'moe_ln_b', 'router_w', 'router_b', 'e_fc1_w', 'e_fc1_b', 'e_fc2_w', 'e_fc2_b')}
    del _L1_xattn_all

    def _L2_xattn_setup():
        import jax, jax.numpy as jnp
        import numpy as np
        D, H, DFF, MD = (256, 16, 1024, 128)
        B, TS, TT = (8, 128, 128)
        EPS = 1e-06

        def _ln(x, s, b):
            m = jnp.mean(x, axis=-1, keepdims=True)
            v = jnp.mean((x - m) ** 2, axis=-1, keepdims=True)
            return (x - m) * jax.lax.rsqrt(v + EPS) * s + b

        def _rel_bias(emb, qlen, klen):
            q = jnp.arange(qlen)[:, None]
            k = jnp.arange(klen)[None, :]
            rp = k - q
            bucket = jnp.where(rp < 0, jnp.minimum(-rp, MD - 1), jnp.minimum(rp, MD - 1) + MD)
            return emb[bucket].transpose(2, 0, 1)

        def _mha(xq, xkv, w_in, b_in, w_out, b_out, bias):
            Bq, Tq, _ = xq.shape
            Tk = xkv.shape[1]
            hd = D // H
            wq, wk, wv = jnp.split(w_in, 3, axis=0)
            bq, bk, bv = jnp.split(b_in, 3, axis=0)
            q = (xq @ wq.T + bq).reshape(Bq, Tq, H, hd).transpose(0, 2, 1, 3)
            k = (xkv @ wk.T + bk).reshape(Bq, Tk, H, hd).transpose(0, 2, 1, 3)
            v = (xkv @ wv.T + bv).reshape(Bq, Tk, H, hd).transpose(0, 2, 1, 3)
            scores = jnp.einsum('bhqd,bhkd->bhqk', q, k) / jnp.sqrt(jnp.asarray(hd, xq.dtype))
            scores = scores + bias[None]
            attn = jax.nn.softmax(scores, axis=-1)
            out = jnp.einsum('bhqk,bhkd->bhqd', attn, v)
            out = out.transpose(0, 2, 1, 3).reshape(Bq, Tq, D)
            return out @ w_out.T + b_out
        key = jax.random.key(seed)
        ks = jax.random.split(key, 40)
        std = 0.02

        def n(i, shape):
            return jax.random.normal(ks[i], shape, dtype=jnp.float32) * std
        return {'src': jax.random.normal(ks[0], (B, TS, D), dtype=jnp.float32), 'tgt': jax.random.normal(ks[1], (B, TT, D), dtype=jnp.float32), 'enc_in_w': n(2, (3 * D, D)), 'enc_in_b': jnp.zeros((3 * D,)), 'enc_out_w': n(3, (D, D)), 'enc_out_b': jnp.zeros((D,)), 'enc_ff1_w': n(4, (DFF, D)), 'enc_ff1_b': jnp.zeros((DFF,)), 'enc_ff2_w': n(5, (D, DFF)), 'enc_ff2_b': jnp.zeros((D,)), 'enc_n1_s': jnp.ones((D,)), 'enc_n1_b': jnp.zeros((D,)), 'enc_n2_s': jnp.ones((D,)), 'enc_n2_b': jnp.zeros((D,)), 'enc_rel': n(6, (2 * MD, H)), 'dec_sa_in_w': n(7, (3 * D, D)), 'dec_sa_in_b': jnp.zeros((3 * D,)), 'dec_sa_out_w': n(8, (D, D)), 'dec_sa_out_b': jnp.zeros((D,)), 'dec_ca_in_w': n(9, (3 * D, D)), 'dec_ca_in_b': jnp.zeros((3 * D,)), 'dec_ca_out_w': n(10, (D, D)), 'dec_ca_out_b': jnp.zeros((D,)), 'dec_ff1_w': n(11, (DFF, D)), 'dec_ff1_b': jnp.zeros((DFF,)), 'dec_ff2_w': n(12, (D, DFF)), 'dec_ff2_b': jnp.zeros((D,)), 'dec_n1_s': jnp.ones((D,)), 'dec_n1_b': jnp.zeros((D,)), 'dec_n2_s': jnp.ones((D,)), 'dec_n2_b': jnp.zeros((D,)), 'dec_n3_s': jnp.ones((D,)), 'dec_n3_b': jnp.zeros((D,)), 'dec_rel_self': n(13, (2 * MD, H)), 'dec_rel_cross': n(14, (2 * MD, H))}
    _L2_xattn_all = _L2_xattn_setup()
    _L2_xattn_in = {k: v for k, v in _L2_xattn_all.items() if k in ('enc_in_w', 'enc_in_b', 'enc_out_w', 'enc_out_b', 'enc_ff1_w', 'enc_ff1_b', 'enc_ff2_w', 'enc_ff2_b', 'enc_n1_s', 'enc_n1_b', 'enc_n2_s', 'enc_n2_b', 'enc_rel', 'dec_sa_in_w', 'dec_sa_in_b', 'dec_sa_out_w', 'dec_sa_out_b', 'dec_ca_in_w', 'dec_ca_in_b', 'dec_ca_out_w', 'dec_ca_out_b', 'dec_ff1_w', 'dec_ff1_b', 'dec_ff2_w', 'dec_ff2_b', 'dec_n1_s', 'dec_n1_b', 'dec_n2_s', 'dec_n2_b', 'dec_n3_s', 'dec_n3_b', 'dec_rel_self', 'dec_rel_cross')}
    del _L2_xattn_all

    def _L3_xattn_setup():
        import jax, jax.numpy as jnp
        import numpy as np
        B, LX, LY = (2, 512, 512)
        E, H = (256, 16)
        HD = E // H
        FF = 1024
        EPS = 1e-05

        def _rope_tables(L, d):
            inv = 1.0 / 10000.0 ** (jnp.arange(0, d, 2, dtype=jnp.float32) / d)
            t = jnp.arange(L, dtype=jnp.float32)
            f = jnp.outer(t, inv)
            return (jnp.cos(f), jnp.sin(f))

        def _apply_rope(x, cos, sin):
            d2 = x.shape[-1] // 2
            x1, x2 = (x[..., :d2], x[..., d2:])
            c = cos[None, :, None, :]
            s = sin[None, :, None, :]
            return jnp.concatenate([x1 * c - x2 * s, x2 * c + x1 * s], axis=-1)

        def _ln(x, g, b):
            m = jnp.mean(x, axis=-1, keepdims=True)
            v = jnp.var(x, axis=-1, keepdims=True)
            return (x - m) / jnp.sqrt(v + EPS) * g + b

        def _attn(q, k, v, causal):
            s = jnp.einsum('blhd,bmhd->bhlm', q, k)
            if causal:
                Lq, Lk = (s.shape[2], s.shape[3])
                mask = jnp.tril(jnp.ones((Lq, Lk), dtype=bool))
                s = jnp.where(mask, s, -jnp.inf)
            p = jax.nn.softmax(s, axis=-1)
            return jnp.einsum('bhlm,bmhd->blhd', p, v)

        def _forward(x, y, ln1_g, ln1_b, sa_wq, sa_bq, sa_wk, sa_bk, sa_wv, sa_bv, sa_wo, sa_bo, ln2_g, ln2_b, ca_wq, ca_bq, ca_wk, ca_bk, ca_wv, ca_bv, ca_wo, ca_bo, ln3_g, ln3_b, fc1_w, fc1_b, fc2_w, fc2_b):
            Bx, Lx, _ = x.shape
            Ly = y.shape[1]
            cos, sin = _rope_tables(max(Lx, Ly), HD)
            scale = HD ** (-0.5)
            h = _ln(x, ln1_g, ln1_b)
            q = (h @ sa_wq + sa_bq).reshape(Bx, Lx, H, HD) * scale
            k = (h @ sa_wk + sa_bk).reshape(Bx, Lx, H, HD)
            v = (h @ sa_wv + sa_bv).reshape(Bx, Lx, H, HD)
            q = _apply_rope(q, cos[:Lx], sin[:Lx])
            k = _apply_rope(k, cos[:Lx], sin[:Lx])
            a = _attn(q, k, v, causal=True).reshape(Bx, Lx, E)
            x = x + (a @ sa_wo + sa_bo)
            h = _ln(x, ln2_g, ln2_b)
            q = (h @ ca_wq + ca_bq).reshape(Bx, Lx, H, HD) * scale
            k = (y @ ca_wk + ca_bk).reshape(Bx, Ly, H, HD)
            v = (y @ ca_wv + ca_bv).reshape(Bx, Ly, H, HD)
            q = _apply_rope(q, cos[:Lx], sin[:Lx])
            k = _apply_rope(k, cos[:Ly], sin[:Ly])
            a = _attn(q, k, v, causal=False).reshape(Bx, Lx, E)
            x = x + (a @ ca_wo + ca_bo)
            h = _ln(x, ln3_g, ln3_b)
            return x + (jax.nn.gelu(h @ fc1_w + fc1_b) @ fc2_w + fc2_b)
        key = jax.random.key(seed)
        ks = jax.random.split(key, 16)

        def w(k, *s):
            return jax.random.normal(k, s, jnp.float32) * 0.02
        z = lambda *s: jnp.zeros(s, jnp.float32)
        o = lambda *s: jnp.ones(s, jnp.float32)
        return {'x': jax.random.normal(ks[0], (B, LX, E), jnp.float32), 'y': jax.random.normal(ks[1], (B, LY, E), jnp.float32), 'ln1_g': o(E), 'ln1_b': z(E), 'sa_wq': w(ks[2], E, E), 'sa_bq': z(E), 'sa_wk': w(ks[3], E, E), 'sa_bk': z(E), 'sa_wv': w(ks[4], E, E), 'sa_bv': z(E), 'sa_wo': w(ks[5], E, E), 'sa_bo': z(E), 'ln2_g': o(E), 'ln2_b': z(E), 'ca_wq': w(ks[6], E, E), 'ca_bq': z(E), 'ca_wk': w(ks[7], E, E), 'ca_bk': z(E), 'ca_wv': w(ks[8], E, E), 'ca_bv': z(E), 'ca_wo': w(ks[9], E, E), 'ca_bo': z(E), 'ln3_g': o(E), 'ln3_b': z(E), 'fc1_w': w(ks[10], E, FF), 'fc1_b': z(FF), 'fc2_w': w(ks[11], FF, E), 'fc2_b': z(E)}
    _L3_xattn_all = _L3_xattn_setup()
    _L3_xattn_in = {k: v for k, v in _L3_xattn_all.items() if k in ('ln1_g', 'ln1_b', 'sa_wq', 'sa_bq', 'sa_wk', 'sa_bk', 'sa_wv', 'sa_bv', 'sa_wo', 'sa_bo', 'ln2_g', 'ln2_b', 'ca_wq', 'ca_bq', 'ca_wk', 'ca_bk', 'ca_wv', 'ca_bv', 'ca_wo', 'ca_bo', 'ln3_g', 'ln3_b', 'fc1_w', 'fc1_b', 'fc2_w', 'fc2_b')}
    del _L3_xattn_all
    return {'x': x, 'ctx_1024': ctx_1024, 'L0_xattn_W_qkv': _L0_xattn_in['W_qkv'], 'L0_xattn_b_qkv': _L0_xattn_in['b_qkv'], 'L0_xattn_W_o': _L0_xattn_in['W_o'], 'L0_xattn_b_o': _L0_xattn_in['b_o'], 'L0_xattn_ln_gamma': _L0_xattn_in['ln_gamma'], 'L0_xattn_ln_beta': _L0_xattn_in['ln_beta'], 'L1_xattn_sa_ln_g': _L1_xattn_in['sa_ln_g'], 'L1_xattn_sa_ln_b': _L1_xattn_in['sa_ln_b'], 'L1_xattn_sa_in_w': _L1_xattn_in['sa_in_w'], 'L1_xattn_sa_in_b': _L1_xattn_in['sa_in_b'], 'L1_xattn_sa_out_w': _L1_xattn_in['sa_out_w'], 'L1_xattn_sa_out_b': _L1_xattn_in['sa_out_b'], 'L1_xattn_ca_q_ln_g': _L1_xattn_in['ca_q_ln_g'], 'L1_xattn_ca_q_ln_b': _L1_xattn_in['ca_q_ln_b'], 'L1_xattn_ca_kv_ln_g': _L1_xattn_in['ca_kv_ln_g'], 'L1_xattn_ca_kv_ln_b': _L1_xattn_in['ca_kv_ln_b'], 'L1_xattn_ca_in_w': _L1_xattn_in['ca_in_w'], 'L1_xattn_ca_in_b': _L1_xattn_in['ca_in_b'], 'L1_xattn_ca_out_w': _L1_xattn_in['ca_out_w'], 'L1_xattn_ca_out_b': _L1_xattn_in['ca_out_b'], 'L1_xattn_moe_ln_g': _L1_xattn_in['moe_ln_g'], 'L1_xattn_moe_ln_b': _L1_xattn_in['moe_ln_b'], 'L1_xattn_router_w': _L1_xattn_in['router_w'], 'L1_xattn_router_b': _L1_xattn_in['router_b'], 'L1_xattn_e_fc1_w': _L1_xattn_in['e_fc1_w'], 'L1_xattn_e_fc1_b': _L1_xattn_in['e_fc1_b'], 'L1_xattn_e_fc2_w': _L1_xattn_in['e_fc2_w'], 'L1_xattn_e_fc2_b': _L1_xattn_in['e_fc2_b'], 'L2_xattn_enc_in_w': _L2_xattn_in['enc_in_w'], 'L2_xattn_enc_in_b': _L2_xattn_in['enc_in_b'], 'L2_xattn_enc_out_w': _L2_xattn_in['enc_out_w'], 'L2_xattn_enc_out_b': _L2_xattn_in['enc_out_b'], 'L2_xattn_enc_ff1_w': _L2_xattn_in['enc_ff1_w'], 'L2_xattn_enc_ff1_b': _L2_xattn_in['enc_ff1_b'], 'L2_xattn_enc_ff2_w': _L2_xattn_in['enc_ff2_w'], 'L2_xattn_enc_ff2_b': _L2_xattn_in['enc_ff2_b'], 'L2_xattn_enc_n1_s': _L2_xattn_in['enc_n1_s'], 'L2_xattn_enc_n1_b': _L2_xattn_in['enc_n1_b'], 'L2_xattn_enc_n2_s': _L2_xattn_in['enc_n2_s'], 'L2_xattn_enc_n2_b': _L2_xattn_in['enc_n2_b'], 'L2_xattn_enc_rel': _L2_xattn_in['enc_rel'], 'L2_xattn_dec_sa_in_w': _L2_xattn_in['dec_sa_in_w'], 'L2_xattn_dec_sa_in_b': _L2_xattn_in['dec_sa_in_b'], 'L2_xattn_dec_sa_out_w': _L2_xattn_in['dec_sa_out_w'], 'L2_xattn_dec_sa_out_b': _L2_xattn_in['dec_sa_out_b'], 'L2_xattn_dec_ca_in_w': _L2_xattn_in['dec_ca_in_w'], 'L2_xattn_dec_ca_in_b': _L2_xattn_in['dec_ca_in_b'], 'L2_xattn_dec_ca_out_w': _L2_xattn_in['dec_ca_out_w'], 'L2_xattn_dec_ca_out_b': _L2_xattn_in['dec_ca_out_b'], 'L2_xattn_dec_ff1_w': _L2_xattn_in['dec_ff1_w'], 'L2_xattn_dec_ff1_b': _L2_xattn_in['dec_ff1_b'], 'L2_xattn_dec_ff2_w': _L2_xattn_in['dec_ff2_w'], 'L2_xattn_dec_ff2_b': _L2_xattn_in['dec_ff2_b'], 'L2_xattn_dec_n1_s': _L2_xattn_in['dec_n1_s'], 'L2_xattn_dec_n1_b': _L2_xattn_in['dec_n1_b'], 'L2_xattn_dec_n2_s': _L2_xattn_in['dec_n2_s'], 'L2_xattn_dec_n2_b': _L2_xattn_in['dec_n2_b'], 'L2_xattn_dec_n3_s': _L2_xattn_in['dec_n3_s'], 'L2_xattn_dec_n3_b': _L2_xattn_in['dec_n3_b'], 'L2_xattn_dec_rel_self': _L2_xattn_in['dec_rel_self'], 'L2_xattn_dec_rel_cross': _L2_xattn_in['dec_rel_cross'], 'L3_xattn_ln1_g': _L3_xattn_in['ln1_g'], 'L3_xattn_ln1_b': _L3_xattn_in['ln1_b'], 'L3_xattn_sa_wq': _L3_xattn_in['sa_wq'], 'L3_xattn_sa_bq': _L3_xattn_in['sa_bq'], 'L3_xattn_sa_wk': _L3_xattn_in['sa_wk'], 'L3_xattn_sa_bk': _L3_xattn_in['sa_bk'], 'L3_xattn_sa_wv': _L3_xattn_in['sa_wv'], 'L3_xattn_sa_bv': _L3_xattn_in['sa_bv'], 'L3_xattn_sa_wo': _L3_xattn_in['sa_wo'], 'L3_xattn_sa_bo': _L3_xattn_in['sa_bo'], 'L3_xattn_ln2_g': _L3_xattn_in['ln2_g'], 'L3_xattn_ln2_b': _L3_xattn_in['ln2_b'], 'L3_xattn_ca_wq': _L3_xattn_in['ca_wq'], 'L3_xattn_ca_bq': _L3_xattn_in['ca_bq'], 'L3_xattn_ca_wk': _L3_xattn_in['ca_wk'], 'L3_xattn_ca_bk': _L3_xattn_in['ca_bk'], 'L3_xattn_ca_wv': _L3_xattn_in['ca_wv'], 'L3_xattn_ca_bv': _L3_xattn_in['ca_bv'], 'L3_xattn_ca_wo': _L3_xattn_in['ca_wo'], 'L3_xattn_ca_bo': _L3_xattn_in['ca_bo'], 'L3_xattn_ln3_g': _L3_xattn_in['ln3_g'], 'L3_xattn_ln3_b': _L3_xattn_in['ln3_b'], 'L3_xattn_fc1_w': _L3_xattn_in['fc1_w'], 'L3_xattn_fc1_b': _L3_xattn_in['fc1_b'], 'L3_xattn_fc2_w': _L3_xattn_in['fc2_w'], 'L3_xattn_fc2_b': _L3_xattn_in['fc2_b']}

def reference(x, ctx_1024, L0_xattn_W_qkv, L0_xattn_b_qkv, L0_xattn_W_o, L0_xattn_b_o, L0_xattn_ln_gamma, L0_xattn_ln_beta, L1_xattn_sa_ln_g, L1_xattn_sa_ln_b, L1_xattn_sa_in_w, L1_xattn_sa_in_b, L1_xattn_sa_out_w, L1_xattn_sa_out_b, L1_xattn_ca_q_ln_g, L1_xattn_ca_q_ln_b, L1_xattn_ca_kv_ln_g, L1_xattn_ca_kv_ln_b, L1_xattn_ca_in_w, L1_xattn_ca_in_b, L1_xattn_ca_out_w, L1_xattn_ca_out_b, L1_xattn_moe_ln_g, L1_xattn_moe_ln_b, L1_xattn_router_w, L1_xattn_router_b, L1_xattn_e_fc1_w, L1_xattn_e_fc1_b, L1_xattn_e_fc2_w, L1_xattn_e_fc2_b, L2_xattn_enc_in_w, L2_xattn_enc_in_b, L2_xattn_enc_out_w, L2_xattn_enc_out_b, L2_xattn_enc_ff1_w, L2_xattn_enc_ff1_b, L2_xattn_enc_ff2_w, L2_xattn_enc_ff2_b, L2_xattn_enc_n1_s, L2_xattn_enc_n1_b, L2_xattn_enc_n2_s, L2_xattn_enc_n2_b, L2_xattn_enc_rel, L2_xattn_dec_sa_in_w, L2_xattn_dec_sa_in_b, L2_xattn_dec_sa_out_w, L2_xattn_dec_sa_out_b, L2_xattn_dec_ca_in_w, L2_xattn_dec_ca_in_b, L2_xattn_dec_ca_out_w, L2_xattn_dec_ca_out_b, L2_xattn_dec_ff1_w, L2_xattn_dec_ff1_b, L2_xattn_dec_ff2_w, L2_xattn_dec_ff2_b, L2_xattn_dec_n1_s, L2_xattn_dec_n1_b, L2_xattn_dec_n2_s, L2_xattn_dec_n2_b, L2_xattn_dec_n3_s, L2_xattn_dec_n3_b, L2_xattn_dec_rel_self, L2_xattn_dec_rel_cross, L3_xattn_ln1_g, L3_xattn_ln1_b, L3_xattn_sa_wq, L3_xattn_sa_bq, L3_xattn_sa_wk, L3_xattn_sa_bk, L3_xattn_sa_wv, L3_xattn_sa_bv, L3_xattn_sa_wo, L3_xattn_sa_bo, L3_xattn_ln2_g, L3_xattn_ln2_b, L3_xattn_ca_wq, L3_xattn_ca_bq, L3_xattn_ca_wk, L3_xattn_ca_bk, L3_xattn_ca_wv, L3_xattn_ca_bv, L3_xattn_ca_wo, L3_xattn_ca_bo, L3_xattn_ln3_g, L3_xattn_ln3_b, L3_xattn_fc1_w, L3_xattn_fc1_b, L3_xattn_fc2_w, L3_xattn_fc2_b):
    import jax
    import jax.numpy as jnp

    def _L0_xattn_ref(query, key_value, W_qkv, b_qkv, W_o, b_o, ln_gamma, ln_beta):
        import jax, jax.numpy as jnp
        import numpy as np
        D_MODEL = 256
        N_HEADS = 16
        D_K = D_MODEL // N_HEADS
        LN_EPS = 1e-05

        def _attention(query, key_value, W_qkv, b_qkv, W_o, b_o, ln_gamma, ln_beta):
            B, Sq, _ = query.shape
            Skv = key_value.shape[1]
            Wq, Wk, Wv = (W_qkv[:D_MODEL], W_qkv[D_MODEL:2 * D_MODEL], W_qkv[2 * D_MODEL:])
            bq, bk, bv = (b_qkv[:D_MODEL], b_qkv[D_MODEL:2 * D_MODEL], b_qkv[2 * D_MODEL:])
            Q = (query @ Wq.T + bq).reshape(B, Sq, N_HEADS, D_K).transpose(0, 2, 1, 3)
            K = (key_value @ Wk.T + bk).reshape(B, Skv, N_HEADS, D_K).transpose(0, 2, 1, 3)
            V = (key_value @ Wv.T + bv).reshape(B, Skv, N_HEADS, D_K).transpose(0, 2, 1, 3)
            scores = jnp.einsum('bhqd,bhkd->bhqk', Q.astype(jnp.float32), K.astype(jnp.float32))
            scores = scores / np.sqrt(D_K)
            attn = jax.nn.softmax(scores, axis=-1)
            context = jnp.einsum('bhqk,bhkd->bhqd', attn, V.astype(jnp.float32)).astype(query.dtype)
            context = context.transpose(0, 2, 1, 3).reshape(B, Sq, D_MODEL)
            output = context @ W_o.T + b_o
            x = output + query
            mu = jnp.mean(x, axis=-1, keepdims=True)
            var = jnp.mean(jnp.square(x - mu), axis=-1, keepdims=True)
            return (x - mu) / jnp.sqrt(var + LN_EPS) * ln_gamma + ln_beta
        return _attention(query, key_value, W_qkv, b_qkv, W_o, b_o, ln_gamma, ln_beta)

    def _L1_xattn_ref(latents, tokens, sa_ln_g, sa_ln_b, sa_in_w, sa_in_b, sa_out_w, sa_out_b, ca_q_ln_g, ca_q_ln_b, ca_kv_ln_g, ca_kv_ln_b, ca_in_w, ca_in_b, ca_out_w, ca_out_b, moe_ln_g, moe_ln_b, router_w, router_b, e_fc1_w, e_fc1_b, e_fc2_w, e_fc2_b):
        import jax, jax.numpy as jnp
        import numpy as np
        D, H, E, K, DFF = (256, 16, 8, 2, 1024)
        B, L, T = (4, 128, 512)
        EPS = 1e-05

        def _xavier(key, shape):
            fan_in, fan_out = (shape[-1], shape[-2])
            a = jnp.sqrt(6.0 / (fan_in + fan_out))
            return jax.random.uniform(key, shape, jnp.float32, -a, a)

        def _ln(x, g, b):
            m = x.mean(-1, keepdims=True)
            v = ((x - m) ** 2).mean(-1, keepdims=True)
            return (x - m) / jnp.sqrt(v + EPS) * g + b

        def _mha(q_in, kv_in, in_w, in_b, out_w, out_b):
            wq, wk, wv = jnp.split(in_w, 3, axis=0)
            bq, bk, bv = jnp.split(in_b, 3, axis=0)
            dh = D // H

            def heads(x, w, b):
                y = x @ w.T + b
                return y.reshape(x.shape[0], x.shape[1], H, dh).transpose(0, 2, 1, 3)
            q = heads(q_in, wq, bq)
            k = heads(kv_in, wk, bk)
            v = heads(kv_in, wv, bv)
            scores = jnp.einsum('bhqd,bhkd->bhqk', q, k) / jnp.sqrt(jnp.float32(dh))
            attn = jax.nn.softmax(scores, axis=-1)
            out = jnp.einsum('bhqk,bhkd->bhqd', attn, v)
            out = out.transpose(0, 2, 1, 3).reshape(q_in.shape[0], q_in.shape[1], D)
            return out @ out_w.T + out_b

        def _fuse_moe(x, ln_g, ln_b, rw, rb, fc1_w, fc1_b, fc2_w, fc2_b):
            h = _ln(x, ln_g, ln_b)
            logits = h @ rw.T + rb
            vals, idx = jax.lax.top_k(logits, K)
            gates = jax.nn.softmax(vals, axis=-1)
            N = x.shape[0] * x.shape[1]
            hf = h.reshape(N, D)
            h1 = jax.nn.gelu(jnp.einsum('nd,efd->enf', hf, fc1_w) + fc1_b[:, None, :], approximate=False)
            eo = jnp.einsum('enf,edf->end', h1, fc2_w) + fc2_b[:, None, :]
            idx_f = idx.reshape(N, K)
            gates_f = gates.reshape(N, K)
            gathered = eo[idx_f, jnp.arange(N)[:, None], :]
            mixed = (gathered * gates_f[..., None]).sum(axis=1).reshape(x.shape)
            return x + mixed
        q = _ln(latents, sa_ln_g, sa_ln_b)
        x = latents + _mha(q, q, sa_in_w, sa_in_b, sa_out_w, sa_out_b)
        qc = _ln(x, ca_q_ln_g, ca_q_ln_b)
        kv = _ln(tokens, ca_kv_ln_g, ca_kv_ln_b)
        x = x + _mha(qc, kv, ca_in_w, ca_in_b, ca_out_w, ca_out_b)
        return _fuse_moe(x, moe_ln_g, moe_ln_b, router_w, router_b, e_fc1_w, e_fc1_b, e_fc2_w, e_fc2_b)

    def _L2_xattn_ref(src, tgt, enc_in_w, enc_in_b, enc_out_w, enc_out_b, enc_ff1_w, enc_ff1_b, enc_ff2_w, enc_ff2_b, enc_n1_s, enc_n1_b, enc_n2_s, enc_n2_b, enc_rel, dec_sa_in_w, dec_sa_in_b, dec_sa_out_w, dec_sa_out_b, dec_ca_in_w, dec_ca_in_b, dec_ca_out_w, dec_ca_out_b, dec_ff1_w, dec_ff1_b, dec_ff2_w, dec_ff2_b, dec_n1_s, dec_n1_b, dec_n2_s, dec_n2_b, dec_n3_s, dec_n3_b, dec_rel_self, dec_rel_cross):
        import jax, jax.numpy as jnp
        import numpy as np
        D, H, DFF, MD = (256, 16, 1024, 128)
        B, TS, TT = (8, 128, 128)
        EPS = 1e-06

        def _ln(x, s, b):
            m = jnp.mean(x, axis=-1, keepdims=True)
            v = jnp.mean((x - m) ** 2, axis=-1, keepdims=True)
            return (x - m) * jax.lax.rsqrt(v + EPS) * s + b

        def _rel_bias(emb, qlen, klen):
            q = jnp.arange(qlen)[:, None]
            k = jnp.arange(klen)[None, :]
            rp = k - q
            bucket = jnp.where(rp < 0, jnp.minimum(-rp, MD - 1), jnp.minimum(rp, MD - 1) + MD)
            return emb[bucket].transpose(2, 0, 1)

        def _mha(xq, xkv, w_in, b_in, w_out, b_out, bias):
            Bq, Tq, _ = xq.shape
            Tk = xkv.shape[1]
            hd = D // H
            wq, wk, wv = jnp.split(w_in, 3, axis=0)
            bq, bk, bv = jnp.split(b_in, 3, axis=0)
            q = (xq @ wq.T + bq).reshape(Bq, Tq, H, hd).transpose(0, 2, 1, 3)
            k = (xkv @ wk.T + bk).reshape(Bq, Tk, H, hd).transpose(0, 2, 1, 3)
            v = (xkv @ wv.T + bv).reshape(Bq, Tk, H, hd).transpose(0, 2, 1, 3)
            scores = jnp.einsum('bhqd,bhkd->bhqk', q, k) / jnp.sqrt(jnp.asarray(hd, xq.dtype))
            scores = scores + bias[None]
            attn = jax.nn.softmax(scores, axis=-1)
            out = jnp.einsum('bhqk,bhkd->bhqd', attn, v)
            out = out.transpose(0, 2, 1, 3).reshape(Bq, Tq, D)
            return out @ w_out.T + b_out
        Ts, Tt = (src.shape[1], tgt.shape[1])
        eb = _rel_bias(enc_rel, Ts, Ts)
        x = src
        x = x + _mha(_ln(x, enc_n1_s, enc_n1_b), _ln(x, enc_n1_s, enc_n1_b), enc_in_w, enc_in_b, enc_out_w, enc_out_b, eb)
        h = _ln(x, enc_n2_s, enc_n2_b)
        x = x + (jax.nn.relu(h @ enc_ff1_w.T + enc_ff1_b) @ enc_ff2_w.T + enc_ff2_b)
        memory = x
        causal = jnp.where(jnp.arange(Tt)[None, :] > jnp.arange(Tt)[:, None], -jnp.inf, 0.0)
        sb = _rel_bias(dec_rel_self, Tt, Tt) + causal[None]
        cb = _rel_bias(dec_rel_cross, Tt, Ts)
        y = tgt
        yn = _ln(y, dec_n1_s, dec_n1_b)
        y = y + _mha(yn, yn, dec_sa_in_w, dec_sa_in_b, dec_sa_out_w, dec_sa_out_b, sb)
        y = y + _mha(_ln(y, dec_n2_s, dec_n2_b), memory, dec_ca_in_w, dec_ca_in_b, dec_ca_out_w, dec_ca_out_b, cb)
        h = _ln(y, dec_n3_s, dec_n3_b)
        y = y + (jax.nn.relu(h @ dec_ff1_w.T + dec_ff1_b) @ dec_ff2_w.T + dec_ff2_b)
        return y

    def _L3_xattn_ref(x, y, ln1_g, ln1_b, sa_wq, sa_bq, sa_wk, sa_bk, sa_wv, sa_bv, sa_wo, sa_bo, ln2_g, ln2_b, ca_wq, ca_bq, ca_wk, ca_bk, ca_wv, ca_bv, ca_wo, ca_bo, ln3_g, ln3_b, fc1_w, fc1_b, fc2_w, fc2_b):
        import jax, jax.numpy as jnp
        import numpy as np
        B, LX, LY = (2, 512, 512)
        E, H = (256, 16)
        HD = E // H
        FF = 1024
        EPS = 1e-05

        def _rope_tables(L, d):
            inv = 1.0 / 10000.0 ** (jnp.arange(0, d, 2, dtype=jnp.float32) / d)
            t = jnp.arange(L, dtype=jnp.float32)
            f = jnp.outer(t, inv)
            return (jnp.cos(f), jnp.sin(f))

        def _apply_rope(x, cos, sin):
            d2 = x.shape[-1] // 2
            x1, x2 = (x[..., :d2], x[..., d2:])
            c = cos[None, :, None, :]
            s = sin[None, :, None, :]
            return jnp.concatenate([x1 * c - x2 * s, x2 * c + x1 * s], axis=-1)

        def _ln(x, g, b):
            m = jnp.mean(x, axis=-1, keepdims=True)
            v = jnp.var(x, axis=-1, keepdims=True)
            return (x - m) / jnp.sqrt(v + EPS) * g + b

        def _attn(q, k, v, causal):
            s = jnp.einsum('blhd,bmhd->bhlm', q, k)
            if causal:
                Lq, Lk = (s.shape[2], s.shape[3])
                mask = jnp.tril(jnp.ones((Lq, Lk), dtype=bool))
                s = jnp.where(mask, s, -jnp.inf)
            p = jax.nn.softmax(s, axis=-1)
            return jnp.einsum('bhlm,bmhd->blhd', p, v)

        def _forward(x, y, ln1_g, ln1_b, sa_wq, sa_bq, sa_wk, sa_bk, sa_wv, sa_bv, sa_wo, sa_bo, ln2_g, ln2_b, ca_wq, ca_bq, ca_wk, ca_bk, ca_wv, ca_bv, ca_wo, ca_bo, ln3_g, ln3_b, fc1_w, fc1_b, fc2_w, fc2_b):
            Bx, Lx, _ = x.shape
            Ly = y.shape[1]
            cos, sin = _rope_tables(max(Lx, Ly), HD)
            scale = HD ** (-0.5)
            h = _ln(x, ln1_g, ln1_b)
            q = (h @ sa_wq + sa_bq).reshape(Bx, Lx, H, HD) * scale
            k = (h @ sa_wk + sa_bk).reshape(Bx, Lx, H, HD)
            v = (h @ sa_wv + sa_bv).reshape(Bx, Lx, H, HD)
            q = _apply_rope(q, cos[:Lx], sin[:Lx])
            k = _apply_rope(k, cos[:Lx], sin[:Lx])
            a = _attn(q, k, v, causal=True).reshape(Bx, Lx, E)
            x = x + (a @ sa_wo + sa_bo)
            h = _ln(x, ln2_g, ln2_b)
            q = (h @ ca_wq + ca_bq).reshape(Bx, Lx, H, HD) * scale
            k = (y @ ca_wk + ca_bk).reshape(Bx, Ly, H, HD)
            v = (y @ ca_wv + ca_bv).reshape(Bx, Ly, H, HD)
            q = _apply_rope(q, cos[:Lx], sin[:Lx])
            k = _apply_rope(k, cos[:Ly], sin[:Ly])
            a = _attn(q, k, v, causal=False).reshape(Bx, Lx, E)
            x = x + (a @ ca_wo + ca_bo)
            h = _ln(x, ln3_g, ln3_b)
            return x + (jax.nn.gelu(h @ fc1_w + fc1_b) @ fc2_w + fc2_b)
        return _forward(x, y, ln1_g, ln1_b, sa_wq, sa_bq, sa_wk, sa_bk, sa_wv, sa_bv, sa_wo, sa_bo, ln2_g, ln2_b, ca_wq, ca_bq, ca_wk, ca_bk, ca_wv, ca_bv, ca_wo, ca_bo, ln3_g, ln3_b, fc1_w, fc1_b, fc2_w, fc2_b)
    x = _L0_xattn_ref(x, ctx_1024, L0_xattn_W_qkv, L0_xattn_b_qkv, L0_xattn_W_o, L0_xattn_b_o, L0_xattn_ln_gamma, L0_xattn_ln_beta)
    x = _L1_xattn_ref(x, ctx_1024, L1_xattn_sa_ln_g, L1_xattn_sa_ln_b, L1_xattn_sa_in_w, L1_xattn_sa_in_b, L1_xattn_sa_out_w, L1_xattn_sa_out_b, L1_xattn_ca_q_ln_g, L1_xattn_ca_q_ln_b, L1_xattn_ca_kv_ln_g, L1_xattn_ca_kv_ln_b, L1_xattn_ca_in_w, L1_xattn_ca_in_b, L1_xattn_ca_out_w, L1_xattn_ca_out_b, L1_xattn_moe_ln_g, L1_xattn_moe_ln_b, L1_xattn_router_w, L1_xattn_router_b, L1_xattn_e_fc1_w, L1_xattn_e_fc1_b, L1_xattn_e_fc2_w, L1_xattn_e_fc2_b)
    x = _L2_xattn_ref(ctx_1024, x, L2_xattn_enc_in_w, L2_xattn_enc_in_b, L2_xattn_enc_out_w, L2_xattn_enc_out_b, L2_xattn_enc_ff1_w, L2_xattn_enc_ff1_b, L2_xattn_enc_ff2_w, L2_xattn_enc_ff2_b, L2_xattn_enc_n1_s, L2_xattn_enc_n1_b, L2_xattn_enc_n2_s, L2_xattn_enc_n2_b, L2_xattn_enc_rel, L2_xattn_dec_sa_in_w, L2_xattn_dec_sa_in_b, L2_xattn_dec_sa_out_w, L2_xattn_dec_sa_out_b, L2_xattn_dec_ca_in_w, L2_xattn_dec_ca_in_b, L2_xattn_dec_ca_out_w, L2_xattn_dec_ca_out_b, L2_xattn_dec_ff1_w, L2_xattn_dec_ff1_b, L2_xattn_dec_ff2_w, L2_xattn_dec_ff2_b, L2_xattn_dec_n1_s, L2_xattn_dec_n1_b, L2_xattn_dec_n2_s, L2_xattn_dec_n2_b, L2_xattn_dec_n3_s, L2_xattn_dec_n3_b, L2_xattn_dec_rel_self, L2_xattn_dec_rel_cross)
    x = _L3_xattn_ref(x, ctx_1024, L3_xattn_ln1_g, L3_xattn_ln1_b, L3_xattn_sa_wq, L3_xattn_sa_bq, L3_xattn_sa_wk, L3_xattn_sa_bk, L3_xattn_sa_wv, L3_xattn_sa_bv, L3_xattn_sa_wo, L3_xattn_sa_bo, L3_xattn_ln2_g, L3_xattn_ln2_b, L3_xattn_ca_wq, L3_xattn_ca_bq, L3_xattn_ca_wk, L3_xattn_ca_bk, L3_xattn_ca_wv, L3_xattn_ca_bv, L3_xattn_ca_wo, L3_xattn_ca_bo, L3_xattn_ln3_g, L3_xattn_ln3_b, L3_xattn_fc1_w, L3_xattn_fc1_b, L3_xattn_fc2_w, L3_xattn_fc2_b)
    return x

_drawn_inputs = setup_inputs


def setup_inputs(seed=0):
    import zlib

    import numpy as np

    out = dict(_drawn_inputs(seed))
    spreads = {'L0_xattn_ln_gamma': (1.0, 0.2),
     'L0_xattn_ln_beta': (0.0, 0.1),
     'L1_xattn_sa_ln_g': (1.0, 0.2),
     'L1_xattn_sa_ln_b': (0.0, 0.1),
     'L1_xattn_sa_in_b': (0.0, 0.1),
     'L1_xattn_sa_out_b': (0.0, 0.1),
     'L1_xattn_ca_q_ln_g': (1.0, 0.6),
     'L1_xattn_ca_q_ln_b': (0.0, 0.573),
     'L1_xattn_ca_kv_ln_g': (1.0, 0.2),
     'L1_xattn_ca_kv_ln_b': (0.0, 0.1),
     'L1_xattn_ca_in_b': (0.0, 0.1),
     'L1_xattn_ca_out_b': (0.0, 0.1),
     'L1_xattn_moe_ln_g': (1.0, 0.2),
     'L1_xattn_moe_ln_b': (0.0, 0.1),
     'L1_xattn_router_b': (0.0, 0.1),
     'L1_xattn_e_fc1_b': (0.0, 0.1),
     'L1_xattn_e_fc2_b': (0.0, 0.1),
     'L2_xattn_enc_in_b': (0.0, 0.8),
     'L2_xattn_enc_out_b': (0.0, 0.8),
     'L2_xattn_enc_ff1_b': (0.0, 0.8),
     'L2_xattn_enc_ff2_b': (0.0, 0.8),
     'L2_xattn_enc_n1_s': (1.0, 0.6),
     'L2_xattn_enc_n1_b': (0.0, 0.8),
     'L2_xattn_enc_n2_s': (1.0, 0.6),
     'L2_xattn_enc_n2_b': (0.0, 0.8),
     'L2_xattn_dec_sa_in_b': (0.0, 0.297),
     'L2_xattn_dec_sa_out_b': (0.0, 0.1),
     'L2_xattn_dec_ca_in_b': (0.0, 0.33),
     'L2_xattn_dec_ca_out_b': (0.0, 0.1),
     'L2_xattn_dec_ff1_b': (0.0, 0.347),
     'L2_xattn_dec_ff2_b': (0.0, 0.1),
     'L2_xattn_dec_n1_s': (1.0, 0.6),
     'L2_xattn_dec_n1_b': (0.0, 0.8),
     'L2_xattn_dec_n2_s': (1.0, 0.6),
     'L2_xattn_dec_n2_b': (0.0, 0.8),
     'L2_xattn_dec_n3_s': (1.0, 0.6),
     'L2_xattn_dec_n3_b': (0.0, 0.79),
     'L3_xattn_ln1_g': (1.0, 0.6),
     'L3_xattn_ln1_b': (0.0, 0.8),
     'L3_xattn_sa_bq': (0.0, 2.0),
     'L3_xattn_sa_bk': (0.0, 2.0),
     'L3_xattn_sa_bv': (0.0, 0.359),
     'L3_xattn_sa_bo': (0.0, 0.1),
     'L3_xattn_ln2_g': (1.0, 0.6),
     'L3_xattn_ln2_b': (0.0, 0.8),
     'L3_xattn_ca_bq': (0.0, 2.0),
     'L3_xattn_ca_bk': (0.0, 2.0),
     'L3_xattn_ca_bv': (0.0, 0.33),
     'L3_xattn_ca_bo': (0.0, 0.1),
     'L3_xattn_ln3_g': (1.0, 0.6),
     'L3_xattn_ln3_b': (0.0, 0.8),
     'L3_xattn_fc1_b': (0.0, 0.275),
     'L3_xattn_fc2_b': (0.0, 0.1)}
    factors = {'L0_xattn_b_qkv': 3.203,
     'L0_xattn_b_o': 2.816,
     'L2_xattn_enc_in_w': 8.0,
     'L2_xattn_enc_out_w': 8.0,
     'L2_xattn_enc_ff1_w': 8.0,
     'L2_xattn_enc_ff2_w': 5.595,
     'L2_xattn_enc_rel': 42.792,
     'L2_xattn_dec_rel_self': 200.0,
     'L2_xattn_dec_rel_cross': 51.871,
     'L3_xattn_sa_wq': 8.0,
     'L3_xattn_sa_wk': 8.0,
     'L3_xattn_ca_wq': 8.0,
     'L3_xattn_ca_wk': 8.0}
    for name, (base, spread) in spreads.items():
        noise = np.random.default_rng([zlib.crc32(name.encode()), seed]).standard_normal(out[name].shape)
        drawn = base * np.exp(spread * noise) if base else spread * noise
        out[name] = jnp.asarray(drawn.astype(out[name].dtype))
    for name, factor in factors.items():
        out[name] = (out[name] * factor).astype(out[name].dtype)
    return out
```

```python
from contextlib import ExitStack

import numpy as np
import concourse.bass as bass
from concourse import mybir

F32 = mybir.dt.float32
BF16 = mybir.dt.bfloat16
F16 = mybir.dt.float16
U32 = mybir.dt.uint32
ALU = mybir.AluOpType
ACT = mybir.ActivationFunctionType
AX = mybir.AxisListType

P = 128
D = 256
KT = D // P
H = 16
DK = D // H
HT = P // DK
B = 4
SQ = 1024
SC = 64
NT = B * SQ // P
TB = SQ // P
FF = 1024
FT = FF // P
E = 8
CH = 512
SCALE = DK ** -0.5
PIECES = 6
KS = PIECES * DK
Q_PART = (0, 0, 0, 1, 1, 2)
K_PART = (0, 1, 2, 0, 1, 0)
VW = 3 * DK + 1
PW = 2 * (DK + 1)
NEG = -3.0e38
MASKED = -1.0e30


class Signal:

    def __init__(self, sem):
        self.sem, self.base, self.total = sem, 0, 0

    def at(self, n):
        return self.base + n


class Signals:

    def __init__(self, nc, ctx):
        self.nc, self.ctx, self.known = nc, ctx, {}

    def __call__(self, name, total):
        if name not in self.known:
            self.known[name] = Signal(self.ctx.enter_context(self.nc.semaphore(name)))
        s = self.known[name]
        assert s.total == 0, name
        s.total = total
        return s

    def phase_over(self):
        for s in self.known.values():
            s.base, s.total = s.base + s.total, 0


class Phase:

    def __init__(self, nc, signals, name):
        self.nc, self.signals, self.name = nc, signals, name
        self.ctx = ExitStack()

    def __enter__(self):
        return self

    def __exit__(self, *a):
        self.ctx.close()
        self.signals.phase_over()
        return False

    def sb(self, name, shape, dt=F32):
        return self.ctx.enter_context(self.nc.sbuf_tensor(f"{self.name}_{name}", shape, dt))

    def ps(self, name, shape, dt=F32):
        return self.ctx.enter_context(self.nc.psum_tensor(f"{self.name}_{name}", shape, dt))

    def sig(self, name, total):
        return self.signals(name, total)


def load_all(eng, pairs, loaded):
    for dst, src in pairs:
        eng.dma_start(dst, src).then_inc(loaded.sem, 16)


MOMENT_STEPS = 6


def statistics_signals(ph, tiles):
    return ph.sig("stats_done", tiles), ph.sig("moments_step", MOMENT_STEPS), ph.sig("rstd_done", 2)


def vector_statistics(eng, x, rows, tiles, raw, moments, stats_done, moments_step):
    with eng.Fori(0, tiles) as t:
        eng.bn_stats(raw[0:rows, t, :], x[0:rows, t, :]).then_inc(stats_done.sem, 1)
    mean_e, sq_e, mean_o, sq_o = (raw[0:rows, :, c] for c in (1, 2, 4, 5))
    mean, spread = moments[0:rows, 0, :], moments[0:rows, 1, :]
    eng.wait_ge(stats_done.sem, stats_done.at(tiles))
    eng.tensor_tensor(mean, mean_e, mean_o, ALU.add).then_inc(moments_step.sem, 1)
    eng.tensor_tensor(spread, mean_e, mean_o, ALU.subtract).then_inc(moments_step.sem, 1)
    eng.wait_ge(moments_step.sem, moments_step.at(2))
    eng.tensor_scalar(mean, mean, 0.5, None, ALU.mult).then_inc(moments_step.sem, 1)
    eng.scalar_tensor_tensor(spread, spread, D / 4.0, spread, ALU.mult, ALU.mult).then_inc(moments_step.sem, 1)
    eng.wait_ge(moments_step.sem, moments_step.at(4))
    eng.tensor_tensor(spread, spread, sq_e, ALU.add).then_inc(moments_step.sem, 1)
    eng.wait_ge(moments_step.sem, moments_step.at(5))
    eng.tensor_tensor(spread, spread, sq_o, ALU.add).then_inc(moments_step.sem, 1)


def gpsimd_rstd(eng, rows, tiles, moments, rstd, halves, eps, moments_step, rstd_done):
    eng.wait_ge(moments_step.sem, moments_step.at(MOMENT_STEPS))
    eng.tensor_scalar(rstd[0:rows, :], moments[0:rows, 1, :], 1.0 / D, eps, ALU.mult, ALU.add)\
       .then_inc(rstd_done.sem, 1)
    eng.wait_ge(rstd_done.sem, rstd_done.at(1))
    eng.tensor_tensor(rstd[0:rows, :], rstd[0:rows, :], halves[0:rows, 0:tiles], ALU.pow).then_inc(rstd_done.sem, 1)


def pairs(eng, tiles, body):
    if tiles <= 4:
        for t in range(0, tiles, 2):
            body(t)
    else:
        with eng.Fori(0, tiles // 2) as pair:
            body(pair * 2)


def transpose_phase(nc, signals, name, x, hT, consts, rows, tiles, cols=None, eps=1e-5):
    ident = consts["ident"]
    with Phase(nc, signals, name) as ph:
        norm = cols is not None
        nrm = [ph.sb(f"nrm{u}", [P, D]) for u in range(2)]
        psT = [ph.ps(f"psT{u}", [P, KT, P]) for u in range(2)]
        if norm:
            raw = ph.sb("raw", [P, tiles, 6])
            moments = ph.sb("moments", [P, 2, tiles])
            rstd = ph.sb("rstd", [P, tiles])
            stats_done, moments_step, rstd_done = statistics_signals(ph, tiles)
        ready = ph.sig("normalized", tiles)
        turned = ph.sig("transposed", tiles)
        stored = ph.sig("transpose_stored", tiles + 2)
        with nc.Block() as block:
            if norm:
                @block.gpsimd
                def _(eng):
                    gpsimd_rstd(eng, rows, tiles, moments, rstd, consts["minus_half"], eps, moments_step, rstd_done)

            @block.vector
            def _(eng):
                if norm:
                    vector_statistics(eng, x, rows, tiles, raw, moments, stats_done, moments_step)
                    eng.wait_ge(rstd_done.sem, rstd_done.at(2))
                def body(t):
                    for u in range(2):
                        eng.wait_ge(stored.sem, stored.at(t + (u + 1)))
                        if norm:
                            eng.tensor_scalar(nrm[u][0:rows, :], x[0:rows, t + u, :],
                                              moments[0:rows, 0, bass.ds(t + u, 1)], rstd[0:rows, bass.ds(t + u, 1)],
                                              ALU.subtract, ALU.mult).then_inc(ready.sem, 1)
                        else:
                            eng.tensor_copy(nrm[u][0:rows, :], x[0:rows, t + u, :]).then_inc(ready.sem, 1)

                pairs(eng, tiles, body)

            @block.tensor
            def _(eng):
                def body(t):
                    for u in range(2):
                        eng.wait_ge(ready.sem, ready.at(t + (u + 1)))
                        eng.wait_ge(stored.sem, stored.at(t + (u + 1)))
                        for k in range(KT):
                            mm = eng.transpose(psT[u][:, k, 0:rows], nrm[u][0:rows, k * P:(k + 1) * P],
                                               ident[0:rows, 0:rows])
                        mm.then_inc(turned.sem, 1)

                pairs(eng, tiles, body)

            @block.scalar
            def _(eng):
                eng.sem_inc(stored.sem, 2)
                def body(t):
                    for u in range(2):
                        eng.wait_ge(turned.sem, turned.at(t + (u + 1)))
                        for k in range(KT):
                            dst = hT[:, k, bass.ds((t + u) * rows, rows)]
                            if norm:
                                act = eng.activation(dst, psT[u][:, k, 0:rows], ACT.Identity,
                                                     bias=cols[1][:, k:k + 1], scale=cols[0][:, k:k + 1])
                            else:
                                act = eng.activation(dst, psT[u][:, k, 0:rows], ACT.Copy)
                        act.then_inc(stored.sem, 1)

                pairs(eng, tiles, body)


def output_norm_phase(nc, signals, name, x, consts, gain_row, shift_row, eps):
    with Phase(nc, signals, name) as ph:
        raw = ph.sb("raw", [P, NT, 6])
        moments = ph.sb("moments", [P, 2, NT])
        rstd = ph.sb("rstd", [P, NT])
        gain = ph.sb("gain", [P, D])
        shift = ph.sb("shift", [P, D])
        stats_done, moments_step, rstd_done = statistics_signals(ph, NT)
        loaded = ph.sig("weights_loaded", 32)
        ready = ph.sig("normalized", NT)
        scaled = ph.sig("gain_applied", NT)
        with nc.Block() as block:
            @block.sync
            def _(eng):
                eng.dma_start(gain[:], gain_row.partition_broadcast(P)).then_inc(loaded.sem, 16)
                eng.dma_start(shift[:], shift_row.partition_broadcast(P)).then_inc(loaded.sem, 16)

            @block.gpsimd
            def _(eng):
                gpsimd_rstd(eng, P, NT, moments, rstd, consts["minus_half"], eps, moments_step, rstd_done)
                eng.wait_ge(loaded.sem, loaded.at(32))
                with eng.Fori(0, NT) as t:
                    eng.wait_ge(scaled.sem, scaled.at(t + 1))
                    eng.tensor_tensor(x[:, t, :], x[:, t, :], shift[:], ALU.add)

            @block.vector
            def _(eng):
                vector_statistics(eng, x, P, NT, raw, moments, stats_done, moments_step)
                eng.wait_ge(rstd_done.sem, rstd_done.at(2))
                with eng.Fori(0, NT) as t:
                    eng.tensor_scalar(x[:, t, :], x[:, t, :], moments[:, 0, bass.ds(t, 1)], rstd[:, bass.ds(t, 1)],
                                      ALU.subtract, ALU.mult).then_inc(ready.sem, 1)
                eng.wait_ge(loaded.sem, loaded.at(32))
                with eng.Fori(0, NT) as t:
                    eng.wait_ge(ready.sem, ready.at(t + 1))
                    eng.tensor_tensor(x[:, t, :], x[:, t, :], gain[:], ALU.mult).then_inc(scaled.sem, 1)


def context_heads_phase(nc, signals, name, sT, w_k, w_v, b_k, b_v, consts, Kbd, Vbd, rope=None):
    n_k = KT * (2 if rope else 1)
    with Phase(nc, signals, name) as ph:
        wk = ph.sb("wk", [P, KT, D])
        wk2 = ph.sb("wk2", [P, KT, D]) if rope else None
        wv = ph.sb("wv", [P, KT, D])
        bv = ph.sb("bv", [1, D])
        sT2 = ph.sb("sT2", [P, KT, B, 2, SC])
        kT = [ph.sb(f"kT{t}", [P, B, SC]) for t in range(KT)]
        kS = [ph.sb(f"kS{t}", [P, B, SC]) for t in range(KT)] if rope else None
        psK = [ph.ps(f"psK{i}", [P, B * SC]) for i in range(n_k)]
        psV = [ph.ps(f"psV{b}", [P, D]) for b in range(B)]
        loaded = ph.sig("weights_loaded", 16 * (4 if rope else 3))
        doubled = ph.sig("context_doubled", 1)
        cleared = ph.sig("cleared", 1)
        k_ready = ph.sig("keys_in_psum", 1)
        v_ready = ph.sig("values_in_psum", 1)
        kT_ready = ph.sig("keys_biased", KT)
        turned = ph.sig("keys_turned", 2 * KT)
        with nc.Block() as block:
            @block.sync
            def _(eng):
                eng.dma_start(wk[:], w_k[0]).then_inc(loaded.sem, 16)
                if rope:
                    eng.dma_start(wk2[:], w_k[1]).then_inc(loaded.sem, 16)
                eng.dma_start(wv[:], w_v).then_inc(loaded.sem, 16)
                eng.dma_start(bv[:], b_v).then_inc(loaded.sem, 16)

            @block.gpsimd
            def _(eng):
                src = sT[:, :, :].rearrange("p k (b c) -> p (k b) c", c=SC)
                for s in range(2):
                    op = eng.tensor_copy(sT2[:, :, :, s, :].rearrange("p k b c -> p (k b) c"), src)
                op.then_inc(doubled.sem, 1)

            @block.tensor
            def _(eng):
                eng.wait_ge(loaded.sem, loaded.at(loaded.total))
                for t in range(KT):
                    for r in range(2 if rope else 1):
                        for k in range(KT):
                            mm = eng.matmul(psK[r * KT + t][:], (wk2 if r else wk)[:, k, t * P:(t + 1) * P],
                                            sT[:, k, :], start=(k == 0), stop=(k == KT - 1))
                mm.then_inc(k_ready.sem, 1)
                eng.wait_ge(doubled.sem, doubled.at(1))
                for b in range(B):
                    eng.matmul(psV[b][:], consts["ones"][0:1, 0:P], bv[:], start=True, stop=False)
                    for k in range(KT):
                        mm = eng.matmul(psV[b][:], sT2[:, k, b, :, :].rearrange("p s c -> p (s c)"),
                                        wv[:, k, :], start=False, stop=(k == KT - 1))
                mm.then_inc(v_ready.sem, 1)

            @block.scalar
            def _(eng):
                eng.wait_ge(k_ready.sem, k_ready.at(1))
                if not rope:
                    for t in range(KT):
                        eng.activation(kT[t][:].rearrange("p b c -> p (b c)"), psK[t][:], ACT.Identity,
                                       bias=b_k[0][:, t:t + 1], scale=1.0).then_inc(kT_ready.sem, 1)
                eng.wait_ge(v_ready.sem, v_ready.at(1))
                eng.wait_ge(cleared.sem, cleared.at(1))
                for b in range(B):
                    for s in range(2):
                        rows = slice(s * SC, (s + 1) * SC)
                        src = psV[b][rows, :].rearrange("p (j s d) -> p j s d", s=2, d=DK)[:, :, s, :]
                        eng.activation(Vbd[rows, b, :, s * (DK + 1):s * (DK + 1) + DK], src, ACT.Copy)

            @block.vector
            def _(eng):
                eng.memset(Vbd[:], 0.0).then_inc(turned.sem, 1)
                eng.wait_ge(turned.sem, turned.at(1))
                eng.memset(Vbd[0:SC, :, :, DK:DK + 1], 1.0)
                eng.memset(Vbd[SC:P, :, :, PW - 1:PW], 1.0).then_inc(cleared.sem, 1)
                if rope:
                    cos, sin = rope
                    eng.wait_ge(k_ready.sem, k_ready.at(1))
                    for t in range(KT):
                        for b in range(B):
                            cols = slice(b * SC, (b + 1) * SC)
                            eng.scalar_tensor_tensor(kT[t][:, b, :], psK[t][:, cols], b_k[0][:, t:t + 1],
                                                     cos[:, 0:SC], ALU.add, ALU.mult)
                            op = eng.scalar_tensor_tensor(kS[t][:, b, :], psK[KT + t][:, cols],
                                                          b_k[1][:, t:t + 1], sin[:, 0:SC], ALU.add, ALU.mult)
                    op.then_inc(turned.sem, 1)
                    eng.wait_ge(turned.sem, turned.at(2))
                    for t in range(KT):
                        eng.tensor_tensor(kT[t][:], kT[t][:], kS[t][:], ALU.add).then_inc(kT_ready.sem, 1)
                else:
                    eng.sem_inc(turned.sem, 1)
                for t in range(KT):
                    eng.wait_ge(kT_ready.sem, kT_ready.at(t + 1))
                    for b in range(B):
                        op = eng.tensor_tensor(Kbd[:, b, t, :].rearrange("p (h c) -> p h c", c=SC),
                                               kT[t][:, b, :].unsqueeze(1).to_broadcast([P, HT, SC]),
                                               consts["head_rows"][:].unsqueeze(2).to_broadcast([P, HT, SC]),
                                               ALU.mult)
                    op.then_inc(turned.sem, 1)


def cross_attention_phase(nc, signals, name, hT, x, rows, tiles, w_q, b_q, w_o, b_o, Kbd, Vbd, consts,
                          bias=None, rope=None):
    chunks = max(1, tiles * rows // CH)
    tpc = tiles // chunks
    cw = tpc * rows
    n_r = 2 if rope else 1
    with Phase(nc, signals, name) as ph:
        wq = [ph.sb(f"wq{r}", [P, KT, D]) for r in range(n_r)]
        wo = ph.sb("wo", [P, KT, D])
        bo = ph.sb("bo", [1, D])
        bq_scaled = ph.sb("bq_scaled", [P, KT])
        table = ph.sb("table", [P, bias[1], H * SC]) if bias else None
        qT = [[ph.sb(f"qT{u}{t}", [P, CH]) for t in range(KT)] for u in range(2)]
        qS = ph.sb("qS", [P, CH]) if rope else None
        sc = [ph.sb(f"sc{u}", [P, H, SC]) for u in range(2)]
        top = [ph.sb(f"top{u}", [P, H]) for u in range(2)]
        pT = [ph.sb(f"pT{u}", [P, H // 2, P]) for u in range(2)]
        rden = [ph.sb(f"rden{u}", [P, H]) for u in range(2)]
        cx = [ph.sb(f"cx{u}", [P, D]) for u in range(2)]
        cT = [ph.sb(f"cT{u}", [P, KT, P]) for u in range(2)]
        psS = ph.ps("psS", [P, H, SC])
        psT = ph.ps("psT", [P, H // 4, P])
        psQ = [ph.ps(f"psQ{i}", [P, CH]) for i in range(n_r)]
        psO = ph.ps("psO", [P, 512])
        psC = ph.ps("psC", [P, KT, P])
        psY = ph.ps("psY", [P, 512])
        n = B * tiles
        n_load = 16 * (n_r + 2 + bool(bias))
        loaded = ph.sig("weights_loaded", n_load)
        scaled = ph.sig("bias_scaled", 1)
        q_psum = ph.sig("query_in_psum", B * chunks * KT)
        q_halves = ph.sig("query_halves", B * chunks * KT if rope else 0)
        q_ready = ph.sig("query_ready", B * chunks * KT)
        s_psum = ph.sig("scores_in_psum", n)
        s_biased = ph.sig("scores_biased", n if bias else 0)
        s_top = ph.sig("scores_top", n)
        s_less = ph.sig("scores_less_top", n)
        p_ready = ph.sig("probs_ready", n)
        p_psum = ph.sig("probs_transposed", 2 * n)
        p_turned = ph.sig("probs_turned", 2 * n)
        c_psum = ph.sig("context_in_psum", n)
        c_inv = ph.sig("context_inverse", n)
        c_ready = ph.sig("context_ready", n)
        ct_psum = ph.sig("context_transposed", n)
        ct_ready = ph.sig("context_turned", n)
        y_psum = ph.sig("output_in_psum", n)
        y_added = ph.sig("output_added", n)

        def each_batch(eng, batch):
            if tiles > 1:
                with eng.Fori(0, B) as b:
                    batch(b)
            else:
                for b in range(B):
                    batch(b)

        def chunk_due(s):
            for c in range(chunks):
                if s == max(0, c * tpc - 2):
                    return c
            return None

        with nc.Block() as block:
            @block.sync
            def _(eng):
                for r in range(n_r):
                    eng.dma_start(wq[r][:], w_q[r]).then_inc(loaded.sem, 16)
                eng.dma_start(wo[:], w_o).then_inc(loaded.sem, 16)
                eng.dma_start(bo[:], b_o).then_inc(loaded.sem, 16)
                if bias:
                    eng.dma_start(table[0:rows], bias[0]).then_inc(loaded.sem, 16)

            @block.tensor
            def _(eng):
                def transpose_probs(b, s, half):
                    u, tile = (s - 1) % 2, b * tiles + (s - 1)
                    if s >= 2 or half:
                        eng.wait_ge(p_turned.sem, p_turned.at(tile * 2 + half))
                    for j in range(H // 4):
                        h = half * (H // 2) + 2 * j
                        mm = eng.transpose(psT[:, j, 0:rows],
                                           sc[u][0:rows, h:h + 2, :].rearrange("p h c -> p (h c)"),
                                           consts["ident"][0:rows, 0:rows])
                    mm.then_inc(p_psum.sem, 1)

                eng.wait_ge(loaded.sem, loaded.at(n_load))
                def batch(b):
                    for s in range(tiles + 4):
                        c = chunk_due(s)
                        if c is not None:
                            for t in range(KT):
                                if c + t > 0:
                                    eng.wait_ge(q_ready.sem, q_ready.at(b * (chunks * KT) + (c * KT + t)))
                                for r in range(n_r):
                                    for k in range(KT):
                                        mm = eng.matmul(psQ[r][:, 0:cw], wq[r][:, k, t * P:(t + 1) * P],
                                                        hT[:, k, bass.ds(b * (tiles * rows) + c * cw, cw)],
                                                        start=(k == 0), stop=(k == KT - 1))
                                mm.then_inc(q_psum.sem, 1)
                        if s < tiles:
                            c = s // tpc
                            eng.wait_ge(q_ready.sem, q_ready.at(b * (chunks * KT) + (c + 1) * KT))
                            if s >= 1:
                                eng.wait_ge(s_less.sem, s_less.at(b * tiles + s))
                            for t in range(KT):
                                mm = eng.matmul(psS[0:rows, t * HT:(t + 1) * HT, :].rearrange("p h c -> p (h c)"),
                                                qT[c % 2][t][:, (s % tpc) * rows:(s % tpc + 1) * rows],
                                                Kbd[:, b, t, :], start=True, stop=True)
                            mm.then_inc(s_psum.sem, 1)
                        if 1 <= s <= tiles:
                            eng.wait_ge(p_ready.sem, p_ready.at(b * tiles + s))
                            transpose_probs(b, s, 0)
                        if 2 <= s <= tiles + 1:
                            u, tile = s % 2, b * tiles + (s - 2)
                            eng.wait_ge(p_turned.sem, p_turned.at(tile * 2 + 2))
                            if s >= 3:
                                eng.wait_ge(c_ready.sem, c_ready.at(tile))
                            for j in range(H // 2):
                                mm = eng.matmul(psO[0:rows, j * PW:(j + 1) * PW], pT[u][:, j, 0:rows],
                                                Vbd[:, b, j, :], start=True, stop=True)
                            mm.then_inc(c_psum.sem, 1)
                        if 3 <= s <= tiles + 2:
                            u, tile = (s - 3) % 2, b * tiles + (s - 3)
                            eng.wait_ge(c_ready.sem, c_ready.at(tile + 1))
                            if s >= 4:
                                eng.wait_ge(ct_ready.sem, ct_ready.at(tile))
                            for k in range(KT):
                                mm = eng.transpose(psC[:, k, 0:rows],
                                                   cx[u][0:rows, k * P:(k + 1) * P],
                                                   consts["ident"][0:rows, 0:rows])
                            mm.then_inc(ct_psum.sem, 1)
                        if 4 <= s:
                            u, tile = s % 2, b * tiles + (s - 4)
                            eng.wait_ge(ct_ready.sem, ct_ready.at(tile + 1))
                            if s >= 5:
                                eng.wait_ge(y_added.sem, y_added.at(tile))
                            eng.matmul(psY[0:rows, 0:D], consts["ones"][0:1, 0:rows], bo[:],
                                       start=True, stop=False)
                            for k in range(KT):
                                mm = eng.matmul(psY[0:rows, 0:D], cT[u][:, k, 0:rows], wo[:, k, :],
                                                start=False, stop=(k == KT - 1))
                            mm.then_inc(y_psum.sem, 1)
                        if 1 <= s <= tiles:
                            transpose_probs(b, s, 1)

                each_batch(eng, batch)

            @block.scalar
            def _(eng):
                def turn_probs(b, s, half):
                    u, tile = (s - 1) % 2, b * tiles + (s - 1)
                    eng.wait_ge(p_psum.sem, p_psum.at(tile * 2 + half + 1))
                    eng.activation(pT[u][:, half * 4:half * 4 + 4, 0:rows], psT[:, :, 0:rows], ACT.Copy)\
                       .then_inc(p_turned.sem, 1)

                eng.wait_ge(loaded.sem, loaded.at(n_load))
                if not rope:
                    eng.mul(bq_scaled[:], b_q[0], SCALE).then_inc(scaled.sem, 1)
                    eng.wait_ge(scaled.sem, scaled.at(1))
                def batch(b):
                    for s in range(tiles + 4):
                        c = chunk_due(s)
                        if c is not None and not rope:
                            for t in range(KT):
                                q = b * (chunks * KT) + (c * KT + t)
                                eng.wait_ge(q_psum.sem, q_psum.at(q + 1))
                                eng.activation(qT[c % 2][t][:, 0:cw], psQ[0][:, 0:cw], ACT.Identity,
                                               bias=bq_scaled[:, t:t + 1], scale=SCALE).then_inc(q_ready.sem, 1)
                        if 1 <= s <= tiles:
                            if s >= 3:
                                eng.wait_ge(c_psum.sem, c_psum.at(b * tiles + (s - 2)))
                            turn_probs(b, s, 0)
                        if s < tiles:
                            u, tile = s % 2, b * tiles + s
                            eng.wait_ge(s_less.sem, s_less.at(tile + 1))
                            eng.activation(sc[u][0:rows], sc[u][0:rows], ACT.Exp).then_inc(p_ready.sem, 1)
                        if 3 <= s <= tiles + 2:
                            u, tile = (s - 3) % 2, b * tiles + (s - 3)
                            eng.wait_ge(ct_psum.sem, ct_psum.at(tile + 1))
                            if s >= 5:
                                eng.wait_ge(y_psum.sem, y_psum.at(tile - 1))
                            eng.activation(cT[u][:, :, 0:rows],
                                           psC[:, :, 0:rows],
                                           ACT.Copy).then_inc(ct_ready.sem, 1)
                        if 1 <= s <= tiles:
                            turn_probs(b, s, 1)

                each_batch(eng, batch)

            @block.vector
            def _(eng):
                eng.wait_ge(loaded.sem, loaded.at(n_load))
                def batch(b):
                    for s in range(tiles + 4):
                        c = chunk_due(s)
                        if c is not None and rope:
                            cos, sin = rope
                            for t in range(KT):
                                q = b * (chunks * KT) + (c * KT + t)
                                eng.wait_ge(q_psum.sem, q_psum.at(q + 1))
                                eng.scalar_tensor_tensor(qT[c % 2][t][:, 0:cw], psQ[0][:, 0:cw], b_q[0][:, t:t + 1],
                                                         cos[:, c * cw:(c + 1) * cw], ALU.add, ALU.mult)
                                eng.scalar_tensor_tensor(qS[:, 0:cw], psQ[1][:, 0:cw], b_q[1][:, t:t + 1],
                                                         sin[:, c * cw:(c + 1) * cw], ALU.add, ALU.mult)\
                                   .then_inc(q_halves.sem, 1)
                                eng.wait_ge(q_halves.sem, q_halves.at(q + 1))
                                eng.tensor_tensor(qT[c % 2][t][:, 0:cw], qT[c % 2][t][:, 0:cw], qS[:, 0:cw],
                                                  ALU.add).then_inc(q_ready.sem, 1)
                                eng.wait_ge(q_ready.sem, q_ready.at(q + 1))
                        if s < tiles:
                            u, tile = s % 2, b * tiles + s
                            eng.wait_ge(s_psum.sem, s_psum.at(tile + 1))
                            if s >= 2:
                                eng.wait_ge(p_psum.sem, p_psum.at((tile - 1) * 2))
                            src = psS
                            if bias:
                                j = min(s, bias[1] - 1)
                                eng.tensor_tensor(sc[u][0:rows], psS[0:rows],
                                                  table[0:rows, j, :].rearrange("p (h c) -> p h c", c=SC),
                                                  ALU.add).then_inc(s_biased.sem, 1)
                                eng.wait_ge(s_biased.sem, s_biased.at(tile + 1))
                                src = sc[u]
                            eng.tensor_reduce(top[u][0:rows], src[0:rows], AX.X, ALU.max).then_inc(s_top.sem, 1)
                            eng.wait_ge(s_top.sem, s_top.at(tile + 1))
                            eng.tensor_tensor(sc[u][0:rows], src[0:rows],
                                              top[u][0:rows].unsqueeze(2).to_broadcast([rows, H, SC]),
                                              ALU.subtract).then_inc(s_less.sem, 1)
                        if 2 <= s <= tiles + 1:
                            u, tile = s % 2, b * tiles + (s - 2)
                            got = psO[0:rows, 0:H * (DK + 1)].rearrange("p (h d) -> p h d", d=DK + 1)
                            eng.wait_ge(c_psum.sem, c_psum.at(tile + 1))
                            eng.reciprocal(rden[u][0:rows], got[:, :, DK]).then_inc(c_inv.sem, 1)
                            eng.wait_ge(c_inv.sem, c_inv.at(tile + 1))
                            if s >= 4:
                                eng.wait_ge(ct_psum.sem, ct_psum.at(tile - 1))
                            eng.tensor_tensor(cx[u][0:rows].rearrange("p (h d) -> p h d", d=DK),
                                              got[:, :, 0:DK],
                                              rden[u][0:rows].unsqueeze(2).to_broadcast([rows, H, DK]),
                                              ALU.mult).then_inc(c_ready.sem, 1)
                        if 4 <= s:
                            tile = b * tiles + (s - 4)
                            xt = x[0:rows, tile, :]
                            eng.wait_ge(y_psum.sem, y_psum.at(tile + 1))
                            eng.tensor_tensor(xt, xt, psY[0:rows, 0:D], ALU.add).then_inc(y_added.sem, 1)

                each_batch(eng, batch)


def self_heads_phase(nc, signals, name, hT, w_q, w_k, w_v, b_q, b_k, b_v, consts, Qd, Kd, Vd, rope=None):
    n_r = 2 if rope else 1
    ITEMS = []
    for half in range(2):
        ITEMS += [("qk", half, t, kind) for t in range(KT) for kind in range(2)]
        ITEMS += [("v", half, j, 0) for j in range(4)]
    n_qk, n_v = 8, 8
    index, seen = [], {"qk": 0, "v": 0}
    for item in ITEMS:
        index.append(seen[item[0]])
        seen[item[0]] += 1
    with Phase(nc, signals, name) as ph:
        w = [[ph.sb(f"w{kind}{r}", [P, KT, D]) for r in range(n_r)] for kind in range(2)]
        wv = ph.sb("wv", [P, KT, D])
        bv = ph.sb("bv", [1, D])
        Vst = ph.sb("Vst", [P, B * H, TB, VW + 1], BF16)
        bq_scaled = ph.sb("bq_scaled", [P, KT])
        hS = [ph.sb(f"hS{u}", [P, KT, CH]) for u in range(2)]
        y = [ph.sb(f"y{u}", [P, CH]) for u in range(2)]
        y2 = [ph.sb(f"y2{u}", [P, CH]) for u in range(2)] if rope else None
        rest = [ph.sb(f"rest{u}", [P, CH]) for u in range(2)]
        piece = [ph.sb(f"piece{u}", [P, 3, CH], BF16) for u in range(2)]
        vrest = [ph.sb(f"vrest{u}", [P, H, DK]) for u in range(2)]
        psQ = [[ph.ps(f"psQ{u}{r}", [P, CH]) for r in range(n_r)] for u in range(2)]
        psV = [ph.ps(f"psV{u}", [P, 512]) for u in range(2)]
        n_load = 16 * (2 * n_r + 2)
        loaded = ph.sig("weights_loaded", n_load)
        scaled = ph.sig("bias_scaled", 1)
        staged = [ph.sig(f"chunk_staged{u}", 16 * B) for u in range(2)]
        qk_psum = ph.sig("projection_in_psum", n_qk * B)
        qk_read = ph.sig("projection_read", n_qk * B)
        y_ready = ph.sig("projection_ready", n_qk * B if rope else 0)
        high = ph.sig("high_ready", n_qk * B)
        rested = ph.sig("rest_ready", n_qk * B)
        mid = ph.sig("mid_ready", n_qk * B)
        low = ph.sig("low_ready", n_qk * B)
        written = [ph.sig(f"pieces_written{u}", 16 * n_qk * B // 2) for u in range(2)]
        v_written = ph.sig("values_written", 16 * B)
        v_psum = ph.sig("value_in_psum", n_v * B)
        v_high = ph.sig("value_high_ready", n_v * B)
        v_rest = ph.sig("value_rest_ready", n_v * B)
        v_mid = ph.sig("value_mid_ready", n_v * B)
        v_low = ph.sig("value_low_ready", n_v * B)

        def batch_over(eng, b):
            for u in range(2):
                eng.wait_ge(written[u].sem, written[u].at(b * (8 * n_qk) + 8 * n_qk))
            eng.wait_ge(v_low.sem, v_low.at(b * n_v + n_v))

        def vst(b, j, part):
            return Vst[:, bass.ds(b * H, H), j, part * DK:(part + 1) * DK]

        with nc.Block() as block:
            @block.sync
            def _(eng):
                for dst, src in ((w[0], w_q), (w[1], w_k)):
                    for r in range(n_r):
                        eng.dma_start(dst[r][:], src[r]).then_inc(loaded.sem, 16)
                eng.dma_start(wv[:], w_v).then_inc(loaded.sem, 16)
                eng.dma_start(bv[:], b_v).then_inc(loaded.sem, 16)
                with eng.Fori(0, B) as b:
                    for half in range(2):
                        eng.dma_start(hS[half][:], hT[:, :, bass.ds(b * SQ + half * CH, CH)])\
                           .then_inc(staged[half].sem, 16)
                    for n, (what, half, t, kind) in enumerate(ITEMS):
                        if what == "qk":
                            g = b * n_qk + index[n]
                            eng.wait_ge(low.sem, low.at(g + 1))
                            eng.wait_ge(mid.sem, mid.at(g + 1))
                            eng.wait_ge(high.sem, high.at(g + 1))
                            if index[n] == n_qk - 1:
                                eng.wait_ge(v_low.sem, v_low.at(b * n_v + n_v))
                            dst = (Kd if kind else Qd)[:, bass.ds(b * D + t * P, P), half * CH:(half + 1) * CH]
                            eng.dma_start(dst.rearrange("r p c -> p r c"), piece[index[n] % 2][:])\
                               .then_inc(written[index[n] % 2].sem, 16)
                    heads = bass.ds(b * H, H)
                    eng.dma_start(Vd[heads].rearrange("g p j c -> p g (j c)"),
                                  Vst[:, heads].rearrange("p g j c -> p g (j c)")).then_inc(v_written.sem, 16)
                for u in range(2):
                    eng.wait_ge(written[u].sem, written[u].at(B * 8 * n_qk))
                eng.wait_ge(v_written.sem, v_written.at(16 * B))

            @block.tensor
            def _(eng):
                eng.wait_ge(loaded.sem, loaded.at(n_load))
                with eng.Fori(0, B) as b:
                    for n, (what, half, t, kind) in enumerate(ITEMS):
                        i = index[n]
                        if n % 8 == 0:
                            eng.wait_ge(staged[half].sem, staged[half].at(b * 16 + 16))
                        if what == "qk":
                            if i >= 2:
                                eng.wait_ge(qk_read.sem, qk_read.at(b * n_qk + (i - 1)))
                            for r in range(n_r):
                                for k in range(KT):
                                    mm = eng.matmul(psQ[i % 2][r][:], w[kind][r][:, k, t * P:(t + 1) * P],
                                                    hS[half][:, k, :], start=(k == 0), stop=(k == KT - 1))
                            mm.then_inc(qk_psum.sem, 1)
                        else:
                            if i >= 2:
                                eng.wait_ge(v_rest.sem, v_rest.at(b * n_v + (i - 1)))
                            eng.matmul(psV[i % 2][:, 0:D], consts["ones"][0:1, 0:P], bv[:], start=True, stop=False)
                            for k in range(KT):
                                mm = eng.matmul(psV[i % 2][:, 0:D], hS[half][:, k, t * P:(t + 1) * P], wv[:, k, :],
                                                start=False, stop=(k == KT - 1))
                            mm.then_inc(v_psum.sem, 1)
                    batch_over(eng, b)

            @block.scalar
            def _(eng):
                if not rope:
                    eng.mul(bq_scaled[:], b_q[0], SCALE).then_inc(scaled.sem, 1)
                    eng.wait_ge(scaled.sem, scaled.at(1))
                with eng.Fori(0, B) as b:
                    for n in range(len(ITEMS) + 1):
                        if n < len(ITEMS):
                            what, half, t, kind = ITEMS[n]
                            i = index[n]
                            if what == "qk" and not rope:
                                eng.wait_ge(qk_psum.sem, qk_psum.at(b * n_qk + (i + 1)))
                                if i >= 2:
                                    eng.wait_ge(rested.sem, rested.at(b * n_qk + (i - 1)))
                                bias = (b_k[0] if kind else bq_scaled)[:, t:t + 1]
                                eng.activation(y[i % 2][:], psQ[i % 2][0][:], ACT.Identity, bias=bias,
                                               scale=1.0 if kind else SCALE).then_inc(qk_read.sem, 1)
                            if what == "v":
                                eng.wait_ge(v_psum.sem, v_psum.at(b * n_v + (i + 1)))
                                src = psV[i % 2][:, 0:D].rearrange("p (h d) -> p h d", d=DK)
                                eng.activation(vst(b, i, 0), src, ACT.Copy).then_inc(v_high.sem, 1)
                        if n >= 1:
                            what, half, t, kind = ITEMS[n - 1]
                            i = index[n - 1]
                            if what == "qk":
                                eng.wait_ge(rested.sem, rested.at(b * n_qk + (i + 1)))
                                if i >= 2:
                                    eng.wait_ge(written[i % 2].sem, written[i % 2].at(b * (8 * n_qk) + 16 * (i // 2)))
                                eng.activation(piece[i % 2][:, 1, :], rest[i % 2][:], ACT.Copy).then_inc(mid.sem, 1)
                            else:
                                eng.wait_ge(v_rest.sem, v_rest.at(b * n_v + (i + 1)))
                                eng.activation(vst(b, i, 1), vrest[i % 2][:], ACT.Copy).then_inc(v_mid.sem, 1)
                    batch_over(eng, b)

            @block.vector
            def _(eng):
                with eng.Fori(0, B) as b:
                    for n, (what, half, t, kind) in enumerate(ITEMS):
                        i = index[n]
                        u = i % 2
                        if what == "qk":
                            g = b * n_qk + i
                            if rope:
                                cos, sin = rope[kind]
                                bias = b_k if kind else b_q
                                cs = slice(half * CH, (half + 1) * CH)
                                eng.wait_ge(qk_psum.sem, qk_psum.at(g + 1))
                                if i >= 2:
                                    eng.wait_ge(y_ready.sem, y_ready.at(b * n_qk + (i - 1)))
                                eng.scalar_tensor_tensor(y[u][:], psQ[u][0][:], bias[0][:, t:t + 1], cos[:, cs],
                                                         ALU.add, ALU.mult)
                                eng.scalar_tensor_tensor(y2[u][:], psQ[u][1][:], bias[1][:, t:t + 1], sin[:, cs],
                                                         ALU.add, ALU.mult).then_inc(qk_read.sem, 1)
                                eng.wait_ge(y_ready.sem, y_ready.at(g + 1))
                            else:
                                eng.wait_ge(qk_read.sem, qk_read.at(g + 1))
                            if i >= 2:
                                eng.wait_ge(written[i % 2].sem, written[i % 2].at(b * (8 * n_qk) + 16 * (i // 2)))
                                eng.wait_ge(low.sem, low.at(b * n_qk + (i - 1)))
                            eng.tensor_copy(piece[u][:, 0, :], y[u][:]).then_inc(high.sem, 1)
                            eng.wait_ge(high.sem, high.at(g + 1))
                            eng.tensor_tensor(rest[u][:], y[u][:], piece[u][:, 0, :], ALU.subtract)\
                               .then_inc(rested.sem, 1)
                        else:
                            eng.wait_ge(v_high.sem, v_high.at(b * n_v + (i + 1)))
                            if i >= 2:
                                eng.wait_ge(v_low.sem, v_low.at(b * n_v + (i - 1)))
                            eng.tensor_tensor(vrest[u][:], psV[u][:, 0:D].rearrange("p (h d) -> p h d", d=DK),
                                              vst(b, i, 0), ALU.subtract).then_inc(v_rest.sem, 1)
                    batch_over(eng, b)

            @block.gpsimd
            def _(eng):
                eng.memset(Vst[:, :, :, 3 * DK:VW + 1], 1.0)
                with eng.Fori(0, B) as b:
                    for n in range(len(ITEMS) + 1):
                        if n < len(ITEMS) and ITEMS[n][0] == "qk" and rope:
                            i = index[n]
                            eng.wait_ge(qk_read.sem, qk_read.at(b * n_qk + (i + 1)))
                            eng.tensor_tensor(y[i % 2][:], y[i % 2][:], y2[i % 2][:], ALU.add).then_inc(y_ready.sem, 1)
                        if n >= 1:
                            i = index[n - 1]
                            u = i % 2
                            if ITEMS[n - 1][0] == "qk":
                                eng.wait_ge(mid.sem, mid.at(b * n_qk + (i + 1)))
                                if i >= 2:
                                    eng.wait_ge(written[i % 2].sem, written[i % 2].at(b * (8 * n_qk) + 16 * (i // 2)))
                                eng.tensor_tensor(piece[u][:, 2, :], rest[u][:], piece[u][:, 1, :], ALU.subtract)\
                                   .then_inc(low.sem, 1)
                            else:
                                eng.wait_ge(v_mid.sem, v_mid.at(b * n_v + (i + 1)))
                                eng.tensor_tensor(vst(b, i, 2), vrest[u][:], vst(b, i, 1), ALU.subtract)\
                                   .then_inc(v_low.sem, 1)
                    batch_over(eng, b)


def near_blocks_phase(nc, signals, name, q_rel, k_rel, far, mask_q, mask_k, q_near, k_near):
    HN = 17
    with Phase(nc, signals, name) as ph:
        rel = ph.sb("rel", [P, HN, 2 * P])
        rest = ph.sb("rest", [P, HN, 2 * P])
        far_sb = ph.sb("far", [P, HN])
        mask = ph.sb("mask", [P, 2 * P])
        loaded = ph.sig("weights_loaded", 16 * 5)
        step = ph.sig("near_step", 10)
        with nc.Block() as block:
            @block.sync
            def _(eng):
                eng.dma_start(far_sb[:], far.partition_broadcast(P)).then_inc(loaded.sem, 16)
                eng.dma_start(rel[:], q_rel).then_inc(loaded.sem, 16)
                eng.dma_start(mask[:], mask_q).then_inc(loaded.sem, 16)
                eng.wait_ge(step.sem, step.at(3))
                eng.dma_start(rel[:], k_rel).then_inc(loaded.sem, 16)
                eng.dma_start(mask[:], mask_k).then_inc(loaded.sem, 16)

            @block.vector
            def _(eng):
                done = 0
                far_b = far_sb[:].unsqueeze(2).to_broadcast([P, HN, 2 * P])
                mask_b = mask[:].unsqueeze(1).to_broadcast([P, HN, 2 * P])
                for side in range(2):
                    eng.wait_ge(loaded.sem, loaded.at(48 if side == 0 else 80))
                    eng.tensor_tensor(rel[:], rel[:], far_b, ALU.subtract).then_inc(step.sem, 1)
                    eng.wait_ge(step.sem, step.at(done + 1))
                    eng.tensor_tensor(rel[:], rel[:], mask_b, ALU.add).then_inc(step.sem, 1)
                    eng.wait_ge(step.sem, step.at(done + 2))
                    eng.tensor_copy((k_near[0] if side else q_near)[:], rel[:]).then_inc(step.sem, 1)
                    eng.wait_ge(step.sem, step.at(done + 3))
                    done += 3
                for piece in range(2):
                    src = rel if piece == 0 else rest
                    eng.tensor_tensor(rest[:], src[:], k_near[piece][:], ALU.subtract).then_inc(step.sem, 1)
                    eng.wait_ge(step.sem, step.at(done + 1))
                    eng.tensor_copy(k_near[piece + 1][:], rest[:]).then_inc(step.sem, 1)
                    eng.wait_ge(step.sem, step.at(done + 2))
                    done += 2


def self_attention_phase(nc, signals, name, Qd, Kd, Vd, cx, consts, causal, near=None):
    KB = SQ // P
    LOAD_AHEAD = 2
    RING = 4

    def max_units(qt):
        end = (qt + 1) * P if causal else SQ
        return [("A", qt, hf, min(CH, end - hf * CH)) for hf in range(2) if end > hf * CH]

    units = [m for qt in range(KB) for m in max_units(qt)]
    per_step = -(-(len(units) + 2) // 6)
    plan = [[] for _ in range(KB)]
    queue = list(units)
    for s in range(6):
        take = per_step - (2 if s == 3 else 0)
        if s == 3:
            plan[s] += [("C", 0), ("C", 1)]
        plan[s] += queue[:take]
        queue = queue[take:]
    assert not queue
    plan[6] = [("M", 0), ("M", 1)]
    flat = [m for s in plan for m in s]
    NU = len(flat)
    assert NU % 2 == 0
    nA = len(units)

    def q_from(kt):
        return kt * P if causal else 0

    def banks(lo, hi):
        return [(max(lo, c * CH), min(hi, (c + 1) * CH)) for c in range(2) if min(hi, (c + 1) * CH) > max(lo, c * CH)]

    with Phase(nc, signals, name) as ph:
        Qs = [ph.sb(f"Qs{r}", [KS + 1, SQ], BF16) for r in range(RING)]
        Ks = [ph.sb(f"Ks{r}", [KS + 1, SQ], BF16) for r in range(RING)]
        Pf = [ph.sb(f"Pf{r}", [P, SQ]) for r in range(4)]
        Pl = [ph.sb(f"Pl{r}", [P, SQ], F16) for r in range(4)]
        Vs = [ph.sb(f"Vs{r}", [P, TB, VW + 1], BF16) for r in range(RING)]
        oT = ph.sb("oT", [VW, SQ])
        mxp = ph.sb("mxp", [P, KB, 2])
        mx = ph.sb("mx", [P, KB], BF16)
        rden = [ph.sb(f"rden{u}", [P, 4]) for u in range(2)]
        psA = [ph.ps(f"psA{u}", [P, CH]) for u in range(2)]
        psB = [ph.ps(f"psB{u}", [P, SQ]) for u in range(2)]
        psO = ph.ps("psO", [P, SQ])
        HEADS = B * H
        padded = ph.sig("heads_padded", 48)
        cleared = ph.sig("cleared", 1)
        prep = ph.sig("prepared", 3)
        q_loaded = [ph.sig(f"head_loaded{r}", 16 * 13 * ((HEADS + LOAD_AHEAD - r + RING - 1) // RING)) for r in range(RING)]
        a_psum = ph.sig("unit_in_psum", nA + 2 + HEADS * NU + 2)
        a_read = ph.sig("unit_read", 2 + nA + 2 + HEADS * NU + 2)
        maxed = ph.sig("maxima_ready", HEADS + 1)
        b_psum = ph.sig("scores_in_psum", LOAD_AHEAD * KB + HEADS * KB)
        p_ready = ph.sig("probs_ready", 2 + HEADS * KB)
        l_vec = ph.sig("low_probs_vector", 1 + HEADS * KB // 2)
        l_pool = ph.sig("low_probs_pool", 1 + HEADS * KB // 2)
        o_read = ph.sig("context_read", HEADS + 1)
        pv_done = ph.sig("key_tile_used", 2 + 2 + HEADS * KB)
        inverse = ph.sig("context_inverse", 2 * (HEADS + 1))

        def hi(t, lo, hi_):
            return Pf[t][:].bitcast(BF16).rearrange("p (q two) -> p q two", two=2)[:, lo:hi_, 1]

        def each_head(eng, body):
            with eng.Fori(0, B) as b:
                with eng.Fori(0, H // RING) as quarter:
                    hq = quarter * RING
                    for r in range(RING):
                        body(b * H + hq + r, hq + r, r)

        with nc.Block() as block:
            @block.sync
            def _(eng):
                def load(g, r):
                    for dst, src, parts in ((Qs, Qd, Q_PART), (Ks, Kd, K_PART)):
                        for n, part in enumerate(parts):
                            eng.dma_start(dst[r][n * DK:(n + 1) * DK, :], src[part, bass.ds(g * DK, DK), :])\
                               .then_inc(q_loaded[r].sem, 16)
                    eng.dma_start(Vs[r][:], Vd[bass.ds(g, 1)].rearrange("g p j c -> (g p) j c"))\
                       .then_inc(q_loaded[r].sem, 16)

                for dram in (Qd, Kd):
                    eng.dma_start(dram[:, B * D:B * D + LOAD_AHEAD * DK, :], dram[:, 0:LOAD_AHEAD * DK, :])\
                       .then_inc(padded.sem, 16)
                eng.dma_start(Vd[B * H:B * H + LOAD_AHEAD], Vd[0:LOAD_AHEAD]).then_inc(padded.sem, 16)
                for g in range(LOAD_AHEAD):
                    load(g, g)
                eng.wait_ge(padded.sem, padded.at(48))

                def body(g, h, r):
                    eng.wait_ge(b_psum.sem, b_psum.at(g * KB + (KB + 3)))
                    load(g + LOAD_AHEAD, (r + LOAD_AHEAD) % RING)

                each_head(eng, body)
                for r in range(RING):
                    eng.wait_ge(q_loaded[r].sem, q_loaded[r].at(q_loaded[r].total))

            @block.tensor
            def _(eng):
                def unit(m, n, count, r_next, h_next):
                    bank = psA[n % 2]
                    eng.wait_ge(a_read.sem, a_read.at(count + 1))
                    if m[0] == "A":
                        _, qt, hf, width = m
                        add = []
                        if near:
                            q_near, _, wide, per_head = near
                            for blk in ((qt - 1, qt) if wide else (qt,)):
                                if blk >= 0 and hf * CH <= blk * P < hf * CH + width:
                                    add.append(blk)
                        mm = eng.matmul(bank[:, 0:width], Qs[r_next][0:KS, qt * P:(qt + 1) * P],
                                        Ks[r_next][0:KS, hf * CH:hf * CH + width], start=True, stop=not add)
                        for blk in add:
                            at = (blk - qt + 1) * P if wide else 0
                            src = q_near[:, bass.ds(h_next, 1), at:at + P].rearrange("p h c -> p (h c)") \
                                if per_head else q_near[:, at:at + P]
                            mm = eng.matmul(bank[:, blk * P - hf * CH:blk * P - hf * CH + P], consts["identb"][:],
                                            src, start=False, stop=(blk == add[-1]))
                    elif m[0] == "C":
                        for j in range(4):
                            q = m[1] * 4 + j
                            mm = eng.matmul(bank[:, j * (DK + 1):(j + 1) * (DK + 1)], oT[:, q * P:(q + 1) * P],
                                            consts["combine"][:], start=True, stop=True)
                    else:
                        for j in range(4):
                            q = m[1] * 4 + j
                            mm = eng.matmul(bank[0:1, j * P:(j + 1) * P], mx[:, q:q + 1], consts["identb"][:],
                                            start=True, stop=True)
                    mm.then_inc(a_psum.sem, 1)

                def values(g, r, kt, part):
                    if part:
                        l_ready = l_pool if kt % 2 else l_vec
                        eng.wait_ge(l_ready.sem, l_ready.at(g * (KB // 2) + (kt // 2 + 1)))
                    elif kt == 2:
                        eng.wait_ge(o_read.sem, o_read.at(g + 1))
                    v = (kt - 2) % KB
                    lhs = Vs[r if kt >= 2 else (r - 1) % RING][:, v, 0:VW]
                    for lo, up in banks(q_from(v), SQ):
                        src = Pl[v % 4][:, lo:up] if part else hi(v % 4, lo, up)
                        final = KB - 1 if (not causal or lo >= CH) else CH // P - 1
                        mm = eng.matmul(psO[0:VW, lo:up], lhs, src, start=(v == 0 and part == 0),
                                        stop=(v == final and part == 1))
                    if part:
                        mm.then_inc(pv_done.sem, 1)

                eng.sem_inc(b_psum.sem, LOAD_AHEAD * KB)
                eng.sem_inc(pv_done.sem, 2)
                eng.wait_ge(prep.sem, prep.at(3))
                eng.wait_ge(cleared.sem, cleared.at(1))
                for c in range(2):
                    eng.matmul(psO[0:VW, c * CH:(c + 1) * CH], Vs[RING - 1][:, KB - 1, 0:VW],
                               hi(KB // 2 - 1, c * CH, (c + 1) * CH), start=True, stop=(causal and c == 0))
                eng.wait_ge(q_loaded[0].sem, q_loaded[0].at(16 * 13))
                for n, m in enumerate(units):
                    unit(m, n, n, 0, 0)
                eng.wait_ge(maxed.sem, maxed.at(1))
                for n in range(2):
                    unit(("M", n), nA + n, nA + n, 0, 0)

                def body(g, h, r):
                    nxt = (r + 1) % RING
                    it = (g - r) if r < RING - 1 else (g + 1)
                    eng.wait_ge(q_loaded[nxt].sem,
                                q_loaded[nxt].at(it * (16 * 13 // RING) + 16 * 13))
                    n = 0
                    for kt in range(KB):
                        if kt == 0:
                            eng.wait_ge(a_read.sem, a_read.at(g * NU + (nA + 2 + 2)))
                        eng.wait_ge(p_ready.sem, p_ready.at(g * KB + (kt + 1)))
                        k_near, wide, per_head = (near[1], near[2], near[3]) if near else ([], False, False)
                        for lo, up in banks(q_from(kt), SQ):
                            near_end = (kt + 2) * P if wide else (kt + 1) * P
                            adds = banks(max(lo, kt * P), min(up, near_end)) if k_near else []
                            mm = eng.matmul(psB[kt % 2][:, lo:up], Ks[r][:, kt * P:(kt + 1) * P], Qs[r][:, lo:up],
                                            start=True, stop=not adds)
                            for lo2, up2 in adds:
                                for piece in k_near:
                                    at = lo2 - kt * P
                                    src = piece[:, bass.ds(h, 1), at:at + up2 - lo2].rearrange("p h c -> p (h c)") \
                                        if per_head else piece[:, at:at + up2 - lo2]
                                    mm = eng.matmul(psB[kt % 2][:, lo2:up2], consts["identb"][:], src,
                                                    start=False, stop=(piece is k_near[-1]))
                        mm.then_inc(b_psum.sem, 1)
                        first, then = (plan[kt][0:2], plan[kt][2:]) if kt < 6 else ([], [])
                        for todo, part in ((first, 0), (then, 1)):
                            for m in todo:
                                if m == ("C", 0):
                                    eng.wait_ge(o_read.sem, o_read.at(g + 1))
                                unit(m, nA + 2 + n, g * NU + (nA + 2 + n), nxt, h + 1)
                                n += 1
                            values(g, r, kt, part)
                        if kt == 6:
                            eng.wait_ge(maxed.sem, maxed.at(g + 2))
                            for m in plan[kt]:
                                unit(m, nA + 2 + n, g * NU + (nA + 2 + n), nxt, h + 1)
                                n += 1

                each_head(eng, body)
                for kt in range(2):
                    eng.wait_ge(p_ready.sem, p_ready.at(HEADS * KB + (kt + 1)))
                    for part in range(2):
                        values(HEADS, 0, kt, part)
                eng.wait_ge(o_read.sem, o_read.at(HEADS + 1))
                for n in range(2):
                    unit(("C", n), nA + n, nA + 2 + HEADS * NU + n, 0, 0)

            @block.scalar
            def _(eng):
                eng.sem_inc(p_ready.sem, 2)

                def copy_context(g):
                    eng.wait_ge(pv_done.sem, pv_done.at(g * KB + 4))
                    eng.wait_ge(a_psum.sem, a_psum.at(g * NU + (nA + 2 + flat.index(("C", 1)) + 1 - NU)))
                    eng.activation(oT[:], psO[0:VW, :], ACT.Copy).then_inc(o_read.sem, 1)

                def shift_row(count, half, r_next):
                    eng.wait_ge(a_psum.sem, a_psum.at(count + 1))
                    eng.activation(Qs[r_next][KS:KS + 1, half * CH:(half + 1) * CH], psA[half][0:1, :], ACT.Copy)\
                       .then_inc(a_read.sem, 1)

                for half in range(2):
                    shift_row(nA + half, half, 0)

                def body(g, h, r):
                    for kt in range(KB):
                        if kt == 2:
                            copy_context(g)
                        eng.wait_ge(b_psum.sem, b_psum.at(g * KB + (kt + 1 + LOAD_AHEAD * KB)))
                        eng.wait_ge(pv_done.sem, pv_done.at(g * KB + (kt + 1)))
                        lo = q_from(kt)
                        eng.activation(Pf[kt % 4][:, lo:SQ], psB[kt % 2][:, lo:SQ], ACT.Exp).then_inc(p_ready.sem, 1)
                        if kt == 6:
                            for half in range(2):
                                shift_row(g * NU + (nA + 2 + nA + 2 + half), half, (r + 1) % RING)

                each_head(eng, body)
                copy_context(HEADS)

            def rests(eng, g, kt, done):
                eng.wait_ge(p_ready.sem, p_ready.at(g * KB + (kt + 3)))
                eng.wait_ge(pv_done.sem, pv_done.at(g * KB + (kt + 1)))
                lo = q_from(kt)
                eng.tensor_tensor(Pl[kt % 4][:, lo:SQ], Pf[kt % 4][:, lo:SQ], hi(kt % 4, lo, SQ),
                                  ALU.subtract).then_inc(done.sem, 1)

            @block.gpsimd
            def _(eng):
                for t in (2, 3):
                    eng.memset(Pf[t][:], 1.0)
                    eng.memset(Pl[t][:], 1.0)
                eng.memset(Vs[RING - 1][:], 1.0).then_inc(cleared.sem, 1)
                eng.sem_inc(l_pool.sem, 1)

                def body(g, h, r):
                    for kt in range(1, KB, 2):
                        rests(eng, g, kt, l_pool)

                each_head(eng, body)

            @block.vector
            def _(eng):
                for r in range(RING):
                    eng.memset(Ks[r][KS:KS + 1, :], 1.0)
                eng.memset(mxp[:], NEG).then_inc(prep.sem, 1)
                eng.wait_ge(prep.sem, prep.at(1))
                eng.sem_inc(a_read.sem, 2)
                eng.sem_inc(prep.sem, 2)
                eng.sem_inc(l_vec.sem, 1)

                def unit(m, n, count, g_out):
                    bank = psA[n % 2]
                    eng.wait_ge(a_psum.sem, a_psum.at(count + 1))
                    if m[0] == "A":
                        _, qt, hf, width = m
                        eng.tensor_reduce(mxp[:, qt, hf:hf + 1], bank[:, 0:width], AX.X, ALU.max)\
                           .then_inc(a_read.sem, 1)
                    else:
                        got = bank[:, 0:4 * (DK + 1)].rearrange("p (j d) -> p j d", d=DK + 1)
                        rd = rden[m[1]]
                        eng.reciprocal(rd[:], got[:, :, DK]).then_inc(inverse.sem, 1)
                        eng.wait_ge(inverse.sem, inverse.at(g_out * 2 + (m[1] + 1)))
                        dst = cx[:, bass.ds(g_out, 1), m[1] * 4:m[1] * 4 + 4, :].rearrange("p g j d -> p (g j) d")
                        eng.tensor_tensor(dst, got[:, :, 0:DK], rd[:].unsqueeze(2).to_broadcast([P, 4, DK]),
                                          ALU.mult).then_inc(a_read.sem, 1)

                def maxima(count, g_next):
                    eng.wait_ge(a_read.sem, a_read.at(count))
                    eng.tensor_reduce(mx[:], mxp[:], AX.X, ALU.max, negate=True).then_inc(maxed.sem, 1)
                    eng.wait_ge(maxed.sem, maxed.at(g_next + 1))

                for n, m in enumerate(units):
                    unit(m, n, n, 0)
                maxima(nA + 2, 0)

                def body(g, h, r):
                    n = 0
                    for kt in range(KB):
                        if kt == 6:
                            maxima(g * NU + (nA + 2 + nA + 2 + 2), g + 1)
                        else:
                            for m in plan[kt]:
                                unit(m, nA + 2 + n, g * NU + (nA + 2 + n), g)
                                n += 1
                        if kt % 2 == 0:
                            rests(eng, g, kt, l_vec)

                each_head(eng, body)
                for n in range(2):
                    unit(("C", n), nA + n, nA + 2 + HEADS * NU + n, HEADS)


def output_phase(nc, signals, name, cx, x, w_o, b_o, consts):
    with Phase(nc, signals, name) as ph:
        wo = ph.sb("wo", [P, KT, D])
        bo = ph.sb("bo", [1, D])
        cs = [ph.sb(f"cs{u}", [P, D]) for u in range(2)]
        cT = [ph.sb(f"cT{u}", [P, KT, P]) for u in range(2)]
        psC = [ph.ps(f"psC{u}", [P, KT, P]) for u in range(2)]
        psY = [ph.ps(f"psY{u}", [P, D]) for u in range(2)]
        loaded = ph.sig("weights_loaded", 32)
        staged = ph.sig("context_staged", NT)
        c_psum = ph.sig("context_transposed", NT)
        c_ready = ph.sig("context_turned", NT)
        y_psum = ph.sig("output_in_psum", NT)
        y_added = ph.sig("output_added", NT)

        with nc.Block() as block:
            @block.sync
            def _(eng):
                eng.dma_start(wo[:], w_o).then_inc(loaded.sem, 16)
                eng.dma_start(bo[:], b_o).then_inc(loaded.sem, 16)

            @block.gpsimd
            def _(eng):
                with eng.Fori(0, B) as b:
                    for j in range(TB):
                        if j >= 2:
                            eng.wait_ge(c_psum.sem, c_psum.at(b * TB + (j - 1)))
                        eng.tensor_copy(cs[j % 2][:].rearrange("p (h d) -> p h d", d=DK),
                                        cx[:, bass.ds(b * H + 1, H), j, :]).then_inc(staged.sem, 1)
                    eng.wait_ge(c_psum.sem, c_psum.at(b * TB + TB))

            @block.tensor
            def _(eng):
                eng.wait_ge(loaded.sem, loaded.at(32))
                with eng.Fori(0, B) as b:
                    for s in range(TB + 1):
                        if s < TB:
                            u = s % 2
                            eng.wait_ge(staged.sem, staged.at(b * TB + (s + 1)))
                            if s >= 2:
                                eng.wait_ge(c_ready.sem, c_ready.at(b * TB + (s - 1)))
                            for k in range(KT):
                                mm = eng.transpose(psC[u][:, k, :], cs[u][:, k * P:(k + 1) * P], consts["ident"][:])
                            mm.then_inc(c_psum.sem, 1)
                        if s >= 1:
                            u = (s - 1) % 2
                            eng.wait_ge(c_ready.sem, c_ready.at(b * TB + s))
                            if s >= 3:
                                eng.wait_ge(y_added.sem, y_added.at(b * TB + (s - 2)))
                            eng.matmul(psY[u][:], consts["ones"][0:1, 0:P], bo[:], start=True, stop=False)
                            for k in range(KT):
                                mm = eng.matmul(psY[u][:], cT[u][:, k, :], wo[:, k, :], start=False, stop=(k == KT - 1))
                            mm.then_inc(y_psum.sem, 1)
                    eng.wait_ge(y_added.sem, y_added.at(b * TB + TB))

            @block.scalar
            def _(eng):
                with eng.Fori(0, B) as b:
                    for j in range(TB):
                        eng.wait_ge(c_psum.sem, c_psum.at(b * TB + (j + 1)))
                        if j >= 2:
                            eng.wait_ge(y_psum.sem, y_psum.at(b * TB + (j - 1)))
                        eng.activation(cT[j % 2][:], psC[j % 2][:], ACT.Copy).then_inc(c_ready.sem, 1)
                    eng.wait_ge(y_psum.sem, y_psum.at(b * TB + TB))

            @block.vector
            def _(eng):
                with eng.Fori(0, B) as b:
                    for j in range(TB):
                        eng.wait_ge(y_psum.sem, y_psum.at(b * TB + (j + 1)))
                        xt = x[:, b * TB + j, :]
                        eng.tensor_tensor(xt, xt, psY[j % 2][:], ALU.add).then_inc(y_added.sem, 1)


def router_phase(nc, signals, name, hT, gates, w_r, b_r, consts):
    chunks = NT * P // CH
    with Phase(nc, signals, name) as ph:
        wr = ph.sb("wr", [P, KT, E])
        br = ph.sb("br", [E, 1])
        lT = [ph.sb(f"lT{u}", [E, CH]) for u in range(2)]
        lg = ph.sb("logits", [P, NT, E])
        rank = ph.sb("rank", [P, E])
        one = [ph.sb(f"onehot{i}", [P, NT, E]) for i in range(2)]
        wt = ph.sb("weighted", [P, NT, E])
        m = [ph.sb(f"m{i}", [P, NT]) for i in range(5)]
        psL = [ph.ps(f"psL{u}", [P, CH]) for u in range(2)]
        psT = [ph.ps(f"psT{u}", [P, 4, E]) for u in range(2)]
        loaded = ph.sig("weights_loaded", 48)
        l_psum = ph.sig("logits_in_psum", chunks)
        l_ready = ph.sig("logits_biased", chunks)
        t_psum = ph.sig("logits_transposed", chunks)
        t_read = ph.sig("logits_read", chunks)
        step = ph.sig("gate_step", 17)
        exped = ph.sig("gate_exp", 1)
        with nc.Block() as block:
            @block.sync
            def _(eng):
                eng.dma_start(wr[:], w_r).then_inc(loaded.sem, 16)
                eng.dma_start(br[:], b_r).then_inc(loaded.sem, 16)
                eng.dma_start(rank[:], consts["rank"]).then_inc(loaded.sem, 16)

            @block.tensor
            def _(eng):
                eng.wait_ge(loaded.sem, loaded.at(48))
                for c in range(chunks + 1):
                    if c < chunks:
                        if c >= 2:
                            eng.wait_ge(l_ready.sem, l_ready.at(c - 1))
                        for k in range(KT):
                            mm = eng.matmul(psL[c % 2][0:E, :], wr[:, k, :], hT[:, k, c * CH:(c + 1) * CH],
                                            start=(k == 0), stop=(k == KT - 1))
                        mm.then_inc(l_psum.sem, 1)
                    if c >= 1:
                        u = (c - 1) % 2
                        eng.wait_ge(l_ready.sem, l_ready.at(c))
                        if c >= 3:
                            eng.wait_ge(t_read.sem, t_read.at(c - 2))
                        for j in range(4):
                            mm = eng.transpose(psT[u][:, j, :], lT[u][:, j * P:(j + 1) * P], consts["ident"][0:E, 0:E])
                        mm.then_inc(t_psum.sem, 1)

            @block.scalar
            def _(eng):
                eng.wait_ge(loaded.sem, loaded.at(48))
                for c in range(chunks):
                    eng.wait_ge(l_psum.sem, l_psum.at(c + 1))
                    if c >= 2:
                        eng.wait_ge(t_psum.sem, t_psum.at(c - 1))
                    eng.activation(lT[c % 2][:], psL[c % 2][0:E, :], ACT.Identity, bias=br[:], scale=1.0)\
                       .then_inc(l_ready.sem, 1)
                eng.wait_ge(step.sem, step.at(12))
                eng.activation(m[2][:], m[2][:], ACT.Exp).then_inc(exped.sem, 1)

            @block.vector
            def _(eng):
                for c in range(chunks):
                    eng.wait_ge(t_psum.sem, t_psum.at(c + 1))
                    eng.tensor_copy(lg[:, c * 4:(c + 1) * 4, :], psT[c % 2][:]).then_inc(t_read.sem, 1)
                eng.wait_ge(t_read.sem, t_read.at(chunks))
                eng.wait_ge(loaded.sem, loaded.at(48))
                ranks = rank[:].unsqueeze(1).to_broadcast([P, NT, E])

                def wide(v):
                    return v[:].unsqueeze(2).to_broadcast([P, NT, E])

                n = 0
                for i in range(2):
                    eng.tensor_reduce(m[i][:], lg[:], AX.X, ALU.max).then_inc(step.sem, 1)
                    eng.wait_ge(step.sem, step.at(n + 1))
                    eng.tensor_tensor(wt[:], lg[:], wide(m[i]), ALU.is_equal).then_inc(step.sem, 1)
                    eng.wait_ge(step.sem, step.at(n + 2))
                    eng.tensor_tensor(wt[:], wt[:], ranks, ALU.mult).then_inc(step.sem, 1)
                    eng.wait_ge(step.sem, step.at(n + 3))
                    eng.tensor_reduce(m[4][:], wt[:], AX.X, ALU.max).then_inc(step.sem, 1)
                    eng.wait_ge(step.sem, step.at(n + 4))
                    eng.tensor_tensor(one[i][:], wt[:], wide(m[4]), ALU.is_equal).then_inc(step.sem, 1)
                    eng.wait_ge(step.sem, step.at(n + 5))
                    n += 5
                    if i == 0:
                        eng.scalar_tensor_tensor(lg[:], one[0][:], NEG, lg[:], ALU.mult, ALU.add).then_inc(step.sem, 1)
                        n += 1
                        eng.wait_ge(step.sem, step.at(n))
                eng.tensor_tensor(m[2][:], m[1][:], m[0][:], ALU.subtract).then_inc(step.sem, 1)
                eng.wait_ge(exped.sem, exped.at(1))
                eng.tensor_scalar(m[3][:], m[2][:], 1.0, None, ALU.add).then_inc(step.sem, 1)
                eng.wait_ge(step.sem, step.at(13))
                eng.reciprocal(m[3][:], m[3][:]).then_inc(step.sem, 1)
                eng.wait_ge(step.sem, step.at(14))
                eng.tensor_tensor(m[2][:], m[2][:], m[3][:], ALU.mult).then_inc(step.sem, 1)
                eng.tensor_tensor(one[0][:], one[0][:], wide(m[3]), ALU.mult).then_inc(step.sem, 1)
                eng.wait_ge(step.sem, step.at(16))
                eng.tensor_tensor(one[1][:], one[1][:], wide(m[2]), ALU.mult).then_inc(step.sem, 1)
                eng.wait_ge(step.sem, step.at(17))
                eng.tensor_tensor(gates[:], one[0][:], one[1][:], ALU.add)


def feed_forward_phase(nc, signals, name, hT, x, rows, tokens, experts, w_1, w_2, b_1, b_2, func, consts, gates=None):
    cw = min(CH, tokens)
    chunks = tokens // cw
    tpc = cw // rows
    UC = min(2, chunks)
    UE = min(2, experts)
    with Phase(nc, signals, name) as ph:
        w1 = [ph.sb(f"w1{v}", [P, KT, FF]) for v in range(UE)]
        w2 = [ph.sb(f"w2{v}", [P, FT, D]) for v in range(UE)]
        b1 = [ph.sb(f"b1{v}", [P, FT]) for v in range(UE)]
        b2 = [ph.sb(f"b2{v}", [1, D]) for v in range(UE)]
        h1 = [ph.sb(f"h1{u}", [P, FT, cw]) for u in range(UC)]
        ps1 = [ph.ps(f"ps1{i}", [P, CH]) for i in range(4)]
        ps2 = [ph.ps(f"ps2{i}", [P, 512]) for i in range(2)]
        n_hidden = experts * chunks * FT
        n_out = experts * chunks * tpc
        loaded = [ph.sig(f"expert_loaded{v}", 64 * experts // UE) for v in range(UE)]
        h_psum = ph.sig("hidden_in_psum", n_hidden)
        h_ready = ph.sig("hidden_ready", 4 + n_hidden)
        y_psum = ph.sig("output_in_psum", UC * tpc + n_out)
        y_added = ph.sig("output_added", 2 + n_out)
        expert_done = ph.sig("expert_done", UE + experts if experts > 1 else 0)
        H_FREE, Y_FREE, OUT_FREE = 4, 2, UC * tpc

        def each_chunk(eng, body):
            def chunk_loop(e, v):
                if chunks == UC:
                    for u in range(UC):
                        body(e, v, e * chunks + u, u, u)
                else:
                    with eng.Fori(0, chunks // UC) as pair:
                        c = pair * UC
                        for u in range(UC):
                            body(e, v, e * chunks + c + u, c + u, u)
            if experts == 1:
                chunk_loop(0, 0)
            else:
                with eng.Fori(0, experts // UE) as group:
                    e0 = group * UE
                    for v in range(UE):
                        chunk_loop(e0 + v, v)

        with nc.Block() as block:
            @block.sync
            def _(eng):
                def load(e, v):
                    if experts > 1:
                        eng.wait_ge(expert_done.sem, expert_done.at(e + 1))
                    sel = bass.ds(e, 1)
                    eng.dma_start(w1[v][:], w_1[sel].rearrange("e (k p) n -> p (e k) n", p=P)).then_inc(loaded[v].sem, 16)
                    eng.dma_start(w2[v][:], w_2[sel].rearrange("e (k p) n -> p (e k) n", p=P)).then_inc(loaded[v].sem, 16)
                    eng.dma_start(b1[v][:], b_1[sel].rearrange("e p m -> p (e m)")).then_inc(loaded[v].sem, 16)
                    eng.dma_start(b2[v][:], b_2[sel, :]).then_inc(loaded[v].sem, 16)

                if experts == 1:
                    load(0, 0)
                else:
                    with eng.Fori(0, experts // UE) as group:
                        e0 = group * UE
                        for v in range(UE):
                            load(e0 + v, v)

            @block.tensor
            def _(eng):
                eng.sem_inc(y_psum.sem, OUT_FREE)
                if experts > 1:
                    eng.sem_inc(expert_done.sem, UE)

                def body(e, v, n, c, u):
                    eng.wait_ge(loaded[v].sem, loaded[v].at((e - v) * (64 // UE) + 64))
                    for m in range(FT):
                        eng.wait_ge(h_ready.sem, h_ready.at(n * FT + (m + 1)))
                        for k in range(KT):
                            mm = eng.matmul(ps1[m % 4][:, 0:cw], w1[v][:, k, m * P:(m + 1) * P],
                                            hT[:, k, bass.ds(c * cw, cw)], start=(k == 0), stop=(k == KT - 1))
                        mm.then_inc(h_psum.sem, 1)
                    for j in range(tpc):
                        eng.wait_ge(y_added.sem, y_added.at(n * tpc + (j + 1)))
                        eng.matmul(ps2[j % 2][0:rows, 0:D], consts["ones"][0:1, 0:rows], b2[v][:], start=True, stop=False)
                        for m in range(FT):
                            if j == 0:
                                eng.wait_ge(h_ready.sem, h_ready.at(n * FT + (m + 1 + H_FREE)))
                            mm = eng.matmul(ps2[j % 2][0:rows, 0:D], h1[u][:, m, j * rows:(j + 1) * rows], w2[v][:, m, :],
                                            start=False, stop=(m == FT - 1))
                        mm.then_inc(y_psum.sem, 1)

                if experts == 1:
                    each_chunk(eng, body)
                else:
                    with eng.Fori(0, experts // UE) as group:
                        e0 = group * UE
                        for v in range(UE):
                            with eng.Fori(0, chunks // UC) as pair:
                                c = pair * UC
                                for u in range(UC):
                                    body(e0 + v, v, (e0 + v) * chunks + c + u, c + u, u)
                            eng.drain().then_inc(expert_done.sem, 1)

            @block.scalar
            def _(eng):
                eng.sem_inc(h_ready.sem, H_FREE)

                def body(e, v, n, c, u):
                    eng.wait_ge(y_psum.sem, y_psum.at(n * tpc + tpc))
                    for m in range(FT):
                        eng.wait_ge(h_psum.sem, h_psum.at(n * FT + (m + 1)))
                        eng.activation(h1[u][:, m, :], ps1[m % 4][:, 0:cw], func, bias=b1[v][:, m:m + 1], scale=1.0)\
                           .then_inc(h_ready.sem, 1)

                each_chunk(eng, body)

            @block.vector
            def _(eng):
                eng.sem_inc(y_added.sem, Y_FREE)

                def body(e, v, n, c, u):
                    for j in range(tpc):
                        eng.wait_ge(y_psum.sem, y_psum.at(n * tpc + (j + 1 + OUT_FREE)))
                        eng.wait_ge(y_added.sem, y_added.at(n * tpc + (j + Y_FREE)))
                        xt = x[0:rows, c * tpc + j, :]
                        if gates is None:
                            eng.tensor_tensor(xt, xt, ps2[j % 2][0:rows, 0:D], ALU.add).then_inc(y_added.sem, 1)
                        else:
                            gate = gates[:, c * tpc + j, bass.ds(e, 1)]
                            eng.scalar_tensor_tensor(xt, ps2[j % 2][0:rows, 0:D], gate, xt, ALU.mult, ALU.add)\
                               .then_inc(y_added.sem, 1)

                each_chunk(eng, body)


def build(nc, d, places, out):
    with ExitStack() as ctx:
        def sb(name, shape, dt=F32):
            return ctx.enter_context(nc.sbuf_tensor(name, shape, dt))

        signals = Signals(nc, ctx)
        x = sb("x_res", [P, NT, D])
        big = sb("wide", [P, (B * H + 1) * TB * DK])
        hT = big[:, 0:KT * NT * P].rearrange("p (k t) -> p k t", k=KT)
        cx = big[:].rearrange("p (g j d) -> p g j d", j=TB, d=DK)
        gates = sb("gates", [P, NT, E])
        Qd = nc.dram_tensor("q_pieces", [3, B * D + 2 * DK, SQ], BF16)
        Kd = nc.dram_tensor("k_pieces", [3, B * D + 2 * DK, SQ], BF16)
        Vd = nc.dram_tensor("v_pieces", [B * H + 2, P, TB, VW + 1], BF16)
        cT = sb("contextT", [P, KT, B * SC])
        consts = {"ident": sb("ident", [P, P]), "ones": sb("ones", [1, P]), "head_rows": sb("head_rows", [P, HT]),
                  "minus_half": sb("minus_half", [P, NT]),
                  "identb": sb("identb", [P, P], BF16), "combine": sb("combine", [VW, DK + 1])}
        xe = sb("encoder", [SC, B, D])
        xd = d["x"].rearrange("b s d -> (b s) d").rearrange("(t p) d -> p t d", p=P)
        packed = sb("packed_columns", [P, d["columns"].shape[1]])
        start_loaded = signals("start_loaded", 16 * 10)
        with nc.Block() as block:
            @block.sync
            def _(eng):
                eng.dma_start(packed[:], d["columns"]).then_inc(start_loaded.sem, 16)
                eng.dma_start(consts["ident"][:], d["ident"]).then_inc(start_loaded.sem, 16)
                eng.dma_start(consts["minus_half"][:], d["minus_half"]).then_inc(start_loaded.sem, 16)
                eng.dma_start(consts["ones"][:], d["ones"]).then_inc(start_loaded.sem, 16)
                eng.dma_start(consts["head_rows"][:], d["head_rows"]).then_inc(start_loaded.sem, 16)
                eng.dma_start(cT[:], d["ctxT"].rearrange("(k p) c -> p k c", p=P)).then_inc(start_loaded.sem, 16)
                eng.dma_start(hT[:], d["xT"].rearrange("(k p) t -> p k t", p=P)).then_inc(start_loaded.sem, 16)
                eng.dma_start(x[:], xd).then_inc(start_loaded.sem, 16)
                eng.dma_start(consts["combine"][:], d["combine"]).then_inc(start_loaded.sem, 16)
                eng.dma_start(xe[:], d["ctx"].rearrange("b c d -> c b d")).then_inc(start_loaded.sem, 16)
                eng.wait_ge(start_loaded.sem, start_loaded.at(16 * 10))

            @block.vector
            def _(eng):
                eng.wait_ge(start_loaded.sem, start_loaded.at(16 * 10))
                eng.tensor_copy(consts["identb"][:], consts["ident"][:])
        signals.phase_over()

        def cols(name):
            at, n = places[name]
            return packed[:, at:at + n]

        def weights(name):
            return d[name].rearrange("(k p) n -> p k n", p=P)

        consts["rank"] = d["rank"]

        def cross(name, sT, x_to, rows, tiles, hT_from, bias=None, rope=None):
            pair = range(2) if rope else range(1)
            tag = ("", "_turned")
            with ExitStack() as heads:
                Kbd = heads.enter_context(nc.sbuf_tensor(name + "_Kbd", [P, B, KT, HT * SC], F32))
                Vbd = heads.enter_context(nc.sbuf_tensor(name + "_Vbd", [P, B, H // 2, PW], F32))
                context_heads_phase(nc, signals, name + "kv", sT, [weights(name + "_wk" + tag[r]) for r in pair],
                                    weights(name + "_wv"), [cols(name + "_bk" + tag[r]) for r in pair],
                                    d[name + "_bv"], consts, Kbd, Vbd, rope=rope and rope[1])
                cross_attention_phase(nc, signals, name + "at", hT_from, x_to, rows, tiles,
                                      [weights(name + "_wq" + tag[r]) for r in pair],
                                      [cols(name + "_bq" + tag[r]) for r in pair], weights(name + "_wo"),
                                      d[name + "_bo"], Kbd, Vbd, consts, bias=bias, rope=rope and rope[0])

        def self_attention(name, causal, near=None, rope=None):
            pair = range(2) if rope else range(1)
            tag = ("", "_turned")
            self_heads_phase(nc, signals, name + "qkv", hT, [weights(name + "_wq" + tag[r]) for r in pair],
                             [weights(name + "_wk" + tag[r]) for r in pair], weights(name + "_wv"),
                             [cols(name + "_bq" + tag[r]) for r in pair],
                             [cols(name + "_bk" + tag[r]) for r in pair], d[name + "_bv"], consts,
                             Qd, Kd, Vd, rope=rope)
            self_attention_phase(nc, signals, name + "at", Qd, Kd, Vd, cx, consts, causal, near)
            output_phase(nc, signals, name + "out", cx, x, weights(name + "_wo"), d[name + "_bo"], consts)

        def norm(name):
            return cols(name + "_g"), cols(name + "_b")

        cross("L0", cT, x, P, TB, hT)
        output_norm_phase(nc, signals, "L0ln", x, consts, d["L0_gamma"], d["L0_beta"], 1e-5)

        transpose_phase(nc, signals, "L1t1", x, hT, consts, P, NT, norm("L1_n1"))
        self_attention("L1sa", False)
        transpose_phase(nc, signals, "L1t2", x, hT, consts, P, NT, norm("L1_n2"))
        with ExitStack() as normed:
            nT = normed.enter_context(nc.sbuf_tensor("L1_contextT", [P, KT, B * SC], F32))
            transpose_phase(nc, signals, "L1t3", xe, nT, consts, SC, B, norm("L1_nc"))
            cross("L1ca", nT, x, P, TB, hT)
        transpose_phase(nc, signals, "L1t4", x, hT, consts, P, NT, norm("L1_n3"))
        router_phase(nc, signals, "L1r", hT, gates, weights("L1_wr"), d["L1_br"], consts)
        feed_forward_phase(nc, signals, "L1ff", hT, x, P, NT * P, E, d["L1_w1"], d["L1_w2"], d["L1_b1"],
                           d["L1_b2"], ACT.Gelu, consts, gates=gates)

        with ExitStack() as encoder:
            nT = encoder.enter_context(nc.sbuf_tensor("L2_contextT", [P, KT, B * SC], F32))
            transpose_phase(nc, signals, "L2e1", xe, nT, consts, SC, B, norm("L2_e1"), 1e-6)
            cross("L2e", nT, xe, SC, 1, nT, bias=(d["L2_enc_bias"], 1))
            transpose_phase(nc, signals, "L2e2", xe, nT, consts, SC, B, norm("L2_e2"), 1e-6)
            feed_forward_phase(nc, signals, "L2ef", nT, xe, SC, B * SC, 1, d["L2e_w1"], d["L2e_w2"],
                               d["L2e_b1"], d["L2e_b2"], ACT.Relu, consts)
            transpose_phase(nc, signals, "L2e3", xe, nT, consts, SC, B)
            transpose_phase(nc, signals, "L2t1", x, hT, consts, P, NT, norm("L2_n1"), 1e-6)
            with ExitStack() as tables:
                q_near = tables.enter_context(nc.sbuf_tensor("q_near", [P, H + 1, 2 * P], BF16))
                k_near = [tables.enter_context(nc.sbuf_tensor(f"k_near{i}", [P, H + 1, 2 * P], BF16))
                          for i in range(3)]
                near_blocks_phase(nc, signals, "L2nb", d["L2_rel_q"], d["L2_rel_k"], d["L2_rel_far"],
                                  d["near_mask_q"], d["near_mask_k"], q_near, k_near)
                self_attention("L2sa", True, near=(q_near, k_near, True, True))
            transpose_phase(nc, signals, "L2t2", x, hT, consts, P, NT, norm("L2_n2"), 1e-6)
            cross("L2ca", nT, x, P, TB, hT, bias=(d["L2_cross_bias"], 3))
        transpose_phase(nc, signals, "L2t3", x, hT, consts, P, NT, norm("L2_n3"), 1e-6)
        feed_forward_phase(nc, signals, "L2ff", hT, x, P, NT * P, 1, d["L2_w1"], d["L2_w2"], d["L2_b1"],
                           d["L2_b2"], ACT.Relu, consts)

        with ExitStack() as rotary:
            turn = {}
            for part in ("q_cos", "q_sin", "k_cos", "k_sin"):
                turn[part] = rotary.enter_context(nc.sbuf_tensor("turn_" + part, [P, SQ], F32))
            mask = [rotary.enter_context(nc.sbuf_tensor("diagonal_" + part, [P, P], BF16)) for part in "qk"]
            with Phase(nc, signals, "L3l") as ph:
                mask_f = [ph.sb("mask_" + part, [P, P]) for part in "qk"]
                loaded = ph.sig("weights_loaded", 16 * 6)
                with nc.Block() as block:
                    @block.sync
                    def _(eng):
                        for part, tile in turn.items():
                            eng.dma_start(tile[:], d["turn_" + part]).then_inc(loaded.sem, 16)
                        eng.dma_start(mask_f[0][:], d["near_mask_q"][:, P:2 * P]).then_inc(loaded.sem, 16)
                        eng.dma_start(mask_f[1][:], d["near_mask_k"][:, 0:P]).then_inc(loaded.sem, 16)

                    @block.vector
                    def _(eng):
                        eng.wait_ge(loaded.sem, loaded.at(16 * 6))
                        for i in range(2):
                            eng.tensor_copy(mask[i][:], mask_f[i][:])
            rope = ((turn["q_cos"], turn["q_sin"]), (turn["k_cos"], turn["k_sin"]))
            transpose_phase(nc, signals, "L3t1", x, hT, consts, P, NT, norm("L3_n1"))
            self_attention("L3sa", True, near=(mask[0], [mask[1]], False, False), rope=rope)
            transpose_phase(nc, signals, "L3t2", x, hT, consts, P, NT, norm("L3_n2"))
            cross("L3ca", cT, x, P, TB, hT, rope=rope)
        transpose_phase(nc, signals, "L3t3", x, hT, consts, P, NT, norm("L3_n3"))
        feed_forward_phase(nc, signals, "L3ff", hT, x, P, NT * P, 1, d["L3_w1"], d["L3_w2"], d["L3_b1"],
                           d["L3_b2"], ACT.Gelu_apprx_tanh, consts)

        written = signals("output_written", 16)
        with nc.Block() as block:
            @block.sync
            def _(eng):
                eng.dma_start(out.rearrange("b s d -> (b s) d").rearrange("(t p) d -> p t d", p=P), x[:])\
                   .then_inc(written.sem, 16)
                eng.wait_ge(written.sem, written.at(16))


def lay_out(inp):
    a, places, packed = {}, {}, []

    def columns(name, v):
        v = v.reshape(-1, P).T
        places[name] = (sum(c.shape[1] for c in packed), v.shape[1])
        packed.append(v)

    a["x"] = inp["x"]
    a["xT"] = np.ascontiguousarray(inp["x"].reshape(B * SQ, D).T)
    a["ctxT"] = np.ascontiguousarray(inp["ctx_1024"].reshape(B * SC, D).T)
    a["ident"] = np.eye(P, dtype=np.float32)
    a["minus_half"] = np.full((P, NT), -0.5, np.float32)
    a["ones"] = np.ones((1, P), np.float32)
    a["head_rows"] = np.repeat(np.eye(HT, dtype=np.float32), DK, axis=0)

    def packed_attention(name, w, b, wo, bo):
        for i, part in enumerate("qkv"):
            a[f"{name}_w{part}"] = np.ascontiguousarray(w[i * D:(i + 1) * D].T)
            rows = b[i * D:(i + 1) * D]
            if part == "v":
                a[f"{name}_bv"] = rows.reshape(1, D)
            else:
                columns(f"{name}_b{part}", rows)
        a[f"{name}_wo"] = np.ascontiguousarray(wo.T)
        a[f"{name}_bo"] = bo.reshape(1, D)

    packed_attention("L0", inp["L0_xattn_W_qkv"], inp["L0_xattn_b_qkv"], inp["L0_xattn_W_o"], inp["L0_xattn_b_o"])
    a["L0_gamma"] = inp["L0_xattn_ln_gamma"]
    a["L0_beta"] = inp["L0_xattn_ln_beta"]
    a["ctx"] = inp["ctx_1024"]
    combine = np.zeros((VW, DK + 1), np.float32)
    for part in range(3):
        combine[part * DK:(part + 1) * DK, 0:DK] = np.eye(DK, dtype=np.float32)
    combine[VW - 1, DK] = 1.0
    a["combine"] = combine
    a["rank"] = np.tile(np.arange(E, 0, -1, dtype=np.float32), (P, 1))

    def norm(name, g, b):
        columns(name + "_g", inp[g])
        columns(name + "_b", inp[b])

    def feed_forward(name, w1, b1, w2, b2):
        a[name + "_w1"], a[name + "_w2"] = np.ascontiguousarray(w1), np.ascontiguousarray(w2)
        a[name + "_b1"] = np.ascontiguousarray(b1.reshape(-1, FT, P).transpose(0, 2, 1))
        a[name + "_b2"] = b2.reshape(-1, D)

    L = "L1_xattn_"
    norm("L1_n1", L + "sa_ln_g", L + "sa_ln_b")
    norm("L1_n2", L + "ca_q_ln_g", L + "ca_q_ln_b")
    norm("L1_nc", L + "ca_kv_ln_g", L + "ca_kv_ln_b")
    norm("L1_n3", L + "moe_ln_g", L + "moe_ln_b")
    packed_attention("L1sa", *(inp[L + n] for n in ("sa_in_w", "sa_in_b", "sa_out_w", "sa_out_b")))
    packed_attention("L1ca", *(inp[L + n] for n in ("ca_in_w", "ca_in_b", "ca_out_w", "ca_out_b")))
    a["L1_wr"] = np.ascontiguousarray(inp[L + "router_w"].T)
    a["L1_br"] = inp[L + "router_b"].reshape(E, 1)
    feed_forward("L1", inp[L + "e_fc1_w"].transpose(0, 2, 1), inp[L + "e_fc1_b"], inp[L + "e_fc2_w"].transpose(0, 2, 1),
                 inp[L + "e_fc2_b"])

    L = "L2_xattn_"
    norm("L2_e1", L + "enc_n1_s", L + "enc_n1_b")
    norm("L2_e2", L + "enc_n2_s", L + "enc_n2_b")
    for i in "123":
        norm("L2_n" + i, L + f"dec_n{i}_s", L + f"dec_n{i}_b")
    packed_attention("L2e", *(inp[L + n] for n in ("enc_in_w", "enc_in_b", "enc_out_w", "enc_out_b")))
    packed_attention("L2sa", *(inp[L + n] for n in ("dec_sa_in_w", "dec_sa_in_b", "dec_sa_out_w", "dec_sa_out_b")))
    packed_attention("L2ca", *(inp[L + n] for n in ("dec_ca_in_w", "dec_ca_in_b", "dec_ca_out_w", "dec_ca_out_b")))
    for name, part in (("L2e", "enc"), ("L2", "dec")):
        feed_forward(name, inp[L + part + "_ff1_w"].T[None], inp[L + part + "_ff1_b"],
                     inp[L + part + "_ff2_w"].T[None], inp[L + part + "_ff2_b"])

    def rows_of(queries, keys):
        ahead = keys - queries
        return np.where(ahead < 0, np.minimum(-ahead, P - 1), np.minimum(ahead, P - 1) + P)

    def laid(table, queries, keys):
        return np.ascontiguousarray(table[rows_of(queries, keys)].transpose(0, 2, 1))

    at, to, near = np.arange(P)[:, None], np.arange(SC)[None, :], np.arange(2 * P)[None, :]
    a["L2_enc_bias"] = laid(inp[L + "enc_rel"], at[0:SC], to).reshape(SC, 1, H * SC)
    a["L2_cross_bias"] = np.ascontiguousarray(np.stack(
        [laid(inp[L + "dec_rel_cross"], at + P * j, to).reshape(P, H * SC) for j in range(3)], axis=1))
    rel = inp[L + "dec_rel_self"][:, list(range(H)) + [0]]
    a["L2_rel_q"] = laid(rel, at + P, near)
    a["L2_rel_k"] = laid(rel, near, at)
    a["L2_rel_far"] = np.ascontiguousarray(rel[P - 1])
    a["near_mask_q"] = np.where(near > at + P, MASKED, 0.0).astype(np.float32)
    a["near_mask_k"] = np.where(at > near, MASKED, 0.0).astype(np.float32)

    L = "L3_xattn_"
    for i in "123":
        norm("L3_n" + i, L + f"ln{i}_g", L + f"ln{i}_b")
    swap = (np.arange(D) // DK) * DK + (np.arange(D) % DK + DK // 2) % DK
    for part in ("sa", "ca"):
        for w in "qk":
            weight, bias = inp[L + f"{part}_w{w}"], inp[L + f"{part}_b{w}"]
            a[f"L3{part}_w{w}"] = weight
            a[f"L3{part}_w{w}_turned"] = np.ascontiguousarray(weight[:, swap])
            columns(f"L3{part}_b{w}", bias)
            columns(f"L3{part}_b{w}_turned", bias[swap])
        a[f"L3{part}_wv"], a[f"L3{part}_bv"] = inp[L + part + "_wv"], inp[L + part + "_bv"].reshape(1, D)
        a[f"L3{part}_wo"], a[f"L3{part}_bo"] = inp[L + part + "_wo"], inp[L + part + "_bo"].reshape(1, D)
    frequency = np.float32(1.0) / np.float32(10000.0) ** (np.arange(0, DK, 2, dtype=np.float32) / np.float32(DK))
    angle = np.outer(np.arange(SQ, dtype=np.float32), frequency).astype(np.float32)
    cos = np.tile(np.cos(angle).T, (2 * HT, 1)).astype(np.float32)
    sin = np.tile(np.concatenate([-np.sin(angle), np.sin(angle)], axis=1).T, (HT, 1)).astype(np.float32)
    a["turn_k_cos"], a["turn_k_sin"] = cos, sin
    a["turn_q_cos"], a["turn_q_sin"] = cos * np.float32(SCALE), sin * np.float32(SCALE)
    feed_forward("L3", inp[L + "fc1_w"][None], inp[L + "fc1_b"], inp[L + "fc2_w"][None], inp[L + "fc2_b"])
    a["columns"] = np.ascontiguousarray(np.concatenate(packed, axis=1))
    return a, places


def kernel(**inputs):
    import concourse.bacc as bacc
    from concourse.bass_utils import run_bass_kernel_spmd

    nc = bacc.Bacc("TRN2", target_bir_lowering=False, num_devices=1)
    arrays, places = lay_out({k: np.asarray(v) for k, v in inputs.items()})
    d = {}
    for name, a in arrays.items():
        d[name] = nc.dram_tensor("in_" + name, a.shape, mybir.dt.from_np(a.dtype), kind="ExternalInput").ap()
    out = nc.dram_tensor("out", (B, SQ, D), F32, kind="ExternalOutput").ap()
    build(nc, d, places, out)
    r = run_bass_kernel_spmd(nc, [{"in_" + k: v for k, v in arrays.items()}], core_ids=[0])
    return r.results[0]["out"]
```

```python
from contextlib import ExitStack

import numpy as np
import concourse.bass as bass
from concourse import mybir

F32 = mybir.dt.float32
BF16 = mybir.dt.bfloat16
F16 = mybir.dt.float16
U32 = mybir.dt.uint32
I32 = mybir.dt.int32
ALU = mybir.AluOpType
ACT = mybir.ActivationFunctionType
AX = mybir.AxisListType

P = 128
D = 256
KT = D // P
H = 16
DK = D // H
HT = P // DK
B = 4
SQ = 1024
SC = 64
NT = B * SQ // P
TB = SQ // P
FF = 1024
FT = FF // P
E = 8
CH = 512
BS = 256
NB = 2 * NT * P // BS + E
SCALE = DK ** -0.5
PIECES = 6
KS = PIECES * DK
Q_PART = (0, 0, 0, 1, 1, 2)
K_PART = (0, 1, 2, 0, 1, 0)
VW = 3 * DK + 1
PW = 2 * (DK + 1)
NEG = -3.0e38
MASKED = -1.0e30
ZERO = 1376


class Signal:

    def __init__(self, sem):
        self.sem, self.base, self.total = sem, 0, 0

    def at(self, n):
        return self.base + n


class Signals:

    def __init__(self, nc, ctx):
        self.nc, self.ctx, self.known = nc, ctx, {}

    def __call__(self, name, total):
        if name not in self.known:
            self.known[name] = Signal(self.ctx.enter_context(self.nc.semaphore(name)))
        s = self.known[name]
        assert s.total == 0, name
        s.total = total
        return s

    def phase_over(self):
        for s in self.known.values():
            s.base, s.total = s.base + s.total, 0


class Phase:

    def __init__(self, nc, signals, name):
        self.nc, self.signals, self.name = nc, signals, name
        self.ctx = ExitStack()

    def __enter__(self):
        return self

    def __exit__(self, *a):
        self.ctx.close()
        self.signals.phase_over()
        return False

    def sb(self, name, shape, dt=F32):
        return self.ctx.enter_context(self.nc.sbuf_tensor(f"{self.name}_{name}", shape, dt))

    def ps(self, name, shape, dt=F32):
        return self.ctx.enter_context(self.nc.psum_tensor(f"{self.name}_{name}", shape, dt))

    def sig(self, name, total):
        return self.signals(name, total)


def load_all(eng, pairs, loaded):
    for dst, src in pairs:
        eng.dma_start(dst, src).then_inc(loaded.sem, 16)


MOMENT_STEPS = 6
GROUP = 8
QUAD = 4


class Statistics:

    def __init__(self, ph, x, rows, tiles, eps, minus_half, moments=None):
        self.x, self.rows, self.eps, self.minus_half = x, rows, eps, minus_half
        self.group = min(GROUP, tiles)
        self.groups = tiles // self.group
        self.raw = ph.sb("raw", [P, tiles, 6])
        self.mean = moments[0] if moments else ph.sb("mean", [P, tiles])
        self.spread = ph.sb("spread", [P, tiles])
        self.rstd = moments[1] if moments else ph.sb("rstd", [P, tiles])
        self.stats_done = ph.sig("stats_done", self.groups)
        self.moments_step = ph.sig("moments_step", MOMENT_STEPS * self.groups)
        self.rstd_done = ph.sig("rstd_done", 2 * self.groups)

    def columns(self, tensor, q):
        return tensor[0:self.rows, bass.ds(q * self.group, self.group)]

    def on_vector(self, eng, q):
        rows, step, s = self.rows, self.moments_step, q * MOMENT_STEPS
        for i in range(self.group):
            t = q * self.group + i
            op = eng.bn_stats(self.raw[0:rows, bass.ds(t, 1), :].rearrange("p t c -> p (t c)"), self.x[0:rows, t, :])
        op.then_inc(self.stats_done.sem, 1)
        mean_e, sq_e, mean_o, sq_o = (self.raw[0:rows, bass.ds(q * self.group, self.group), c] for c in (1, 2, 4, 5))
        mean, spread = self.columns(self.mean, q), self.columns(self.spread, q)
        eng.wait_ge(self.stats_done.sem, self.stats_done.at(q + 1))
        eng.tensor_tensor(mean, mean_e, mean_o, ALU.add).then_inc(step.sem, 1)
        eng.tensor_tensor(spread, mean_e, mean_o, ALU.subtract).then_inc(step.sem, 1)
        eng.wait_ge(step.sem, step.at(s + 2))
        eng.tensor_scalar(mean, mean, 0.5, None, ALU.mult).then_inc(step.sem, 1)
        eng.scalar_tensor_tensor(spread, spread, D / 4.0, spread, ALU.mult, ALU.mult).then_inc(step.sem, 1)
        eng.wait_ge(step.sem, step.at(s + 4))
        eng.tensor_tensor(spread, spread, sq_e, ALU.add).then_inc(step.sem, 1)
        eng.wait_ge(step.sem, step.at(s + 5))
        eng.tensor_tensor(spread, spread, sq_o, ALU.add).then_inc(step.sem, 1)

    def on_gpsimd(self, eng):
        for q in range(self.groups):
            rstd = self.columns(self.rstd, q)
            eng.wait_ge(self.moments_step.sem, self.moments_step.at(q * MOMENT_STEPS + MOMENT_STEPS))
            eng.tensor_scalar(rstd, self.columns(self.spread, q), 1.0 / D, self.eps, ALU.mult, ALU.add)\
               .then_inc(self.rstd_done.sem, 1)
            eng.wait_ge(self.rstd_done.sem, self.rstd_done.at(q * 2 + 1))
            eng.tensor_tensor(rstd, rstd, self.minus_half[0:self.rows, 0:self.group], ALU.pow)\
               .then_inc(self.rstd_done.sem, 1)

    def each_group(self, eng, use):
        def ready(q):
            eng.wait_ge(self.rstd_done.sem, self.rstd_done.at(q * 2 + 2))
            use(q)

        self.on_vector(eng, 0)
        if self.groups > 1:
            with eng.Fori(0, self.groups - 1) as q:
                self.on_vector(eng, q + 1)
                ready(q)
        ready(self.groups - 1)


def transpose_phase(nc, signals, name, x, hT, consts, rows, tiles, cols=None, eps=1e-5, moments=None):
    ident = consts["ident"]
    G = min(GROUP, tiles)
    groups = tiles // G
    QG = G // QUAD
    with Phase(nc, signals, name) as ph:
        norm = cols is not None
        nrm = [ph.sb(f"nrm{i}", [P, D]) for i in range(G)]
        psT = [[ph.ps(f"psT{u}{k}", [P, 512]) for k in range(KT)] for u in range(2)]
        stats = Statistics(ph, x, rows, tiles, eps, consts["minus_half"], moments) if norm else None
        ready = ph.sig("normalized", tiles)
        turned = ph.sig("transposed", QG + tiles // QUAD)
        stored = ph.sig("transpose_stored", 2 + tiles // QUAD)

        def each_group(eng, body):
            if groups == 1:
                body(0)
            else:
                with eng.Fori(0, groups) as q:
                    body(q)

        with nc.Block() as block:
            if norm:
                @block.gpsimd
                def _(eng):
                    stats.on_gpsimd(eng)

            @block.vector
            def _(eng):
                def normalize(q):
                    for i in range(G):
                        if i % QUAD == 0:
                            eng.wait_ge(turned.sem, turned.at(q * QG + (i // QUAD + 1)))
                        t = q * G + i
                        if norm:
                            eng.tensor_scalar(nrm[i][0:rows, :], x[0:rows, t, :],
                                              stats.mean[0:rows, bass.ds(t, 1)], stats.rstd[0:rows, bass.ds(t, 1)],
                                              ALU.subtract, ALU.mult).then_inc(ready.sem, 1)
                        else:
                            eng.tensor_copy(nrm[i][0:rows, :], x[0:rows, t, :]).then_inc(ready.sem, 1)

                if norm:
                    stats.each_group(eng, normalize)
                else:
                    each_group(eng, normalize)

            @block.tensor
            def _(eng):
                eng.sem_inc(turned.sem, QG)
                def body(q):
                    for i in range(G):
                        if i % QUAD == 0:
                            eng.wait_ge(stored.sem, stored.at(q * QG + (i // QUAD + 1)))
                        eng.wait_ge(ready.sem, ready.at(q * G + (i + 1)))
                        for k in range(KT):
                            at = (i % QUAD) * rows
                            mm = eng.transpose(psT[i // QUAD][k][:, at:at + rows], nrm[i][0:rows, k * P:(k + 1) * P],
                                               ident[0:rows, 0:rows])
                        if i % QUAD == QUAD - 1:
                            mm.then_inc(turned.sem, 1)

                each_group(eng, body)

            @block.scalar
            def _(eng):
                eng.sem_inc(stored.sem, 2)
                def body(q):
                    for u in range(QG):
                        eng.wait_ge(turned.sem, turned.at(q * QG + (u + 1 + QG)))
                        for k in range(KT):
                            dst = hT[:, k, bass.ds((q * QG + u) * (QUAD * rows), QUAD * rows)]
                            if norm:
                                act = eng.activation(dst, psT[u][k][:, 0:QUAD * rows], ACT.Identity,
                                                     bias=cols[1][:, k:k + 1], scale=cols[0][:, k:k + 1])
                            else:
                                act = eng.activation(dst, psT[u][k][:, 0:QUAD * rows], ACT.Copy)
                        act.then_inc(stored.sem, 1)

                each_group(eng, body)


def output_norm_phase(nc, signals, name, x, consts, gain_row, shift_row, eps):
    with Phase(nc, signals, name) as ph:
        stats = Statistics(ph, x, P, NT, eps, consts["minus_half"])
        gain = ph.sb("gain", [P, D])
        shift = ph.sb("shift", [P, D])
        loaded = ph.sig("weights_loaded", 32)
        centered = ph.sig("centered", NT)
        with nc.Block() as block:
            @block.sync
            def _(eng):
                eng.dma_start(gain[:], gain_row.partition_broadcast(P)).then_inc(loaded.sem, 16)
                eng.dma_start(shift[:], shift_row.partition_broadcast(P)).then_inc(loaded.sem, 16)

            @block.gpsimd
            def _(eng):
                stats.on_gpsimd(eng)

            @block.vector
            def _(eng):
                eng.wait_ge(loaded.sem, loaded.at(32))

                def scale(q):
                    for i in range(GROUP):
                        xt = x[:, q * GROUP + i, :]
                        eng.scalar_tensor_tensor(xt, xt, stats.mean[:, bass.ds(q * GROUP + i, 1)], gain[:],
                                                 ALU.subtract, ALU.mult).then_inc(centered.sem, 1)
                    for i in range(GROUP):
                        xt = x[:, q * GROUP + i, :]
                        eng.wait_ge(centered.sem, centered.at(q * GROUP + (i + 1)))
                        eng.scalar_tensor_tensor(xt, xt, stats.rstd[:, bass.ds(q * GROUP + i, 1)], shift[:],
                                                 ALU.mult, ALU.add)

                stats.each_group(eng, scale)


def context_heads_phase(nc, signals, name, sT, w_k, w_v, b_k, b_v, consts, Kbd, Vbd, rope=None):
    n_k = KT * (2 if rope else 1)
    with Phase(nc, signals, name) as ph:
        wk = ph.sb("wk", [P, KT, D])
        wk2 = ph.sb("wk2", [P, KT, D]) if rope else None
        wv = ph.sb("wv", [P, KT, D])
        bv = ph.sb("bv", [1, D])
        sT2 = ph.sb("sT2", [P, KT, B, 2, SC])
        kT = [ph.sb(f"kT{t}", [P, B, SC]) for t in range(KT)]
        kS = [ph.sb(f"kS{t}", [P, B, SC]) for t in range(KT)] if rope else None
        psK = [ph.ps(f"psK{i}", [P, B * SC]) for i in range(n_k)]
        psV = [ph.ps(f"psV{b}", [P, D]) for b in range(B)]
        loaded = ph.sig("weights_loaded", 16 * (4 if rope else 3))
        doubled = ph.sig("context_doubled", 1)
        cleared = ph.sig("cleared", 1)
        k_ready = ph.sig("keys_in_psum", 1)
        v_ready = ph.sig("values_in_psum", 1)
        kT_ready = ph.sig("keys_biased", KT)
        turned = ph.sig("keys_turned", 2 * KT)
        with nc.Block() as block:
            @block.sync
            def _(eng):
                eng.dma_start(wk[:], w_k[0]).then_inc(loaded.sem, 16)
                if rope:
                    eng.dma_start(wk2[:], w_k[1]).then_inc(loaded.sem, 16)
                eng.dma_start(wv[:], w_v).then_inc(loaded.sem, 16)
                eng.dma_start(bv[:], b_v).then_inc(loaded.sem, 16)

            @block.gpsimd
            def _(eng):
                src = sT[:, :, :].rearrange("p k (b c) -> p (k b) c", c=SC)
                for s in range(2):
                    op = eng.tensor_copy(sT2[:, :, :, s, :].rearrange("p k b c -> p (k b) c"), src)
                op.then_inc(doubled.sem, 1)

            @block.tensor
            def _(eng):
                eng.wait_ge(loaded.sem, loaded.at(loaded.total))
                for t in range(KT):
                    for r in range(2 if rope else 1):
                        for k in range(KT):
                            mm = eng.matmul(psK[r * KT + t][:], (wk2 if r else wk)[:, k, t * P:(t + 1) * P],
                                            sT[:, k, :], start=(k == 0), stop=(k == KT - 1))
                mm.then_inc(k_ready.sem, 1)
                eng.wait_ge(doubled.sem, doubled.at(1))
                for b in range(B):
                    eng.matmul(psV[b][:], consts["ones"][0:1, 0:P], bv[:], start=True, stop=False)
                    for k in range(KT):
                        mm = eng.matmul(psV[b][:], sT2[:, k, b, :, :].rearrange("p s c -> p (s c)"),
                                        wv[:, k, :], start=False, stop=(k == KT - 1))
                mm.then_inc(v_ready.sem, 1)

            @block.scalar
            def _(eng):
                eng.wait_ge(k_ready.sem, k_ready.at(1))
                if not rope:
                    for t in range(KT):
                        eng.activation(kT[t][:].rearrange("p b c -> p (b c)"), psK[t][:], ACT.Identity,
                                       bias=b_k[0][:, t:t + 1], scale=1.0).then_inc(kT_ready.sem, 1)
                eng.wait_ge(v_ready.sem, v_ready.at(1))
                eng.wait_ge(cleared.sem, cleared.at(1))
                for b in range(B):
                    for s in range(2):
                        rows = slice(s * SC, (s + 1) * SC)
                        src = psV[b][rows, :].rearrange("p (j s d) -> p j s d", s=2, d=DK)[:, :, s, :]
                        eng.activation(Vbd[rows, b, :, s * (DK + 1):s * (DK + 1) + DK], src, ACT.Copy)

            @block.vector
            def _(eng):
                eng.memset(Vbd[:], 0.0).then_inc(turned.sem, 1)
                eng.wait_ge(turned.sem, turned.at(1))
                eng.memset(Vbd[0:SC, :, :, DK:DK + 1], 1.0)
                eng.memset(Vbd[SC:P, :, :, PW - 1:PW], 1.0).then_inc(cleared.sem, 1)
                if rope:
                    cos, sin = rope
                    eng.wait_ge(k_ready.sem, k_ready.at(1))
                    for t in range(KT):
                        for b in range(B):
                            cols = slice(b * SC, (b + 1) * SC)
                            eng.scalar_tensor_tensor(kT[t][:, b, :], psK[t][:, cols], b_k[0][:, t:t + 1],
                                                     cos[:, 0:SC], ALU.add, ALU.mult)
                            op = eng.scalar_tensor_tensor(kS[t][:, b, :], psK[KT + t][:, cols],
                                                          b_k[1][:, t:t + 1], sin[:, 0:SC], ALU.add, ALU.mult)
                    op.then_inc(turned.sem, 1)
                    eng.wait_ge(turned.sem, turned.at(2))
                    for t in range(KT):
                        eng.tensor_tensor(kT[t][:], kT[t][:], kS[t][:], ALU.add).then_inc(kT_ready.sem, 1)
                else:
                    eng.sem_inc(turned.sem, 1)
                for t in range(KT):
                    eng.wait_ge(kT_ready.sem, kT_ready.at(t + 1))
                    for b in range(B):
                        op = eng.tensor_tensor(Kbd[:, b, t, :].rearrange("p (h c) -> p h c", c=SC),
                                               kT[t][:, b, :].unsqueeze(1).to_broadcast([P, HT, SC]),
                                               consts["head_rows"][:].unsqueeze(2).to_broadcast([P, HT, SC]),
                                               ALU.mult)
                    op.then_inc(turned.sem, 1)


def cross_attention_phase(nc, signals, name, hT, x, rows, tiles, w_q, b_q, w_o, b_o, Kbd, Vbd, consts,
                          bias=None, rope=None, meanwhile=None):
    chunks = max(1, tiles * rows // CH)
    tpc = tiles // chunks
    cw = tpc * rows
    n_r = 2 if rope else 1
    with Phase(nc, signals, name) as ph:
        wq = [ph.sb(f"wq{r}", [P, KT, D]) for r in range(n_r)]
        wo = ph.sb("wo", [P, KT, D])
        bo = ph.sb("bo", [1, D])
        bq_scaled = ph.sb("bq_scaled", [P, KT])
        table = ph.sb("table", [P, bias[1], H * SC]) if bias else None
        qT = [[ph.sb(f"qT{u}{t}", [P, CH]) for t in range(KT)] for u in range(2)]
        qS = ph.sb("qS", [P, CH]) if rope else None
        sc = [ph.sb(f"sc{u}", [P, H, SC]) for u in range(2)]
        top = [ph.sb(f"top{u}", [P, H]) for u in range(2)]
        pT = [ph.sb(f"pT{u}", [P, H // 2, P]) for u in range(2)]
        rden = [ph.sb(f"rden{u}", [P, H]) for u in range(2)]
        cx = [ph.sb(f"cx{u}", [P, D]) for u in range(2)]
        cT = [ph.sb(f"cT{u}", [P, KT, P]) for u in range(2)]
        psS = ph.ps("psS", [P, H, SC])
        psT = ph.ps("psT", [P, H // 4, P])
        psQ = [ph.ps(f"psQ{i}", [P, CH]) for i in range(n_r)]
        psO = ph.ps("psO", [P, 512])
        psC = ph.ps("psC", [P, KT, P])
        psY = ph.ps("psY", [P, 512])
        n = B * tiles
        n_load = 16 * (n_r + 2 + bool(bias))
        loaded = ph.sig("weights_loaded", n_load)
        scaled = ph.sig("bias_scaled", 1)
        q_psum = ph.sig("query_in_psum", B * chunks * KT)
        q_halves = ph.sig("query_halves", B * chunks * KT if rope else 0)
        q_ready = ph.sig("query_ready", B * chunks * KT)
        s_psum = ph.sig("scores_in_psum", n)
        s_biased = ph.sig("scores_biased", n if bias else 0)
        s_top = ph.sig("scores_top", n)
        s_less = ph.sig("scores_less_top", n)
        p_ready = ph.sig("probs_ready", n)
        p_psum = ph.sig("probs_transposed", 2 * n)
        p_turned = ph.sig("probs_turned", 2 * n)
        c_psum = ph.sig("context_in_psum", n)
        c_inv = ph.sig("context_inverse", n)
        c_ready = ph.sig("context_ready", n)
        ct_psum = ph.sig("context_transposed", n)
        ct_ready = ph.sig("context_turned", n)
        y_psum = ph.sig("output_in_psum", n)
        y_added = ph.sig("output_added", n)

        def each_batch(eng, batch):
            if tiles > 1:
                with eng.Fori(0, B) as b:
                    batch(b)
            else:
                for b in range(B):
                    batch(b)

        def chunk_due(s):
            for c in range(chunks):
                if s == max(0, c * tpc - 2):
                    return c
            return None

        with nc.Block() as block:
            @block.sync
            def _(eng):
                for r in range(n_r):
                    eng.dma_start(wq[r][:], w_q[r]).then_inc(loaded.sem, 16)
                eng.dma_start(wo[:], w_o).then_inc(loaded.sem, 16)
                eng.dma_start(bo[:], b_o).then_inc(loaded.sem, 16)
                if bias:
                    eng.dma_start(table[0:rows], bias[0]).then_inc(loaded.sem, 16)
                if meanwhile:
                    meanwhile(eng)

            @block.tensor
            def _(eng):
                def transpose_probs(b, s, half):
                    u, tile = (s - 1) % 2, b * tiles + (s - 1)
                    if s >= 2 or half:
                        eng.wait_ge(p_turned.sem, p_turned.at(tile * 2 + half))
                    for j in range(H // 4):
                        h = half * (H // 2) + 2 * j
                        mm = eng.transpose(psT[:, j, 0:rows],
                                           sc[u][0:rows, h:h + 2, :].rearrange("p h c -> p (h c)"),
                                           consts["ident"][0:rows, 0:rows])
                    mm.then_inc(p_psum.sem, 1)

                eng.wait_ge(loaded.sem, loaded.at(n_load))
                def batch(b):
                    for s in range(tiles + 4):
                        c = chunk_due(s)
                        if c is not None:
                            for t in range(KT):
                                if c + t > 0:
                                    eng.wait_ge(q_ready.sem, q_ready.at(b * (chunks * KT) + (c * KT + t)))
                                for r in range(n_r):
                                    for k in range(KT):
                                        mm = eng.matmul(psQ[r][:, 0:cw], wq[r][:, k, t * P:(t + 1) * P],
                                                        hT[:, k, bass.ds(b * (tiles * rows) + c * cw, cw)],
                                                        start=(k == 0), stop=(k == KT - 1))
                                mm.then_inc(q_psum.sem, 1)
                        if s < tiles:
                            c = s // tpc
                            eng.wait_ge(q_ready.sem, q_ready.at(b * (chunks * KT) + (c + 1) * KT))
                            if s >= 1:
                                eng.wait_ge(s_less.sem, s_less.at(b * tiles + s))
                            for t in range(KT):
                                mm = eng.matmul(psS[0:rows, t * HT:(t + 1) * HT, :].rearrange("p h c -> p (h c)"),
                                                qT[c % 2][t][:, (s % tpc) * rows:(s % tpc + 1) * rows],
                                                Kbd[:, b, t, :], start=True, stop=True)
                            mm.then_inc(s_psum.sem, 1)
                        if 1 <= s <= tiles:
                            eng.wait_ge(p_ready.sem, p_ready.at(b * tiles + s))
                            transpose_probs(b, s, 0)
                        if 2 <= s <= tiles + 1:
                            u, tile = s % 2, b * tiles + (s - 2)
                            eng.wait_ge(p_turned.sem, p_turned.at(tile * 2 + 2))
                            if s >= 3:
                                eng.wait_ge(c_ready.sem, c_ready.at(tile))
                            for j in range(H // 2):
                                mm = eng.matmul(psO[0:rows, j * PW:(j + 1) * PW], pT[u][:, j, 0:rows],
                                                Vbd[:, b, j, :], start=True, stop=True)
                            mm.then_inc(c_psum.sem, 1)
                        if 3 <= s <= tiles + 2:
                            u, tile = (s - 3) % 2, b * tiles + (s - 3)
                            eng.wait_ge(c_ready.sem, c_ready.at(tile + 1))
                            if s >= 4:
                                eng.wait_ge(ct_ready.sem, ct_ready.at(tile))
                            for k in range(KT):
                                mm = eng.transpose(psC[:, k, 0:rows],
                                                   cx[u][0:rows, k * P:(k + 1) * P],
                                                   consts["ident"][0:rows, 0:rows])
                            mm.then_inc(ct_psum.sem, 1)
                        if 4 <= s:
                            u, tile = s % 2, b * tiles + (s - 4)
                            eng.wait_ge(ct_ready.sem, ct_ready.at(tile + 1))
                            if s >= 5:
                                eng.wait_ge(y_added.sem, y_added.at(tile))
                            eng.matmul(psY[0:rows, 0:D], consts["ones"][0:1, 0:rows], bo[:],
                                       start=True, stop=False)
                            for k in range(KT):
                                mm = eng.matmul(psY[0:rows, 0:D], cT[u][:, k, 0:rows], wo[:, k, :],
                                                start=False, stop=(k == KT - 1))
                            mm.then_inc(y_psum.sem, 1)
                        if 1 <= s <= tiles:
                            transpose_probs(b, s, 1)

                each_batch(eng, batch)

            @block.scalar
            def _(eng):
                def turn_probs(b, s, half):
                    u, tile = (s - 1) % 2, b * tiles + (s - 1)
                    eng.wait_ge(p_psum.sem, p_psum.at(tile * 2 + half + 1))
                    eng.activation(pT[u][:, half * 4:half * 4 + 4, 0:rows], psT[:, :, 0:rows], ACT.Copy)\
                       .then_inc(p_turned.sem, 1)

                eng.wait_ge(loaded.sem, loaded.at(n_load))
                if not rope:
                    eng.mul(bq_scaled[:], b_q[0], SCALE).then_inc(scaled.sem, 1)
                    eng.wait_ge(scaled.sem, scaled.at(1))
                def batch(b):
                    for s in range(tiles + 4):
                        c = chunk_due(s)
                        if c is not None and not rope:
                            for t in range(KT):
                                q = b * (chunks * KT) + (c * KT + t)
                                eng.wait_ge(q_psum.sem, q_psum.at(q + 1))
                                eng.activation(qT[c % 2][t][:, 0:cw], psQ[0][:, 0:cw], ACT.Identity,
                                               bias=bq_scaled[:, t:t + 1], scale=SCALE).then_inc(q_ready.sem, 1)
                        if 1 <= s <= tiles:
                            if s >= 3:
                                eng.wait_ge(c_psum.sem, c_psum.at(b * tiles + (s - 2)))
                            turn_probs(b, s, 0)
                        if s < tiles:
                            u, tile = s % 2, b * tiles + s
                            eng.wait_ge(s_less.sem, s_less.at(tile + 1))
                            eng.activation(sc[u][0:rows], sc[u][0:rows], ACT.Exp).then_inc(p_ready.sem, 1)
                        if 3 <= s <= tiles + 2:
                            u, tile = (s - 3) % 2, b * tiles + (s - 3)
                            eng.wait_ge(ct_psum.sem, ct_psum.at(tile + 1))
                            if s >= 5:
                                eng.wait_ge(y_psum.sem, y_psum.at(tile - 1))
                            eng.activation(cT[u][:, :, 0:rows],
                                           psC[:, :, 0:rows],
                                           ACT.Copy).then_inc(ct_ready.sem, 1)
                        if 1 <= s <= tiles:
                            turn_probs(b, s, 1)

                each_batch(eng, batch)

            @block.vector
            def _(eng):
                eng.wait_ge(loaded.sem, loaded.at(n_load))
                def batch(b):
                    for s in range(tiles + 4):
                        c = chunk_due(s)
                        if c is not None and rope:
                            cos, sin = rope
                            for t in range(KT):
                                q = b * (chunks * KT) + (c * KT + t)
                                eng.wait_ge(q_psum.sem, q_psum.at(q + 1))
                                eng.scalar_tensor_tensor(qT[c % 2][t][:, 0:cw], psQ[0][:, 0:cw], b_q[0][:, t:t + 1],
                                                         cos[:, c * cw:(c + 1) * cw], ALU.add, ALU.mult)
                                eng.scalar_tensor_tensor(qS[:, 0:cw], psQ[1][:, 0:cw], b_q[1][:, t:t + 1],
                                                         sin[:, c * cw:(c + 1) * cw], ALU.add, ALU.mult)\
                                   .then_inc(q_halves.sem, 1)
                                eng.wait_ge(q_halves.sem, q_halves.at(q + 1))
                                eng.tensor_tensor(qT[c % 2][t][:, 0:cw], qT[c % 2][t][:, 0:cw], qS[:, 0:cw],
                                                  ALU.add).then_inc(q_ready.sem, 1)
                                eng.wait_ge(q_ready.sem, q_ready.at(q + 1))
                        if s < tiles:
                            u, tile = s % 2, b * tiles + s
                            eng.wait_ge(s_psum.sem, s_psum.at(tile + 1))
                            if s >= 2:
                                eng.wait_ge(p_psum.sem, p_psum.at((tile - 1) * 2))
                            src = psS
                            if bias:
                                j = min(s, bias[1] - 1)
                                eng.tensor_tensor(sc[u][0:rows], psS[0:rows],
                                                  table[0:rows, j, :].rearrange("p (h c) -> p h c", c=SC),
                                                  ALU.add).then_inc(s_biased.sem, 1)
                                eng.wait_ge(s_biased.sem, s_biased.at(tile + 1))
                                src = sc[u]
                            eng.tensor_reduce(top[u][0:rows], src[0:rows], AX.X, ALU.max).then_inc(s_top.sem, 1)
                            eng.wait_ge(s_top.sem, s_top.at(tile + 1))
                            eng.tensor_tensor(sc[u][0:rows], src[0:rows],
                                              top[u][0:rows].unsqueeze(2).to_broadcast([rows, H, SC]),
                                              ALU.subtract).then_inc(s_less.sem, 1)
                        if 2 <= s <= tiles + 1:
                            u, tile = s % 2, b * tiles + (s - 2)
                            got = psO[0:rows, 0:H * (DK + 1)].rearrange("p (h d) -> p h d", d=DK + 1)
                            eng.wait_ge(c_psum.sem, c_psum.at(tile + 1))
                            eng.reciprocal(rden[u][0:rows], got[:, :, DK]).then_inc(c_inv.sem, 1)
                            eng.wait_ge(c_inv.sem, c_inv.at(tile + 1))
                            if s >= 4:
                                eng.wait_ge(ct_psum.sem, ct_psum.at(tile - 1))
                            eng.tensor_tensor(cx[u][0:rows].rearrange("p (h d) -> p h d", d=DK),
                                              got[:, :, 0:DK],
                                              rden[u][0:rows].unsqueeze(2).to_broadcast([rows, H, DK]),
                                              ALU.mult).then_inc(c_ready.sem, 1)
                        if 4 <= s:
                            tile = b * tiles + (s - 4)
                            xt = x[0:rows, tile, :]
                            eng.wait_ge(y_psum.sem, y_psum.at(tile + 1))
                            eng.tensor_tensor(xt, xt, psY[0:rows, 0:D], ALU.add).then_inc(y_added.sem, 1)

                each_batch(eng, batch)


def self_heads_phase(nc, signals, name, hT, w_q, w_k, w_v, b_q, b_k, b_v, consts, Qd, Kd, Vd, rope=None):
    n_r = 2 if rope else 1
    ITEMS = []
    for half in range(2):
        ITEMS += [("qk", half, t, kind) for t in range(KT) for kind in range(2)]
        ITEMS += [("v", half, j, 0) for j in range(4)]
    n_qk, n_v = 8, 8
    index, seen = [], {"qk": 0, "v": 0}
    for item in ITEMS:
        index.append(seen[item[0]])
        seen[item[0]] += 1
    with Phase(nc, signals, name) as ph:
        w = [[ph.sb(f"w{kind}{r}", [P, KT, D]) for r in range(n_r)] for kind in range(2)]
        wv = ph.sb("wv", [P, KT, D])
        bv = ph.sb("bv", [1, D])
        Vst = ph.sb("Vst", [P, B * H, 3 * DK, TB], BF16)
        bq_scaled = ph.sb("bq_scaled", [P, KT])
        hS = [ph.sb(f"hS{u}", [P, KT, CH]) for u in range(2)]
        y = [ph.sb(f"y{u}", [P, CH]) for u in range(2)]
        y2 = [ph.sb(f"y2{u}", [P, CH]) for u in range(2)] if rope else None
        rest = [ph.sb(f"rest{u}", [P, CH]) for u in range(2)]
        piece = [ph.sb(f"piece{u}", [P, 3, CH], BF16) for u in range(2)]
        vrest = [ph.sb(f"vrest{u}", [P, H, DK]) for u in range(2)]
        psQ = [[ph.ps(f"psQ{u}{r}", [P, CH]) for r in range(n_r)] for u in range(2)]
        psV = [ph.ps(f"psV{u}", [P, 512]) for u in range(2)]
        n_load = 16 * (2 * n_r + 2)
        loaded = ph.sig("weights_loaded", n_load)
        scaled = ph.sig("bias_scaled", 1)
        staged = [ph.sig(f"chunk_staged{u}", 16 * B) for u in range(2)]
        qk_psum = ph.sig("projection_in_psum", n_qk * B)
        qk_read = ph.sig("projection_read", n_qk * B)
        y_ready = ph.sig("projection_ready", n_qk * B if rope else 0)
        high = ph.sig("high_ready", n_qk * B)
        rested = ph.sig("rest_ready", n_qk * B)
        mid = ph.sig("mid_ready", n_qk * B)
        low = ph.sig("low_ready", n_qk * B)
        written = [ph.sig(f"pieces_written{u}", 16 * n_qk * B // 2) for u in range(2)]
        v_written = ph.sig("values_written", 16 * B)
        v_psum = ph.sig("value_in_psum", n_v * B)
        v_high = ph.sig("value_high_ready", n_v * B)
        v_rest = ph.sig("value_rest_ready", n_v * B)
        v_mid = ph.sig("value_mid_ready", n_v * B)
        v_low = ph.sig("value_low_ready", n_v * B)

        def batch_over(eng, b):
            for u in range(2):
                eng.wait_ge(written[u].sem, written[u].at(b * (8 * n_qk) + 8 * n_qk))
            eng.wait_ge(v_low.sem, v_low.at(b * n_v + n_v))

        def vst(b, j, part):
            return Vst[:, bass.ds(b * H, H), part * DK:(part + 1) * DK, j]

        with nc.Block() as block:
            @block.sync
            def _(eng):
                for dst, src in ((w[0], w_q), (w[1], w_k)):
                    for r in range(n_r):
                        eng.dma_start(dst[r][:], src[r]).then_inc(loaded.sem, 16)
                eng.dma_start(wv[:], w_v).then_inc(loaded.sem, 16)
                eng.dma_start(bv[:], b_v).then_inc(loaded.sem, 16)
                with eng.Fori(0, B) as b:
                    for half in range(2):
                        eng.dma_start(hS[half][:], hT[:, :, bass.ds(b * SQ + half * CH, CH)])\
                           .then_inc(staged[half].sem, 16)
                    for n, (what, half, t, kind) in enumerate(ITEMS):
                        if what == "qk":
                            g = b * n_qk + index[n]
                            eng.wait_ge(low.sem, low.at(g + 1))
                            eng.wait_ge(mid.sem, mid.at(g + 1))
                            eng.wait_ge(high.sem, high.at(g + 1))
                            if index[n] == n_qk - 1:
                                eng.wait_ge(v_low.sem, v_low.at(b * n_v + n_v))
                            dst = (Kd if kind else Qd)[:, bass.ds(b * D + t * P, P), half * CH:(half + 1) * CH]
                            eng.dma_start(dst.rearrange("r p c -> p r c"), piece[index[n] % 2][:])\
                               .then_inc(written[index[n] % 2].sem, 16)
                    heads = bass.ds(b * H, H)
                    eng.dma_start(Vd[heads].rearrange("g p c j -> p g (c j)"),
                                  Vst[:, heads].rearrange("p g c j -> p g (c j)")).then_inc(v_written.sem, 16)
                for u in range(2):
                    eng.wait_ge(written[u].sem, written[u].at(B * 8 * n_qk))
                eng.wait_ge(v_written.sem, v_written.at(16 * B))

            @block.tensor
            def _(eng):
                eng.wait_ge(loaded.sem, loaded.at(n_load))
                with eng.Fori(0, B) as b:
                    for n, (what, half, t, kind) in enumerate(ITEMS):
                        i = index[n]
                        if n % 8 == 0:
                            eng.wait_ge(staged[half].sem, staged[half].at(b * 16 + 16))
                        if what == "qk":
                            if i >= 2:
                                eng.wait_ge(qk_read.sem, qk_read.at(b * n_qk + (i - 1)))
                            for r in range(n_r):
                                for k in range(KT):
                                    mm = eng.matmul(psQ[i % 2][r][:], w[kind][r][:, k, t * P:(t + 1) * P],
                                                    hS[half][:, k, :], start=(k == 0), stop=(k == KT - 1))
                            mm.then_inc(qk_psum.sem, 1)
                        else:
                            if i >= 2:
                                eng.wait_ge(v_rest.sem, v_rest.at(b * n_v + (i - 1)))
                            eng.matmul(psV[i % 2][:, 0:D], consts["ones"][0:1, 0:P], bv[:], start=True, stop=False)
                            for k in range(KT):
                                mm = eng.matmul(psV[i % 2][:, 0:D], hS[half][:, k, t * P:(t + 1) * P], wv[:, k, :],
                                                start=False, stop=(k == KT - 1))
                            mm.then_inc(v_psum.sem, 1)
                    batch_over(eng, b)

            @block.scalar
            def _(eng):
                if not rope:
                    eng.mul(bq_scaled[:], b_q[0], SCALE).then_inc(scaled.sem, 1)
                    eng.wait_ge(scaled.sem, scaled.at(1))
                with eng.Fori(0, B) as b:
                    for n in range(len(ITEMS) + 1):
                        if n < len(ITEMS):
                            what, half, t, kind = ITEMS[n]
                            i = index[n]
                            if what == "qk" and not rope:
                                eng.wait_ge(qk_psum.sem, qk_psum.at(b * n_qk + (i + 1)))
                                if i >= 2:
                                    eng.wait_ge(rested.sem, rested.at(b * n_qk + (i - 1)))
                                bias = (b_k[0] if kind else bq_scaled)[:, t:t + 1]
                                eng.activation(y[i % 2][:], psQ[i % 2][0][:], ACT.Identity, bias=bias,
                                               scale=1.0 if kind else SCALE).then_inc(qk_read.sem, 1)
                            if what == "v":
                                eng.wait_ge(v_psum.sem, v_psum.at(b * n_v + (i + 1)))
                                src = psV[i % 2][:, 0:D].rearrange("p (h d) -> p h d", d=DK)
                                eng.activation(vst(b, i, 0), src, ACT.Copy).then_inc(v_high.sem, 1)
                        if n >= 1:
                            what, half, t, kind = ITEMS[n - 1]
                            i = index[n - 1]
                            if what == "qk":
                                eng.wait_ge(rested.sem, rested.at(b * n_qk + (i + 1)))
                                if i >= 2:
                                    eng.wait_ge(written[i % 2].sem, written[i % 2].at(b * (8 * n_qk) + 16 * (i // 2)))
                                eng.activation(piece[i % 2][:, 1, :], rest[i % 2][:], ACT.Copy).then_inc(mid.sem, 1)
                            else:
                                eng.wait_ge(v_rest.sem, v_rest.at(b * n_v + (i + 1)))
                                eng.activation(vst(b, i, 1), vrest[i % 2][:], ACT.Copy).then_inc(v_mid.sem, 1)
                    batch_over(eng, b)

            @block.vector
            def _(eng):
                with eng.Fori(0, B) as b:
                    for n, (what, half, t, kind) in enumerate(ITEMS):
                        i = index[n]
                        u = i % 2
                        if what == "qk":
                            g = b * n_qk + i
                            if rope:
                                cos, sin = rope[kind]
                                bias = b_k if kind else b_q
                                cs = slice(half * CH, (half + 1) * CH)
                                eng.wait_ge(qk_psum.sem, qk_psum.at(g + 1))
                                if i >= 2:
                                    eng.wait_ge(y_ready.sem, y_ready.at(b * n_qk + (i - 1)))
                                eng.scalar_tensor_tensor(y[u][:], psQ[u][0][:], bias[0][:, t:t + 1], cos[:, cs],
                                                         ALU.add, ALU.mult)
                                eng.scalar_tensor_tensor(y2[u][:], psQ[u][1][:], bias[1][:, t:t + 1], sin[:, cs],
                                                         ALU.add, ALU.mult).then_inc(qk_read.sem, 1)
                                eng.wait_ge(y_ready.sem, y_ready.at(g + 1))
                            else:
                                eng.wait_ge(qk_read.sem, qk_read.at(g + 1))
                            if i >= 2:
                                eng.wait_ge(written[i % 2].sem, written[i % 2].at(b * (8 * n_qk) + 16 * (i // 2)))
                                eng.wait_ge(low.sem, low.at(b * n_qk + (i - 1)))
                            eng.tensor_copy(piece[u][:, 0, :], y[u][:]).then_inc(high.sem, 1)
                            eng.wait_ge(high.sem, high.at(g + 1))
                            eng.tensor_tensor(rest[u][:], y[u][:], piece[u][:, 0, :], ALU.subtract)\
                               .then_inc(rested.sem, 1)
                        else:
                            eng.wait_ge(v_high.sem, v_high.at(b * n_v + (i + 1)))
                            if i >= 2:
                                eng.wait_ge(v_low.sem, v_low.at(b * n_v + (i - 1)))
                            eng.tensor_tensor(vrest[u][:], psV[u][:, 0:D].rearrange("p (h d) -> p h d", d=DK),
                                              vst(b, i, 0), ALU.subtract).then_inc(v_rest.sem, 1)
                    batch_over(eng, b)

            @block.gpsimd
            def _(eng):
                with eng.Fori(0, B) as b:
                    for n in range(len(ITEMS) + 1):
                        if n < len(ITEMS) and ITEMS[n][0] == "qk" and rope:
                            i = index[n]
                            eng.wait_ge(qk_read.sem, qk_read.at(b * n_qk + (i + 1)))
                            eng.tensor_tensor(y[i % 2][:], y[i % 2][:], y2[i % 2][:], ALU.add).then_inc(y_ready.sem, 1)
                        if n >= 1:
                            i = index[n - 1]
                            u = i % 2
                            if ITEMS[n - 1][0] == "qk":
                                eng.wait_ge(mid.sem, mid.at(b * n_qk + (i + 1)))
                                if i >= 2:
                                    eng.wait_ge(written[i % 2].sem, written[i % 2].at(b * (8 * n_qk) + 16 * (i // 2)))
                                eng.tensor_tensor(piece[u][:, 2, :], rest[u][:], piece[u][:, 1, :], ALU.subtract)\
                                   .then_inc(low.sem, 1)
                            else:
                                eng.wait_ge(v_mid.sem, v_mid.at(b * n_v + (i + 1)))
                                eng.tensor_tensor(vst(b, i, 2), vrest[u][:], vst(b, i, 1), ALU.subtract)\
                                   .then_inc(v_low.sem, 1)
                    batch_over(eng, b)


def near_blocks_phase(nc, signals, name, q_rel, k_rel, far, mask_q, mask_k, q_near, k_near):
    HN = 17
    with Phase(nc, signals, name) as ph:
        rel = ph.sb("rel", [P, HN, 2 * P])
        rest = ph.sb("rest", [P, HN, 2 * P])
        far_sb = ph.sb("far", [P, HN])
        mask = ph.sb("mask", [P, 2 * P])
        loaded = ph.sig("weights_loaded", 16 * 5)
        step = ph.sig("near_step", 10)
        with nc.Block() as block:
            @block.sync
            def _(eng):
                eng.dma_start(far_sb[:], far.partition_broadcast(P)).then_inc(loaded.sem, 16)
                eng.dma_start(rel[:], q_rel).then_inc(loaded.sem, 16)
                eng.dma_start(mask[:], mask_q).then_inc(loaded.sem, 16)
                eng.wait_ge(step.sem, step.at(3))
                eng.dma_start(rel[:], k_rel).then_inc(loaded.sem, 16)
                eng.dma_start(mask[:], mask_k).then_inc(loaded.sem, 16)

            @block.vector
            def _(eng):
                done = 0
                far_b = far_sb[:].unsqueeze(2).to_broadcast([P, HN, 2 * P])
                mask_b = mask[:].unsqueeze(1).to_broadcast([P, HN, 2 * P])
                for side in range(2):
                    eng.wait_ge(loaded.sem, loaded.at(48 if side == 0 else 80))
                    eng.tensor_tensor(rel[:], rel[:], far_b, ALU.subtract).then_inc(step.sem, 1)
                    eng.wait_ge(step.sem, step.at(done + 1))
                    eng.tensor_tensor(rel[:], rel[:], mask_b, ALU.add).then_inc(step.sem, 1)
                    eng.wait_ge(step.sem, step.at(done + 2))
                    eng.tensor_copy((k_near[0] if side else q_near)[:], rel[:]).then_inc(step.sem, 1)
                    eng.wait_ge(step.sem, step.at(done + 3))
                    done += 3
                for piece in range(2):
                    src = rel if piece == 0 else rest
                    eng.tensor_tensor(rest[:], src[:], k_near[piece][:], ALU.subtract).then_inc(step.sem, 1)
                    eng.wait_ge(step.sem, step.at(done + 1))
                    eng.tensor_copy(k_near[piece + 1][:], rest[:]).then_inc(step.sem, 1)
                    eng.wait_ge(step.sem, step.at(done + 2))
                    done += 2


def self_attention_phase(nc, signals, name, Qd, Kd, Vd, Od, Dd, consts, causal, near=None):
    KB = SQ // P
    LOAD_AHEAD = 2
    RING = 4

    def max_units(qt):
        end = (qt + 1) * P if causal else SQ
        return [("A", qt, hf, min(CH, end - hf * CH)) for hf in range(2) if end > hf * CH]

    units = [m for qt in range(KB) for m in max_units(qt)]
    ON_VECTOR = (1, 3, 6)
    ON_POOL = tuple(kt for kt in range(KB) if kt not in ON_VECTOR)
    steps = (3, 2, 3, 2, 3, 3) if not causal else (2, 2, 2, 2, 2, 2)
    plan = [[] for _ in range(KB)]
    queue = list(units)
    for s in range(6):
        plan[s] += queue[:steps[s]]
        queue = queue[steps[s]:]
    assert not queue
    plan[6] = [("M", 0), ("M", 1)]
    flat = [m for s in plan for m in s]
    NU = len(flat)
    assert NU % 2 == 0
    nA = len(units)

    def q_from(kt):
        return kt * P if causal else 0

    def banks(lo, hi):
        return [(max(lo, c * CH), min(hi, (c + 1) * CH)) for c in range(2) if min(hi, (c + 1) * CH) > max(lo, c * CH)]

    with Phase(nc, signals, name) as ph:
        Qs = [ph.sb(f"Qs{r}", [KS + 1, SQ], BF16) for r in range(RING)]
        Ks = [ph.sb(f"Ks{r}", [KS + 1, SQ], BF16) for r in range(RING)]
        Pf = [ph.sb(f"Pf{r}", [P, SQ]) for r in range(4)]
        Pl = [ph.sb(f"Pl{r}", [P, SQ], F16) for r in range(4)]
        Vs = [ph.sb(f"Vs{r}", [P, VW, TB], BF16) for r in range(RING)]
        oT = [ph.sb(f"oT{u}", [VW, SQ]) for u in range(2)]
        mxp = ph.sb("mxp", [P, KB, 2])
        mx = ph.sb("mx", [P, KB], BF16)
        psA = [ph.ps(f"psA{u}", [P, CH]) for u in range(2)]
        psB = [ph.ps(f"psB{u}", [P, SQ]) for u in range(2)]
        psO = ph.ps("psO", [P, SQ])
        HEADS = B * H
        padded = ph.sig("heads_padded", 48)
        cleared = ph.sig("cleared", 1)
        prep = ph.sig("prepared", 3)
        q_loaded = [ph.sig(f"head_loaded{r}", 16 * 13 * ((HEADS + LOAD_AHEAD - r + RING - 1) // RING)) for r in range(RING)]
        a_psum = ph.sig("unit_in_psum", nA + 2 + HEADS * NU)
        a_read = ph.sig("unit_read", 2 + nA + 2 + HEADS * NU)
        maxed = ph.sig("maxima_ready", HEADS + 1)
        b_psum = ph.sig("scores_in_psum", LOAD_AHEAD * KB + HEADS * KB)
        p_ready = ph.sig("probs_ready", 2 + HEADS * KB)
        l_vec = ph.sig("low_probs_vector", 1 + HEADS * len(ON_VECTOR))
        l_pool = ph.sig("low_probs_pool", 1 + HEADS * len(ON_POOL))
        o_read = ph.sig("context_read", 1 + HEADS + 1)
        o_written = [ph.sig(f"context_written{u}", 16 * u + 64 * (HEADS // 2 + 1)) for u in range(2)]
        pv_done = ph.sig("key_tile_used", 2 + 2 + HEADS * KB)

        def hi(t, lo, hi_):
            return Pf[t][:].bitcast(BF16).rearrange("p (q two) -> p q two", two=2)[:, lo:hi_, 1]

        def each_head(eng, body):
            with eng.Fori(0, B) as b:
                with eng.Fori(0, H // RING) as quarter:
                    hq = quarter * RING
                    for r in range(RING):
                        body(b * H + hq + r, hq + r, r)

        with nc.Block() as block:
            @block.sync
            def _(eng):
                def load(g, r):
                    for dst, src, parts in ((Qs, Qd, Q_PART), (Ks, Kd, K_PART)):
                        for n, part in enumerate(parts):
                            eng.dma_start(dst[r][n * DK:(n + 1) * DK, :], src[part, bass.ds(g * DK, DK), :])\
                               .then_inc(q_loaded[r].sem, 16)
                    eng.dma_start(Vs[r][:, 0:3 * DK, :], Vd[bass.ds(g, 1)].rearrange("g p c j -> (g p) c j"))\
                       .then_inc(q_loaded[r].sem, 16)

                def write_context(g, r):
                    for part in range(3):
                        eng.dma_start(Od[part, bass.ds(g * DK, DK), :], oT[r % 2][part * DK:(part + 1) * DK, :])\
                           .then_inc(o_written[r % 2].sem, 16)
                    eng.dma_start(Dd[bass.ds(g, 1), :], oT[r % 2][3 * DK:VW, :]).then_inc(o_written[r % 2].sem, 16)

                for dram in (Qd, Kd):
                    eng.dma_start(dram[:, B * D:B * D + LOAD_AHEAD * DK, :], dram[:, 0:LOAD_AHEAD * DK, :])\
                       .then_inc(padded.sem, 16)
                eng.dma_start(Vd[B * H:B * H + LOAD_AHEAD], Vd[0:LOAD_AHEAD]).then_inc(padded.sem, 16)
                for g in range(LOAD_AHEAD):
                    load(g, g)
                eng.wait_ge(padded.sem, padded.at(48))
                eng.wait_ge(cleared.sem, cleared.at(1))

                def body(g, h, r):
                    eng.wait_ge(o_read.sem, o_read.at(g + 1))
                    eng.wait_ge(b_psum.sem, b_psum.at(g * KB + (KB + 3)))
                    load(g + LOAD_AHEAD, (r + LOAD_AHEAD) % RING)
                    write_context(g, r)

                each_head(eng, body)
                for g in range(HEADS, HEADS + 2):
                    eng.wait_ge(o_read.sem, o_read.at(g + 1))
                    write_context(g, g % RING)
                for u in range(2):
                    eng.wait_ge(o_written[u].sem, o_written[u].at(o_written[u].total))
                for r in range(RING):
                    eng.wait_ge(q_loaded[r].sem, q_loaded[r].at(q_loaded[r].total))

            @block.tensor
            def _(eng):
                def unit(m, n, count, r_next, h_next):
                    bank = psA[n % 2]
                    eng.wait_ge(a_read.sem, a_read.at(count + 1))
                    if m[0] == "A":
                        _, qt, hf, width = m
                        add = []
                        if near:
                            q_near, _, wide, per_head = near
                            for blk in ((qt - 1, qt) if wide else (qt,)):
                                if blk >= 0 and hf * CH <= blk * P < hf * CH + width:
                                    add.append(blk)
                        mm = eng.matmul(bank[:, 0:width], Qs[r_next][0:KS, qt * P:(qt + 1) * P],
                                        Ks[r_next][0:KS, hf * CH:hf * CH + width], start=True, stop=not add)
                        for blk in add:
                            at = (blk - qt + 1) * P if wide else 0
                            src = q_near[:, bass.ds(h_next, 1), at:at + P].rearrange("p h c -> p (h c)") \
                                if per_head else q_near[:, at:at + P]
                            mm = eng.matmul(bank[:, blk * P - hf * CH:blk * P - hf * CH + P], consts["identb"][:],
                                            src, start=False, stop=(blk == add[-1]))
                    else:
                        for j in range(4):
                            q = m[1] * 4 + j
                            mm = eng.matmul(bank[0:1, j * P:(j + 1) * P], mx[:, q:q + 1], consts["identb"][:],
                                            start=True, stop=True)
                    mm.then_inc(a_psum.sem, 1)

                def values(g, r, kt, part):
                    v = (kt - 2) % KB
                    if part:
                        l_ready, tiles = (l_vec, ON_VECTOR) if v in ON_VECTOR else (l_pool, ON_POOL)
                        before = (0 if kt >= 2 else -len(tiles)) + tiles.index(v)
                        eng.wait_ge(l_ready.sem, l_ready.at(g * len(tiles) + (before + 2)))
                    elif kt == 2:
                        eng.wait_ge(o_read.sem, o_read.at(g + 2))
                    lhs = Vs[r if kt >= 2 else (r - 1) % RING][:, :, v]
                    for lo, up in banks(q_from(v), SQ):
                        src = Pl[v % 4][:, lo:up] if part else hi(v % 4, lo, up)
                        final = KB - 1 if (not causal or lo >= CH) else CH // P - 1
                        mm = eng.matmul(psO[0:VW, lo:up], lhs, src, start=(v == 0 and part == 0),
                                        stop=(v == final and part == 1))
                    if part:
                        mm.then_inc(pv_done.sem, 1)

                eng.sem_inc(b_psum.sem, LOAD_AHEAD * KB)
                eng.sem_inc(pv_done.sem, 2)
                eng.wait_ge(prep.sem, prep.at(3))
                eng.wait_ge(cleared.sem, cleared.at(1))
                for c in range(2):
                    eng.matmul(psO[0:VW, c * CH:(c + 1) * CH], Vs[RING - 1][:, :, KB - 1],
                               hi(KB // 2 - 1, c * CH, (c + 1) * CH), start=True, stop=(causal and c == 0))
                eng.wait_ge(q_loaded[0].sem, q_loaded[0].at(16 * 13))
                for n, m in enumerate(units):
                    unit(m, n, n, 0, 0)
                eng.wait_ge(maxed.sem, maxed.at(1))
                for n in range(2):
                    unit(("M", n), nA + n, nA + n, 0, 0)

                def body(g, h, r):
                    nxt = (r + 1) % RING
                    it = (g - r) if r < RING - 1 else (g + 1)
                    eng.wait_ge(q_loaded[nxt].sem,
                                q_loaded[nxt].at(it * (16 * 13 // RING) + 16 * 13))
                    n = 0
                    for kt in range(KB):
                        if kt == 0:
                            eng.wait_ge(a_read.sem, a_read.at(g * NU + (nA + 2 + 2)))
                        eng.wait_ge(p_ready.sem, p_ready.at(g * KB + (kt + 1)))
                        k_near, wide, per_head = (near[1], near[2], near[3]) if near else ([], False, False)
                        for lo, up in banks(q_from(kt), SQ):
                            near_end = (kt + 2) * P if wide else (kt + 1) * P
                            adds = banks(max(lo, kt * P), min(up, near_end)) if k_near else []
                            mm = eng.matmul(psB[kt % 2][:, lo:up], Ks[r][:, kt * P:(kt + 1) * P], Qs[r][:, lo:up],
                                            start=True, stop=not adds)
                            for lo2, up2 in adds:
                                for piece in k_near:
                                    at = lo2 - kt * P
                                    src = piece[:, bass.ds(h, 1), at:at + up2 - lo2].rearrange("p h c -> p (h c)") \
                                        if per_head else piece[:, at:at + up2 - lo2]
                                    mm = eng.matmul(psB[kt % 2][:, lo2:up2], consts["identb"][:], src,
                                                    start=False, stop=(piece is k_near[-1]))
                        mm.then_inc(b_psum.sem, 1)
                        first, then = (plan[kt][0:2], plan[kt][2:]) if kt < 6 else ([], [])
                        for todo, part in ((first, 0), (then, 1)):
                            for m in todo:
                                unit(m, nA + 2 + n, g * NU + (nA + 2 + n), nxt, h + 1)
                                n += 1
                            values(g, r, kt, part)
                        if kt == 6:
                            eng.wait_ge(maxed.sem, maxed.at(g + 2))
                            for m in plan[kt]:
                                unit(m, nA + 2 + n, g * NU + (nA + 2 + n), nxt, h + 1)
                                n += 1

                each_head(eng, body)
                for kt in range(2):
                    eng.wait_ge(p_ready.sem, p_ready.at(HEADS * KB + (kt + 1)))
                    for part in range(2):
                        values(HEADS, 0, kt, part)

            @block.scalar
            def _(eng):
                eng.sem_inc(p_ready.sem, 2)
                eng.sem_inc(o_written[1].sem, 16)
                eng.sem_inc(o_read.sem, 1)
                eng.wait_ge(cleared.sem, cleared.at(1))

                def copy_context(g, r):
                    eng.wait_ge(pv_done.sem, pv_done.at(g * KB + 4))
                    u = (r + 1) % 2
                    eng.wait_ge(o_written[u].sem, o_written[u].at(g * 32 + (32 if r % 2 else 16)))
                    eng.activation(oT[u][:], psO[0:VW, :], ACT.Copy).then_inc(o_read.sem, 1)

                def shift_row(count, half, r_next):
                    eng.wait_ge(a_psum.sem, a_psum.at(count + 1))
                    eng.activation(Qs[r_next][KS:KS + 1, half * CH:(half + 1) * CH], psA[half][0:1, :], ACT.Copy)\
                       .then_inc(a_read.sem, 1)

                for half in range(2):
                    shift_row(nA + half, half, 0)

                def body(g, h, r):
                    for kt in range(KB):
                        if kt == 2:
                            copy_context(g, r)
                        eng.wait_ge(b_psum.sem, b_psum.at(g * KB + (kt + 1 + LOAD_AHEAD * KB)))
                        eng.wait_ge(pv_done.sem, pv_done.at(g * KB + (kt + 1)))
                        lo = q_from(kt)
                        eng.activation(Pf[kt % 4][:, lo:SQ], psB[kt % 2][:, lo:SQ], ACT.Exp).then_inc(p_ready.sem, 1)
                        if kt == 6:
                            for half in range(2):
                                shift_row(g * NU + (nA + 2 + nA + half), half, (r + 1) % RING)

                each_head(eng, body)
                copy_context(HEADS, 0)

            def rests(eng, g, kt, done):
                eng.wait_ge(p_ready.sem, p_ready.at(g * KB + (kt + 3)))
                eng.wait_ge(pv_done.sem, pv_done.at(g * KB + (kt + 1)))
                lo = q_from(kt)
                eng.tensor_tensor(Pl[kt % 4][:, lo:SQ], Pf[kt % 4][:, lo:SQ], hi(kt % 4, lo, SQ),
                                  ALU.subtract).then_inc(done.sem, 1)

            @block.gpsimd
            def _(eng):
                for t in (2, 3):
                    eng.memset(Pf[t][:], 1.0)
                    eng.memset(Pl[t][:], 1.0)
                for u in range(2):
                    eng.memset(oT[u][:], 1.0)
                for r in range(RING - 1):
                    eng.memset(Vs[r][:, 3 * DK:VW, :], 1.0)
                eng.memset(Vs[RING - 1][:], 1.0).then_inc(cleared.sem, 1)
                eng.sem_inc(l_pool.sem, 1)

                def body(g, h, r):
                    for kt in ON_POOL:
                        rests(eng, g, kt, l_pool)

                each_head(eng, body)

            @block.vector
            def _(eng):
                for r in range(RING):
                    eng.memset(Ks[r][KS:KS + 1, :], 1.0)
                eng.memset(mxp[:], NEG).then_inc(prep.sem, 1)
                eng.wait_ge(prep.sem, prep.at(1))
                eng.sem_inc(a_read.sem, 2)
                eng.sem_inc(prep.sem, 2)
                eng.sem_inc(l_vec.sem, 1)

                def unit(m, n, count):
                    _, qt, hf, width = m
                    eng.wait_ge(a_psum.sem, a_psum.at(count + 1))
                    eng.tensor_reduce(mxp[:, qt, hf:hf + 1], psA[n % 2][:, 0:width], AX.X, ALU.max)\
                       .then_inc(a_read.sem, 1)

                def maxima(count, g_next):
                    eng.wait_ge(a_read.sem, a_read.at(count))
                    eng.tensor_reduce(mx[:], mxp[:], AX.X, ALU.max, negate=True).then_inc(maxed.sem, 1)
                    eng.wait_ge(maxed.sem, maxed.at(g_next + 1))

                for n, m in enumerate(units):
                    unit(m, n, n)
                maxima(nA + 2, 0)

                def body(g, h, r):
                    n = 0
                    for kt in range(KB):
                        if kt == 6:
                            maxima(g * NU + (nA + 2 + nA + 2), g + 1)
                        else:
                            for m in plan[kt]:
                                unit(m, nA + 2 + n, g * NU + (nA + 2 + n))
                                n += 1
                        if kt in ON_VECTOR:
                            rests(eng, g, kt, l_vec)

                each_head(eng, body)


def output_phase(nc, signals, name, Od, Dd, x, w_o, b_o, consts):
    chunks = NT * P // CH
    TC = CH // P
    ROWS = H * DK
    with Phase(nc, signals, name) as ph:
        wo = ph.sb("wo", [P, KT, D])
        bo = ph.sb("bo", [P, D])
        den = ph.sb("den", [B * H, SQ])
        parts = [ph.sb(f"parts{u}", [P, 3, CH]) for u in range(4)]
        cT = [ph.sb(f"cT{u}", [P, CH]) for u in range(4)]
        psY = [ph.ps(f"psY{u}", [P, 512]) for u in range(4)]
        psR = [ph.ps(f"psR{u}", [P, CH]) for u in range(4)]
        loaded = ph.sig("weights_loaded", 32)
        den_loaded = ph.sig("denominators_loaded", 16)
        r_psum = ph.sig("inverse_spread", chunks * KT)
        n = chunks * KT
        parts_loaded = [ph.sig(f"context_loaded{u}", 16 * n // 4) for u in range(4)]
        added = ph.sig("pieces_added", n)
        inverse = ph.sig("denominators_inverse", 1)
        summed = ph.sig("pieces_summed", n)
        c_ready = ph.sig("context_ready", n)
        x_biased = ph.sig("bias_added", NT)
        y_psum = ph.sig("output_in_psum", NT)
        y_added = ph.sig("output_added", NT)

        with nc.Block() as block:
            @block.sync
            def _(eng):
                eng.dma_start(den[:], Dd[2:2 + B * H, :]).then_inc(den_loaded.sem, 16)
                eng.dma_start(wo[:], w_o).then_inc(loaded.sem, 16)
                eng.dma_start(bo[:], b_o.partition_broadcast(P)).then_inc(loaded.sem, 16)
                for i in range(n):
                    c, k = i // KT, i % KT
                    row = 2 * DK + (c // 2) * ROWS + k * P
                    if i >= 4:
                        eng.wait_ge(c_ready.sem, c_ready.at(i - 3))
                    eng.dma_start(parts[i % 4][:], Od[:, row:row + P, (c % 2) * CH:(c % 2 + 1) * CH]
                                  .rearrange("r p c -> p r c")).then_inc(parts_loaded[i % 4].sem, 16)

            @block.gpsimd
            def _(eng):
                eng.wait_ge(loaded.sem, loaded.at(32))
                for i in range(n):
                    eng.wait_ge(parts_loaded[i % 4].sem, parts_loaded[i % 4].at(16 * (i // 4) + 16))
                    eng.tensor_tensor(parts[i % 4][:, 1, :], parts[i % 4][:, 1, :], parts[i % 4][:, 2, :], ALU.add)\
                       .then_inc(added.sem, 1)
                    for t in range(i * 2, i * 2 + 2):
                        eng.tensor_tensor(x[:, t, :], x[:, t, :], bo[:], ALU.add).then_inc(x_biased.sem, 1)

            @block.tensor
            def _(eng):
                def spread_inverse(i):
                    c, k = i // KT, i % KT
                    if i >= 4:
                        eng.wait_ge(c_ready.sem, c_ready.at(i - 3))
                    eng.matmul(psR[i % 4][:], consts["spread"][:, (c // 2) * KT + k, :],
                               den[:, (c % 2) * CH:(c % 2 + 1) * CH], start=True, stop=True).then_inc(r_psum.sem, 1)

                eng.wait_ge(inverse.sem, inverse.at(1))
                for i in range(4):
                    spread_inverse(i)
                eng.wait_ge(loaded.sem, loaded.at(32))
                for c in range(chunks):
                    for j in range(TC):
                        t = c * TC + j
                        if j >= KT and c * KT + 4 + j - KT < n:
                            spread_inverse(c * KT + 4 + j - KT)
                        if t >= 4:
                            eng.wait_ge(y_added.sem, y_added.at(t - 3))
                        for k in range(KT):
                            i = c * KT + k
                            eng.wait_ge(c_ready.sem, c_ready.at(i + 1))
                            mm = eng.matmul(psY[t % 4][:, 0:D], cT[i % 4][:, j * P:(j + 1) * P], wo[:, k, :],
                                            start=(k == 0), stop=(k == KT - 1))
                        mm.then_inc(y_psum.sem, 1)

            @block.vector
            def _(eng):
                eng.wait_ge(den_loaded.sem, den_loaded.at(16))
                eng.reciprocal(den[:], den[:]).then_inc(inverse.sem, 1)
                for c in range(chunks + 1):
                    for k in range(KT):
                        i = c * KT + k
                        if c < chunks:
                            src = parts[i % 4]
                            eng.wait_ge(parts_loaded[i % 4].sem, parts_loaded[i % 4].at(16 * (i // 4) + 16))
                            eng.wait_ge(added.sem, added.at(i + 1))
                            eng.tensor_tensor(src[:, 0, :], src[:, 0, :], src[:, 1, :], ALU.add)\
                               .then_inc(summed.sem, 1)
                            eng.wait_ge(summed.sem, summed.at(i + 1))
                            eng.wait_ge(r_psum.sem, r_psum.at(i + 1))
                            if i >= 4:
                                eng.wait_ge(y_psum.sem, y_psum.at((c - 1) * TC))
                            eng.tensor_tensor(cT[i % 4][:], src[:, 0, :], psR[i % 4][:], ALU.mult)\
                               .then_inc(c_ready.sem, 1)
                        if c >= 1:
                            for t in range((c - 1) * TC + 2 * k, (c - 1) * TC + 2 * k + 2):
                                eng.wait_ge(y_psum.sem, y_psum.at(t + 1))
                                eng.wait_ge(x_biased.sem, x_biased.at(t + 1))
                                eng.tensor_tensor(x[:, t, :], x[:, t, :], psY[t % 4][:, 0:D], ALU.add)\
                                   .then_inc(y_added.sem, 1)


def router_phase(nc, signals, name, hT, gates, slots, block_expert, w_r, b_r, consts):
    chunks = NT * P // CH
    TIMES = NT * P // BS
    SCAN = 5
    assert 1 << SCAN == NT
    with Phase(nc, signals, name) as ph:
        wr = ph.sb("wr", [P, KT, E])
        br = ph.sb("br", [E, 1])
        lT = [ph.sb(f"lT{u}", [E, CH]) for u in range(2)]
        lg = ph.sb("logits", [P, NT, E])
        rank = ph.sb("rank", [P, E])
        one = [ph.sb(f"onehot{i}", [P, NT, E]) for i in range(2)]
        wt = ph.sb("weighted", [P, NT, E])
        m = [ph.sb(f"m{i}", [P, NT]) for i in range(5)]
        before = ph.sb("before", [P, P])
        every = ph.sb("every", [P, P])
        sizes = ph.sb("sizes", [P, E, TIMES])
        behind = ph.sb("behind", [P, E, E])
        number = ph.sb("number", [P, NB, E])
        chosen = ph.sb("chosen", [P, NT, E])
        seen = [ph.sb(f"seen{i}", [P, NT, E]) for i in range(2)]
        place = ph.sb("place", [P, NT, E])
        size_over = ph.sb("size_over", [P, E, TIMES])
        blocks_of = ph.sb("blocks_of", [P, E])
        earlier = ph.sb("earlier", [P, E, E])
        first = ph.sb("first", [P, E])
        last = ph.sb("last", [P, E])
        past = ph.sb("past", [P, NB, E])
        owner = ph.sb("owner", [P, NB])
        dest = ph.sb("dest", [P, 2, NT])
        psN = ph.ps("psN", [P, NT * E])
        psA = ph.ps("psA", [P, NT * E])
        psL = [ph.ps(f"psL{u}", [P, CH]) for u in range(2)]
        psT = [ph.ps(f"psT{u}", [P, 4, E]) for u in range(2)]
        n_load = 16 * 8
        loaded = ph.sig("weights_loaded", n_load)
        l_psum = ph.sig("logits_in_psum", chunks)
        l_ready = ph.sig("logits_biased", chunks)
        t_psum = ph.sig("logits_transposed", chunks)
        t_read = ph.sig("logits_read", chunks)
        step = ph.sig("gate_step", 14 + 2 * SCAN + 19)
        is_chosen = ph.sig("experts_chosen", 1)
        counted = ph.sig("chosen_counted", 1)
        exped = ph.sig("gate_exp", 1)
        with nc.Block() as block:
            @block.sync
            def _(eng):
                eng.dma_start(wr[:], w_r).then_inc(loaded.sem, 16)
                eng.dma_start(br[:], b_r).then_inc(loaded.sem, 16)
                eng.dma_start(rank[:], consts["rank"]).then_inc(loaded.sem, 16)
                for dst, src in ((before, "before"), (every, "every"), (sizes, "sizes"), (behind, "behind"),
                                 (number, "number")):
                    eng.dma_start(dst[:], consts[src]).then_inc(loaded.sem, 16)

            @block.tensor
            def _(eng):
                eng.wait_ge(loaded.sem, loaded.at(n_load))
                for c in range(chunks + 1):
                    if c < chunks:
                        if c >= 2:
                            eng.wait_ge(l_ready.sem, l_ready.at(c - 1))
                        for k in range(KT):
                            mm = eng.matmul(psL[c % 2][0:E, :], wr[:, k, :], hT[:, k, c * CH:(c + 1) * CH],
                                            start=(k == 0), stop=(k == KT - 1))
                        mm.then_inc(l_psum.sem, 1)
                    if c >= 1:
                        u = (c - 1) % 2
                        eng.wait_ge(l_ready.sem, l_ready.at(c))
                        if c >= 3:
                            eng.wait_ge(t_read.sem, t_read.at(c - 2))
                        for j in range(4):
                            mm = eng.transpose(psT[u][:, j, :], lT[u][:, j * P:(j + 1) * P], consts["ident"][0:E, 0:E])
                        mm.then_inc(t_psum.sem, 1)
                eng.wait_ge(is_chosen.sem, is_chosen.at(1))
                sel = chosen[:].rearrange("p t e -> p (t e)")
                eng.matmul(psN[:], before[:], sel, start=True, stop=True)
                eng.matmul(psA[:], every[:], sel, start=True, stop=True).then_inc(counted.sem, 1)

            @block.scalar
            def _(eng):
                eng.wait_ge(loaded.sem, loaded.at(n_load))
                for c in range(chunks):
                    eng.wait_ge(l_psum.sem, l_psum.at(c + 1))
                    if c >= 2:
                        eng.wait_ge(t_psum.sem, t_psum.at(c - 1))
                    eng.activation(lT[c % 2][:], psL[c % 2][0:E, :], ACT.Identity, bias=br[:], scale=1.0)\
                       .then_inc(l_ready.sem, 1)
                eng.wait_ge(step.sem, step.at(12))
                eng.activation(m[2][:], m[2][:], ACT.Exp).then_inc(exped.sem, 1)

            @block.vector
            def _(eng):
                for c in range(chunks):
                    eng.wait_ge(t_psum.sem, t_psum.at(c + 1))
                    eng.tensor_copy(lg[:, c * 4:(c + 1) * 4, :], psT[c % 2][:]).then_inc(t_read.sem, 1)
                eng.wait_ge(t_read.sem, t_read.at(chunks))
                eng.wait_ge(loaded.sem, loaded.at(n_load))
                ranks = rank[:].unsqueeze(1).to_broadcast([P, NT, E])

                def wide(v):
                    return v[:].unsqueeze(2).to_broadcast([P, NT, E])

                n = 0
                for i in range(2):
                    eng.tensor_reduce(m[i][:], lg[:], AX.X, ALU.max).then_inc(step.sem, 1)
                    eng.wait_ge(step.sem, step.at(n + 1))
                    eng.tensor_tensor(wt[:], lg[:], wide(m[i]), ALU.is_equal).then_inc(step.sem, 1)
                    eng.wait_ge(step.sem, step.at(n + 2))
                    eng.tensor_tensor(wt[:], wt[:], ranks, ALU.mult).then_inc(step.sem, 1)
                    eng.wait_ge(step.sem, step.at(n + 3))
                    eng.tensor_reduce(m[4][:], wt[:], AX.X, ALU.max).then_inc(step.sem, 1)
                    eng.wait_ge(step.sem, step.at(n + 4))
                    eng.tensor_tensor(one[i][:], wt[:], wide(m[4]), ALU.is_equal).then_inc(step.sem, 1)
                    eng.wait_ge(step.sem, step.at(n + 5))
                    n += 5
                    if i == 0:
                        eng.scalar_tensor_tensor(lg[:], one[0][:], NEG, lg[:], ALU.mult, ALU.add).then_inc(step.sem, 1)
                        n += 1
                        eng.wait_ge(step.sem, step.at(n))
                eng.tensor_tensor(chosen[:], one[0][:], one[1][:], ALU.add).then_inc(is_chosen.sem, 1)
                eng.tensor_tensor(m[2][:], m[1][:], m[0][:], ALU.subtract).then_inc(step.sem, 1)
                eng.wait_ge(exped.sem, exped.at(1))
                eng.tensor_scalar(m[3][:], m[2][:], 1.0, None, ALU.add).then_inc(step.sem, 1)
                eng.wait_ge(step.sem, step.at(13))
                eng.reciprocal(gates[0][:], m[3][:]).then_inc(step.sem, 1)
                eng.wait_ge(step.sem, step.at(14))
                eng.tensor_tensor(gates[1][:], m[2][:], gates[0][:], ALU.mult)

                n = 14

                def then(op):
                    nonlocal n
                    op.then_inc(step.sem, 1)
                    n += 1
                    eng.wait_ge(step.sem, step.at(n))

                eng.wait_ge(counted.sem, counted.at(1))
                psA_v = psA[:].rearrange("p (t e) -> p t e", e=E)
                then(eng.tensor_copy(seen[0][:], psA_v))
                for k in range(SCAN):
                    old, new, far = seen[k % 2], seen[(k + 1) % 2], 1 << k
                    then(eng.tensor_copy(new[:, 0:far, :], old[:, 0:far, :]))
                    then(eng.tensor_tensor(new[:, far:NT, :], old[:, far:NT, :], old[:, 0:NT - far, :], ALU.add))
                total = seen[SCAN % 2]
                then(eng.tensor_tensor(place[:], total[:], psA_v, ALU.subtract))
                then(eng.tensor_tensor(place[:], place[:], psN[:].rearrange("p (t e) -> p t e", e=E), ALU.add))
                then(eng.tensor_tensor(size_over[:], total[:, NT - 1, :].unsqueeze(2).to_broadcast([P, E, TIMES]),
                                       sizes[:], ALU.is_gt))
                then(eng.tensor_reduce(blocks_of[:], size_over[:], AX.X, ALU.add))
                then(eng.tensor_tensor(earlier[:], blocks_of[:].unsqueeze(1).to_broadcast([P, E, E]), behind[:],
                                       ALU.mult))
                then(eng.tensor_reduce(first[:], earlier[:], AX.X, ALU.add))
                then(eng.tensor_tensor(last[:], first[:], blocks_of[:], ALU.add))
                then(eng.tensor_tensor(past[:], number[:], last[:].unsqueeze(1).to_broadcast([P, NB, E]), ALU.is_ge))
                then(eng.tensor_reduce(owner[:], past[:], AX.X, ALU.add))
                then(eng.tensor_scalar(owner[:], owner[:], float(E - 1), None, ALU.min))
                then(eng.tensor_copy(block_expert[:], owner[0:1, :]))
                then(eng.tensor_scalar(first[:], first[:], float(BS), 2.0 * BS, ALU.mult, ALU.add))
                then(eng.tensor_tensor(place[:], place[:], first[:].unsqueeze(1).to_broadcast([P, NT, E]), ALU.add))
                for i in range(2):
                    then(eng.tensor_tensor(one[i][:], one[i][:], place[:], ALU.mult))
                    then(eng.tensor_reduce(dest[:, i, :], one[i][:], AX.X, ALU.add))
                then(eng.tensor_copy(slots[:], dest[:]))
                assert n == step.total


def dispatch_phase(nc, signals, name, x, moments, slots, Xs):
    SET = 4
    mean, rstd = moments
    with Phase(nc, signals, name) as ph:
        rows = [[ph.sb(f"row{u}_{j}", [P, D]) for j in range(SET)] for u in range(2)]
        index = [ph.sb(f"index{u}", [P, 2, SET], U32) for u in range(2)]
        ready = ph.sig("rows_ready", NT // SET)
        begun = ph.sig("set_begun", NT // SET)
        sent = [ph.sig(f"rows_sent{u}", 16 * 2 * SET * (NT // SET // 2)) for u in range(2)]
        ALL = 16 * 2 * SET
        with nc.Block() as block:
            @block.vector
            def _(eng):
                def fill(pair, u):
                    eng.tensor_copy(index[u][:], slots[:, :, bass.ds((pair * 2 + u) * SET, SET)])
                    for j in range(SET):
                        t = (pair * 2 + u) * SET + j
                        op = eng.tensor_scalar(rows[u][j][:], x[:, t, :], mean[:, bass.ds(t, 1)],
                                               rstd[:, bass.ds(t, 1)], ALU.subtract, ALU.mult)
                    op.then_inc(ready.sem, 1)

                for u in range(2):
                    fill(0, u)
                with eng.Fori(0, NT // SET // 2 - 1) as pair:
                    for u in range(2):
                        eng.wait_ge(sent[u].sem, sent[u].at(pair * ALL + ALL))
                        fill(pair + 1, u)

            @block.gpsimd
            def _(eng):
                with eng.Fori(0, NT // SET // 2) as pair:
                    for u in range(2):
                        eng.wait_ge(ready.sem, ready.at(pair * 2 + (u + 1)))
                        eng.sem_inc(begun.sem, 1)
                        for j in range(SET):
                            for i in range(2):
                                eng.indirect_dma_start(Xs[:], bass.IndirectOffsetOnAxis(index[u][:, i, j:j + 1], 0),
                                                       rows[u][j][:], None).then_inc(sent[u].sem, 16)
                for u in range(2):
                    eng.wait_ge(sent[u].sem, sent[u].at(sent[u].total))


def expert_blocks_phase(nc, signals, name, Xs, Ys, block_expert, cols, w_1, w_2, b_1, b_2, func, consts):
    TS = BS // P
    UNROLL = 2
    with Phase(nc, signals, name) as ph:
        w1 = [ph.sb(f"w1{v}", [P, KT, FF]) for v in range(2)]
        w2 = [ph.sb(f"w2{v}", [P, FT, D]) for v in range(2)]
        b1 = [ph.sb(f"b1{v}", [P, FT]) for v in range(2)]
        b2 = [ph.sb(f"b2{v}", [P, D]) for v in range(2)]
        rows = [ph.sb(f"rows{v}", [P, TS, D]) for v in range(2)]
        h = [ph.sb(f"h{v}", [P, KT, BS]) for v in range(2)]
        h1 = [ph.sb(f"h1{v}", [P, FT, BS]) for v in range(2)]
        y = [ph.sb(f"y{v}", [P, TS, D]) for v in range(2)]
        psX = ph.ps("psX", [P, KT, BS])
        ps1 = [ph.ps(f"ps1{i}", [P, 512]) for i in range(4)]
        ps2 = [ph.ps(f"ps2{i}", [P, 512]) for i in range(TS)]
        loaded = [ph.sig(f"expert_loaded{v}", 64 * NB // 2) for v in range(2)]
        x_loaded = [ph.sig(f"rows_loaded{v}", 16 * (NB // 2 + 1 - v)) for v in range(2)]
        y_clear = ph.sig("outputs_cleared", 1)
        x_psum = ph.sig("rows_turned", 1 + NB + 1)
        h_ready = ph.sig("rows_scaled", NB + 1)
        h_psum = ph.sig("hidden_in_psum", NB * FT)
        h1_ready = ph.sig("hidden_ready", 4 + NB * FT)
        y_psum = ph.sig("output_in_psum", 2 * TS + NB * TS)
        y_ready = ph.sig("output_ready", 2 * TS + NB * TS)
        y_stored = [ph.sig(f"output_stored{v}", 16 * (NB // 2 + 1)) for v in range(2)]

        def each_block(eng, body):
            with eng.Fori(0, NB // UNROLL) as group:
                for v in range(UNROLL):
                    body(group * UNROLL + v, v)

        def load_rows(eng, b, v):
            eng.dma_start(rows[v][:], Xs[bass.ds((b + 2) * BS, BS), :].rearrange("(j p) d -> p j d", p=P))\
               .then_inc(x_loaded[v].sem, 16)

        def store_output(eng, b, v):
            eng.dma_start(Ys[bass.ds(b * BS, BS), :].rearrange("(j p) d -> p j d", p=P), y[v][:])\
               .then_inc(y_stored[v].sem, 16)

        with nc.Block() as block:
            @block.sync
            def _(eng):
                load_rows(eng, 0, 0)
                eng.wait_ge(y_clear.sem, y_clear.at(1))

                def body(b, v):
                    e = eng.value_load(block_expert[0:1, bass.ds(b, 1)], min_val=0, max_val=E - 1)
                    eng.wait_ge(x_psum.sem, x_psum.at(b + 1))
                    eng.wait_ge(y_ready.sem, y_ready.at(b * TS + TS))
                    sel = bass.ds(e, 1)
                    eng.dma_start(w1[v][:], w_1[sel].rearrange("e (k p) n -> p (e k) n", p=P)).then_inc(loaded[v].sem, 16)
                    eng.dma_start(w2[v][:], w_2[sel].rearrange("e (k p) n -> p (e k) n", p=P)).then_inc(loaded[v].sem, 16)
                    eng.dma_start(b1[v][:], b_1[sel].rearrange("e p m -> p (e m)")).then_inc(loaded[v].sem, 16)
                    eng.dma_start(b2[v][:], b_2[sel, :].to_broadcast([P, D])).then_inc(loaded[v].sem, 16)
                    load_rows(eng, b + 1, (v + 1) % 2)
                    store_output(eng, b, v)

                each_block(eng, body)
                for v in range(2):
                    eng.wait_ge(y_ready.sem, y_ready.at((NB + v) * TS + TS))
                    store_output(eng, NB + v, v)
                for v in range(2):
                    eng.wait_ge(y_stored[v].sem, y_stored[v].at(y_stored[v].total))

            @block.gpsimd
            def _(eng):
                eng.memset(y[0][:], 0.0)
                eng.memset(y[1][:], 0.0).then_inc(y_clear.sem, 1)

            @block.tensor
            def _(eng):
                def turn_rows(b, v):
                    eng.wait_ge(x_loaded[v].sem, x_loaded[v].at((b - v) * (16 // UNROLL) + 16))
                    for k in range(KT):
                        for j in range(TS):
                            mm = eng.transpose(psX[:, k, j * P:(j + 1) * P], rows[v][:, j, k * P:(k + 1) * P],
                                               consts["ident"][:])
                    mm.then_inc(x_psum.sem, 1)

                eng.sem_inc(y_psum.sem, 2 * TS)
                eng.sem_inc(x_psum.sem, 1)
                turn_rows(0, 0)

                def body(b, v):
                    eng.wait_ge(loaded[v].sem, loaded[v].at((b - v) * (64 // UNROLL) + 64))
                    eng.wait_ge(h_ready.sem, h_ready.at(b + 1))
                    for m in range(FT):
                        eng.wait_ge(h1_ready.sem, h1_ready.at(b * FT + (m + 1)))
                        for k in range(KT):
                            mm = eng.matmul(ps1[m % 4][:, 0:BS], w1[v][:, k, m * P:(m + 1) * P], h[v][:, k, :],
                                            start=(k == 0), stop=(k == KT - 1))
                        mm.then_inc(h_psum.sem, 1)
                    turn_rows(b + 1, (v + 1) % 2)
                    for j in range(TS):
                        eng.wait_ge(y_ready.sem, y_ready.at(b * TS + (j + 1 + TS)))
                        for m in range(FT):
                            if j == 0:
                                eng.wait_ge(h1_ready.sem, h1_ready.at(b * FT + (m + 1 + 4)))
                            mm = eng.matmul(ps2[j][:, 0:D], h1[v][:, m, j * P:(j + 1) * P], w2[v][:, m, :],
                                            start=(m == 0), stop=(m == FT - 1))
                        mm.then_inc(y_psum.sem, 1)

                each_block(eng, body)

            @block.scalar
            def _(eng):
                eng.sem_inc(h1_ready.sem, 4)

                def body(b, v):
                    eng.wait_ge(y_psum.sem, y_psum.at(b * TS + TS))
                    for m in range(FT):
                        eng.wait_ge(h_psum.sem, h_psum.at(b * FT + (m + 1)))
                        eng.activation(h1[v][:, m, :], ps1[m % 4][:, 0:BS], func, bias=b1[v][:, m:m + 1], scale=1.0)\
                           .then_inc(h1_ready.sem, 1)

                each_block(eng, body)

            @block.vector
            def _(eng):
                def scale_rows(b, v):
                    eng.wait_ge(x_psum.sem, x_psum.at(b + 2))
                    for k in range(KT):
                        op = eng.tensor_scalar(h[v][:, k, :], psX[:, k, :], cols[0][:, k:k + 1], cols[1][:, k:k + 1],
                                               ALU.mult, ALU.add)
                    op.then_inc(h_ready.sem, 1)

                eng.sem_inc(y_ready.sem, 2 * TS)
                for v in range(2):
                    eng.wait_ge(y_clear.sem, y_clear.at(1))
                scale_rows(0, 0)

                def body(b, v):
                    scale_rows(b + 1, (v + 1) % 2)
                    eng.wait_ge(y_stored[v].sem, y_stored[v].at((b - v) * (16 // UNROLL) + 16))
                    for j in range(TS):
                        eng.wait_ge(y_psum.sem, y_psum.at(b * TS + (j + 1 + 2 * TS)))
                        eng.tensor_tensor(y[v][:, j, :], ps2[j][:, 0:D], b2[v][:], ALU.add).then_inc(y_ready.sem, 1)

                each_block(eng, body)


def combine_phase(nc, signals, name, x, gates, slots, Ys):
    SET = 4
    with Phase(nc, signals, name) as ph:
        rows = [[[ph.sb(f"row{u}_{i}_{j}", [P, D]) for j in range(SET)] for i in range(2)] for u in range(2)]
        index = [ph.sb(f"index{u}", [P, 2, SET], U32) for u in range(2)]
        ALL = 16 * 2 * SET
        pairs = NT // SET // 2
        indexed = ph.sig("index_ready", NT // SET)
        begun = ph.sig("set_begun", NT // SET)
        fetched = [ph.sig(f"rows_fetched{u}", ALL * pairs) for u in range(2)]
        added = ph.sig("first_expert_added", NT)
        used = ph.sig("rows_used", 2 + NT // SET)
        with nc.Block() as block:
            @block.vector
            def _(eng):
                eng.sem_inc(used.sem, 2)

                def indices(pair, u):
                    eng.tensor_copy(index[u][:], slots[:, :, bass.ds((pair * 2 + u) * SET, SET)])\
                       .then_inc(indexed.sem, 1)

                def add(pair, u):
                    eng.wait_ge(fetched[u].sem, fetched[u].at(pair * ALL + ALL))
                    for i in range(2):
                        for j in range(SET):
                            t = (pair * 2 + u) * SET + j
                            if i:
                                eng.wait_ge(added.sem, added.at(t + 1))
                            op = eng.scalar_tensor_tensor(x[:, t, :], rows[u][i][j][:], gates[i][:, bass.ds(t, 1)],
                                                          x[:, t, :], ALU.mult, ALU.add)
                            if i == 0:
                                op.then_inc(added.sem, 1)
                    op.then_inc(used.sem, 1)

                for u in range(2):
                    indices(0, u)
                with eng.Fori(0, pairs - 1) as pair:
                    for u in range(2):
                        add(pair, u)
                        indices(pair + 1, u)
                for u in range(2):
                    add(pairs - 1, u)

            @block.gpsimd
            def _(eng):
                with eng.Fori(0, pairs) as pair:
                    for u in range(2):
                        eng.wait_ge(used.sem, used.at(pair * 2 + (u + 1)))
                        eng.wait_ge(indexed.sem, indexed.at(pair * 2 + (u + 1)))
                        eng.sem_inc(begun.sem, 1)
                        for j in range(SET):
                            for i in range(2):
                                eng.indirect_dma_start(rows[u][i][j][:], None, Ys[:],
                                                       bass.IndirectOffsetOnAxis(index[u][:, i, j:j + 1], 0))\
                                   .then_inc(fetched[u].sem, 16)


def feed_forward_phase(nc, signals, name, hT, x, rows, tokens, experts, w_1, w_2, b_1, b_2, func, consts, gates=None):
    cw = min(CH, tokens)
    chunks = tokens // cw
    tpc = cw // rows
    UC = min(2, chunks)
    UE = min(2, experts)
    with Phase(nc, signals, name) as ph:
        w1 = [ph.sb(f"w1{v}", [P, KT, FF]) for v in range(UE)]
        w2 = [ph.sb(f"w2{v}", [P, FT, D]) for v in range(UE)]
        b1 = [ph.sb(f"b1{v}", [P, FT]) for v in range(UE)]
        b2 = [ph.sb(f"b2{v}", [1, D]) for v in range(UE)]
        h1 = [ph.sb(f"h1{u}", [P, FT, cw]) for u in range(UC)]
        ps1 = [ph.ps(f"ps1{i}", [P, CH]) for i in range(4)]
        ps2 = [ph.ps(f"ps2{i}", [P, 512]) for i in range(2)]
        n_hidden = experts * chunks * FT
        n_out = experts * chunks * tpc
        loaded = [ph.sig(f"expert_loaded{v}", 64 * experts // UE) for v in range(UE)]
        h_psum = ph.sig("hidden_in_psum", n_hidden)
        h_ready = ph.sig("hidden_ready", 4 + n_hidden)
        y_psum = ph.sig("output_in_psum", UC * tpc + n_out)
        y_added = ph.sig("output_added", 2 + n_out)
        expert_done = ph.sig("expert_done", UE + experts if experts > 1 else 0)
        H_FREE, Y_FREE, OUT_FREE = 4, 2, UC * tpc

        def each_chunk(eng, body):
            def chunk_loop(e, v):
                if chunks == UC:
                    for u in range(UC):
                        body(e, v, e * chunks + u, u, u)
                else:
                    with eng.Fori(0, chunks // UC) as pair:
                        c = pair * UC
                        for u in range(UC):
                            body(e, v, e * chunks + c + u, c + u, u)
            if experts == 1:
                chunk_loop(0, 0)
            else:
                with eng.Fori(0, experts // UE) as group:
                    e0 = group * UE
                    for v in range(UE):
                        chunk_loop(e0 + v, v)

        with nc.Block() as block:
            @block.sync
            def _(eng):
                def load(e, v):
                    if experts > 1:
                        eng.wait_ge(expert_done.sem, expert_done.at(e + 1))
                    sel = bass.ds(e, 1)
                    eng.dma_start(w1[v][:], w_1[sel].rearrange("e (k p) n -> p (e k) n", p=P)).then_inc(loaded[v].sem, 16)
                    eng.dma_start(w2[v][:], w_2[sel].rearrange("e (k p) n -> p (e k) n", p=P)).then_inc(loaded[v].sem, 16)
                    eng.dma_start(b1[v][:], b_1[sel].rearrange("e p m -> p (e m)")).then_inc(loaded[v].sem, 16)
                    eng.dma_start(b2[v][:], b_2[sel, :]).then_inc(loaded[v].sem, 16)

                if experts == 1:
                    load(0, 0)
                else:
                    with eng.Fori(0, experts // UE) as group:
                        e0 = group * UE
                        for v in range(UE):
                            load(e0 + v, v)

            @block.tensor
            def _(eng):
                eng.sem_inc(y_psum.sem, OUT_FREE)
                if experts > 1:
                    eng.sem_inc(expert_done.sem, UE)

                def body(e, v, n, c, u):
                    eng.wait_ge(loaded[v].sem, loaded[v].at((e - v) * (64 // UE) + 64))
                    for m in range(FT):
                        eng.wait_ge(h_ready.sem, h_ready.at(n * FT + (m + 1)))
                        for k in range(KT):
                            mm = eng.matmul(ps1[m % 4][:, 0:cw], w1[v][:, k, m * P:(m + 1) * P],
                                            hT[:, k, bass.ds(c * cw, cw)], start=(k == 0), stop=(k == KT - 1))
                        mm.then_inc(h_psum.sem, 1)
                    for j in range(tpc):
                        eng.wait_ge(y_added.sem, y_added.at(n * tpc + (j + 1)))
                        eng.matmul(ps2[j % 2][0:rows, 0:D], consts["ones"][0:1, 0:rows], b2[v][:], start=True, stop=False)
                        for m in range(FT):
                            if j == 0:
                                eng.wait_ge(h_ready.sem, h_ready.at(n * FT + (m + 1 + H_FREE)))
                            mm = eng.matmul(ps2[j % 2][0:rows, 0:D], h1[u][:, m, j * rows:(j + 1) * rows], w2[v][:, m, :],
                                            start=False, stop=(m == FT - 1))
                        mm.then_inc(y_psum.sem, 1)

                if experts == 1:
                    each_chunk(eng, body)
                else:
                    with eng.Fori(0, experts // UE) as group:
                        e0 = group * UE
                        for v in range(UE):
                            with eng.Fori(0, chunks // UC) as pair:
                                c = pair * UC
                                for u in range(UC):
                                    body(e0 + v, v, (e0 + v) * chunks + c + u, c + u, u)
                            eng.drain().then_inc(expert_done.sem, 1)

            @block.scalar
            def _(eng):
                eng.sem_inc(h_ready.sem, H_FREE)

                def body(e, v, n, c, u):
                    eng.wait_ge(y_psum.sem, y_psum.at(n * tpc + tpc))
                    for m in range(FT):
                        eng.wait_ge(h_psum.sem, h_psum.at(n * FT + (m + 1)))
                        eng.activation(h1[u][:, m, :], ps1[m % 4][:, 0:cw], func, bias=b1[v][:, m:m + 1], scale=1.0)\
                           .then_inc(h_ready.sem, 1)

                each_chunk(eng, body)

            @block.vector
            def _(eng):
                eng.sem_inc(y_added.sem, Y_FREE)

                def body(e, v, n, c, u):
                    for j in range(tpc):
                        eng.wait_ge(y_psum.sem, y_psum.at(n * tpc + (j + 1 + OUT_FREE)))
                        eng.wait_ge(y_added.sem, y_added.at(n * tpc + (j + Y_FREE)))
                        xt = x[0:rows, c * tpc + j, :]
                        if gates is None:
                            eng.tensor_tensor(xt, xt, ps2[j % 2][0:rows, 0:D], ALU.add).then_inc(y_added.sem, 1)
                        else:
                            gate = gates[:, c * tpc + j, bass.ds(e, 1)]
                            eng.scalar_tensor_tensor(xt, ps2[j % 2][0:rows, 0:D], gate, xt, ALU.mult, ALU.add)\
                               .then_inc(y_added.sem, 1)

                each_chunk(eng, body)


def build(nc, d, places, out):
    with ExitStack() as ctx:
        def sb(name, shape, dt=F32):
            return ctx.enter_context(nc.sbuf_tensor(name, shape, dt))

        signals = Signals(nc, ctx)
        x = sb("x_res", [P, NT, D])
        hT = sb("activationsT", [P, KT, NT * P])
        zeros = sb("zeros", [P, ZERO])
        Qd = nc.dram_tensor("q_pieces", [3, B * D + 2 * DK, SQ], BF16)
        Kd = nc.dram_tensor("k_pieces", [3, B * D + 2 * DK, SQ], BF16)
        Vd = nc.dram_tensor("v_pieces", [B * H + 2, P, 3 * DK, TB], BF16)
        Od = nc.dram_tensor("context_pieces", [3, 2 * DK + B * D, SQ], F32)
        SLOTS = (NB + 3) * BS
        Xs = nc.dram_tensor("tokens_by_expert", [SLOTS, D], F32)
        Ys = nc.dram_tensor("outputs_by_expert", [SLOTS - BS, D], F32)
        Dd = nc.dram_tensor("denominators", [2 + B * H, SQ], F32)
        cT = sb("contextT", [P, KT, B * SC])
        consts = {"ident": sb("ident", [P, P]), "ones": sb("ones", [1, P]), "head_rows": sb("head_rows", [P, HT]),
                  "minus_half": sb("minus_half", [P, NT]),
                  "identb": sb("identb", [P, P], BF16), "spread": sb("spread", [B * H, B * KT, P])}
        xe = sb("encoder", [SC, B, D])
        xd = d["x"].rearrange("b s d -> (b s) d").rearrange("(t p) d -> p t d", p=P)
        packed = sb("packed_columns", [P, d["columns"].shape[1]])
        start_loaded = signals("start_loaded", 16 * 10)
        with nc.Block() as block:
            @block.sync
            def _(eng):
                eng.dma_start(packed[:], d["columns"]).then_inc(start_loaded.sem, 16)
                eng.dma_start(consts["ident"][:], d["ident"]).then_inc(start_loaded.sem, 16)
                eng.dma_start(consts["minus_half"][:], d["minus_half"]).then_inc(start_loaded.sem, 16)
                eng.dma_start(consts["ones"][:], d["ones"]).then_inc(start_loaded.sem, 16)
                eng.dma_start(consts["head_rows"][:], d["head_rows"]).then_inc(start_loaded.sem, 16)
                eng.dma_start(cT[:], d["ctxT"].rearrange("(k p) c -> p k c", p=P)).then_inc(start_loaded.sem, 16)
                eng.dma_start(hT[:], d["xT"].rearrange("(k p) t -> p k t", p=P)).then_inc(start_loaded.sem, 16)
                eng.dma_start(x[:], xd).then_inc(start_loaded.sem, 16)
                eng.dma_start(consts["spread"][:], d["spread"]).then_inc(start_loaded.sem, 16)
                eng.dma_start(xe[:], d["ctx"].rearrange("b c d -> c b d")).then_inc(start_loaded.sem, 16)
                eng.wait_ge(start_loaded.sem, start_loaded.at(16 * 10))

            @block.vector
            def _(eng):
                eng.wait_ge(start_loaded.sem, start_loaded.at(16 * 10))
                eng.tensor_copy(consts["identb"][:], consts["ident"][:])
                eng.memset(zeros[:], 0.0)
        signals.phase_over()

        def cols(name):
            at, n = places[name]
            return packed[:, at:at + n]

        def weights(name):
            return d[name].rearrange("(k p) n -> p k n", p=P)

        for table in ("rank", "before", "every", "sizes", "behind", "number"):
            consts[table] = d[table]

        def cross(name, sT, x_to, rows, tiles, hT_from, bias=None, rope=None, meanwhile=None):
            pair = range(2) if rope else range(1)
            tag = ("", "_turned")
            with ExitStack() as heads:
                Kbd = heads.enter_context(nc.sbuf_tensor(name + "_Kbd", [P, B, KT, HT * SC], F32))
                Vbd = heads.enter_context(nc.sbuf_tensor(name + "_Vbd", [P, B, H // 2, PW], F32))
                context_heads_phase(nc, signals, name + "kv", sT, [weights(name + "_wk" + tag[r]) for r in pair],
                                    weights(name + "_wv"), [cols(name + "_bk" + tag[r]) for r in pair],
                                    d[name + "_bv"], consts, Kbd, Vbd, rope=rope and rope[1])
                cross_attention_phase(nc, signals, name + "at", hT_from, x_to, rows, tiles,
                                      [weights(name + "_wq" + tag[r]) for r in pair],
                                      [cols(name + "_bq" + tag[r]) for r in pair], weights(name + "_wo"),
                                      d[name + "_bo"], Kbd, Vbd, consts, bias=bias, rope=rope and rope[0],
                                      meanwhile=meanwhile)

        def self_attention(name, causal, near=None, rope=None):
            pair = range(2) if rope else range(1)
            tag = ("", "_turned")
            self_heads_phase(nc, signals, name + "qkv", hT, [weights(name + "_wq" + tag[r]) for r in pair],
                             [weights(name + "_wk" + tag[r]) for r in pair], weights(name + "_wv"),
                             [cols(name + "_bq" + tag[r]) for r in pair],
                             [cols(name + "_bk" + tag[r]) for r in pair], d[name + "_bv"], consts,
                             Qd, Kd, Vd, rope=rope)
            self_attention_phase(nc, signals, name + "at", Qd, Kd, Vd, Od, Dd, consts, causal, near)
            output_phase(nc, signals, name + "out", Od, Dd, x, weights(name + "_wo"), d[name + "_bo"], consts)

        def norm(name):
            return cols(name + "_g"), cols(name + "_b")

        def clear_slots(eng):
            runs = SLOTS * D // P // ZERO
            slots_cleared = signals("slots_cleared", 16)
            eng.dma_start(Xs.rearrange("(p r) d -> p (r d)", p=P).rearrange("p (n c) -> p n c", c=ZERO),
                          zeros[:].unsqueeze(1).to_broadcast([P, runs, ZERO])).then_inc(slots_cleared.sem, 16)
            eng.wait_ge(slots_cleared.sem, slots_cleared.at(16))

        cross("L0", cT, x, P, TB, hT, meanwhile=clear_slots)
        output_norm_phase(nc, signals, "L0ln", x, consts, d["L0_gamma"], d["L0_beta"], 1e-5)

        transpose_phase(nc, signals, "L1t1", x, hT, consts, P, NT, norm("L1_n1"))
        self_attention("L1sa", False)
        transpose_phase(nc, signals, "L1t2", x, hT, consts, P, NT, norm("L1_n2"))
        with ExitStack() as normed:
            nT = normed.enter_context(nc.sbuf_tensor("L1_contextT", [P, KT, B * SC], F32))
            transpose_phase(nc, signals, "L1t3", xe, nT, consts, SC, B, norm("L1_nc"))
            cross("L1ca", nT, x, P, TB, hT)
        with ExitStack() as mixture:
            def kept(name, shape, dt=F32):
                return mixture.enter_context(nc.sbuf_tensor(name, shape, dt))

            moments = (kept("L1_mean", [P, NT]), kept("L1_rstd", [P, NT]))
            gates = [kept(f"gate{i}", [P, NT]) for i in range(2)]
            slots = kept("slots", [P, 2, NT], U32)
            block_expert = kept("block_expert", [1, NB], I32)
            transpose_phase(nc, signals, "L1t4", x, hT, consts, P, NT, norm("L1_n3"), moments=moments)
            router_phase(nc, signals, "L1r", hT, gates, slots, block_expert, weights("L1_wr"), d["L1_br"], consts)
            dispatch_phase(nc, signals, "L1d", x, moments, slots, Xs)
            expert_blocks_phase(nc, signals, "L1ff", Xs, Ys, block_expert, norm("L1_n3"), d["L1_w1"], d["L1_w2"],
                                d["L1_b1"], d["L1_b2"], ACT.Gelu, consts)
            combine_phase(nc, signals, "L1c", x, gates, slots, Ys)

        with ExitStack() as encoder:
            nT = encoder.enter_context(nc.sbuf_tensor("L2_contextT", [P, KT, B * SC], F32))
            transpose_phase(nc, signals, "L2e1", xe, nT, consts, SC, B, norm("L2_e1"), 1e-6)
            cross("L2e", nT, xe, SC, 1, nT, bias=(d["L2_enc_bias"], 1))
            transpose_phase(nc, signals, "L2e2", xe, nT, consts, SC, B, norm("L2_e2"), 1e-6)
            feed_forward_phase(nc, signals, "L2ef", nT, xe, SC, B * SC, 1, d["L2e_w1"], d["L2e_w2"],
                               d["L2e_b1"], d["L2e_b2"], ACT.Relu, consts)
            transpose_phase(nc, signals, "L2e3", xe, nT, consts, SC, B)
            transpose_phase(nc, signals, "L2t1", x, hT, consts, P, NT, norm("L2_n1"), 1e-6)
            with ExitStack() as tables:
                q_near = tables.enter_context(nc.sbuf_tensor("q_near", [P, H + 1, 2 * P], BF16))
                k_near = [tables.enter_context(nc.sbuf_tensor(f"k_near{i}", [P, H + 1, 2 * P], BF16))
                          for i in range(3)]
                near_blocks_phase(nc, signals, "L2nb", d["L2_rel_q"], d["L2_rel_k"], d["L2_rel_far"],
                                  d["near_mask_q"], d["near_mask_k"], q_near, k_near)
                self_attention("L2sa", True, near=(q_near, k_near, True, True))
            transpose_phase(nc, signals, "L2t2", x, hT, consts, P, NT, norm("L2_n2"), 1e-6)
            cross("L2ca", nT, x, P, TB, hT, bias=(d["L2_cross_bias"], 3))
        transpose_phase(nc, signals, "L2t3", x, hT, consts, P, NT, norm("L2_n3"), 1e-6)
        feed_forward_phase(nc, signals, "L2ff", hT, x, P, NT * P, 1, d["L2_w1"], d["L2_w2"], d["L2_b1"],
                           d["L2_b2"], ACT.Relu, consts)

        with ExitStack() as rotary:
            turn = {}
            for part in ("q_cos", "q_sin", "k_cos", "k_sin"):
                turn[part] = rotary.enter_context(nc.sbuf_tensor("turn_" + part, [P, SQ], F32))
            mask = [rotary.enter_context(nc.sbuf_tensor("diagonal_" + part, [P, P], BF16)) for part in "qk"]
            with Phase(nc, signals, "L3l") as ph:
                mask_f = [ph.sb("mask_" + part, [P, P]) for part in "qk"]
                loaded = ph.sig("weights_loaded", 16 * 6)
                with nc.Block() as block:
                    @block.sync
                    def _(eng):
                        for part, tile in turn.items():
                            eng.dma_start(tile[:], d["turn_" + part]).then_inc(loaded.sem, 16)
                        eng.dma_start(mask_f[0][:], d["near_mask_q"][:, P:2 * P]).then_inc(loaded.sem, 16)
                        eng.dma_start(mask_f[1][:], d["near_mask_k"][:, 0:P]).then_inc(loaded.sem, 16)

                    @block.vector
                    def _(eng):
                        eng.wait_ge(loaded.sem, loaded.at(16 * 6))
                        for i in range(2):
                            eng.tensor_copy(mask[i][:], mask_f[i][:])
            rope = ((turn["q_cos"], turn["q_sin"]), (turn["k_cos"], turn["k_sin"]))
            transpose_phase(nc, signals, "L3t1", x, hT, consts, P, NT, norm("L3_n1"))
            self_attention("L3sa", True, near=(mask[0], [mask[1]], False, False), rope=rope)
            transpose_phase(nc, signals, "L3t2", x, hT, consts, P, NT, norm("L3_n2"))
            cross("L3ca", cT, x, P, TB, hT, rope=rope)
        transpose_phase(nc, signals, "L3t3", x, hT, consts, P, NT, norm("L3_n3"))
        feed_forward_phase(nc, signals, "L3ff", hT, x, P, NT * P, 1, d["L3_w1"], d["L3_w2"], d["L3_b1"],
                           d["L3_b2"], ACT.Gelu_apprx_tanh, consts)

        written = signals("output_written", 16)
        with nc.Block() as block:
            @block.sync
            def _(eng):
                eng.dma_start(out.rearrange("b s d -> (b s) d").rearrange("(t p) d -> p t d", p=P), x[:])\
                   .then_inc(written.sem, 16)
                eng.wait_ge(written.sem, written.at(16))


def lay_out(inp):
    a, places, packed = {}, {}, []

    def columns(name, v):
        v = v.reshape(-1, P).T
        places[name] = (sum(c.shape[1] for c in packed), v.shape[1])
        packed.append(v)

    a["x"] = inp["x"]
    a["xT"] = np.ascontiguousarray(inp["x"].reshape(B * SQ, D).T)
    a["ctxT"] = np.ascontiguousarray(inp["ctx_1024"].reshape(B * SC, D).T)
    a["ident"] = np.eye(P, dtype=np.float32)
    a["minus_half"] = np.full((P, NT), -0.5, np.float32)
    a["ones"] = np.ones((1, P), np.float32)
    a["head_rows"] = np.repeat(np.eye(HT, dtype=np.float32), DK, axis=0)

    def packed_attention(name, w, b, wo, bo):
        for i, part in enumerate("qkv"):
            a[f"{name}_w{part}"] = np.ascontiguousarray(w[i * D:(i + 1) * D].T)
            rows = b[i * D:(i + 1) * D]
            if part == "v":
                a[f"{name}_bv"] = rows.reshape(1, D)
            else:
                columns(f"{name}_b{part}", rows)
        a[f"{name}_wo"] = np.ascontiguousarray(wo.T)
        a[f"{name}_bo"] = bo.reshape(1, D)

    packed_attention("L0", inp["L0_xattn_W_qkv"], inp["L0_xattn_b_qkv"], inp["L0_xattn_W_o"], inp["L0_xattn_b_o"])
    a["L0_gamma"] = inp["L0_xattn_ln_gamma"]
    a["L0_beta"] = inp["L0_xattn_ln_beta"]
    a["ctx"] = inp["ctx_1024"]
    a["spread"] = np.repeat(np.eye(B * H, dtype=np.float32), DK, axis=1).reshape(B * H, B * KT, P)
    a["rank"] = np.tile(np.arange(E, 0, -1, dtype=np.float32), (P, 1))

    a["before"] = np.triu(np.ones((P, P), np.float32), 1)
    a["every"] = np.ones((P, P), np.float32)
    a["sizes"] = np.tile(np.arange(NT * P // BS, dtype=np.float32) * BS, (P, E, 1))
    a["behind"] = np.tile(np.tril(np.ones((E, E), np.float32), -1), (P, 1, 1))
    a["number"] = np.tile(np.arange(NB, dtype=np.float32)[:, None], (P, 1, E))

    def norm(name, g, b):
        columns(name + "_g", inp[g])
        columns(name + "_b", inp[b])

    def feed_forward(name, w1, b1, w2, b2):
        a[name + "_w1"], a[name + "_w2"] = np.ascontiguousarray(w1), np.ascontiguousarray(w2)
        a[name + "_b1"] = np.ascontiguousarray(b1.reshape(-1, FT, P).transpose(0, 2, 1))
        a[name + "_b2"] = b2.reshape(-1, D)

    L = "L1_xattn_"
    norm("L1_n1", L + "sa_ln_g", L + "sa_ln_b")
    norm("L1_n2", L + "ca_q_ln_g", L + "ca_q_ln_b")
    norm("L1_nc", L + "ca_kv_ln_g", L + "ca_kv_ln_b")
    norm("L1_n3", L + "moe_ln_g", L + "moe_ln_b")
    packed_attention("L1sa", *(inp[L + n] for n in ("sa_in_w", "sa_in_b", "sa_out_w", "sa_out_b")))
    packed_attention("L1ca", *(inp[L + n] for n in ("ca_in_w", "ca_in_b", "ca_out_w", "ca_out_b")))
    a["L1_wr"] = np.ascontiguousarray(inp[L + "router_w"].T)
    a["L1_br"] = inp[L + "router_b"].reshape(E, 1)
    feed_forward("L1", inp[L + "e_fc1_w"].transpose(0, 2, 1), inp[L + "e_fc1_b"], inp[L + "e_fc2_w"].transpose(0, 2, 1),
                 inp[L + "e_fc2_b"])

    L = "L2_xattn_"
    norm("L2_e1", L + "enc_n1_s", L + "enc_n1_b")
    norm("L2_e2", L + "enc_n2_s", L + "enc_n2_b")
    for i in "123":
        norm("L2_n" + i, L + f"dec_n{i}_s", L + f"dec_n{i}_b")
    packed_attention("L2e", *(inp[L + n] for n in ("enc_in_w", "enc_in_b", "enc_out_w", "enc_out_b")))
    packed_attention("L2sa", *(inp[L + n] for n in ("dec_sa_in_w", "dec_sa_in_b", "dec_sa_out_w", "dec_sa_out_b")))
    packed_attention("L2ca", *(inp[L + n] for n in ("dec_ca_in_w", "dec_ca_in_b", "dec_ca_out_w", "dec_ca_out_b")))
    for name, part in (("L2e", "enc"), ("L2", "dec")):
        feed_forward(name, inp[L + part + "_ff1_w"].T[None], inp[L + part + "_ff1_b"],
                     inp[L + part + "_ff2_w"].T[None], inp[L + part + "_ff2_b"])

    def rows_of(queries, keys):
        ahead = keys - queries
        return np.where(ahead < 0, np.minimum(-ahead, P - 1), np.minimum(ahead, P - 1) + P)

    def laid(table, queries, keys):
        return np.ascontiguousarray(table[rows_of(queries, keys)].transpose(0, 2, 1))

    at, to, near = np.arange(P)[:, None], np.arange(SC)[None, :], np.arange(2 * P)[None, :]
    a["L2_enc_bias"] = laid(inp[L + "enc_rel"], at[0:SC], to).reshape(SC, 1, H * SC)
    a["L2_cross_bias"] = np.ascontiguousarray(np.stack(
        [laid(inp[L + "dec_rel_cross"], at + P * j, to).reshape(P, H * SC) for j in range(3)], axis=1))
    rel = inp[L + "dec_rel_self"][:, list(range(H)) + [0]]
    a["L2_rel_q"] = laid(rel, at + P, near)
    a["L2_rel_k"] = laid(rel, near, at)
    a["L2_rel_far"] = np.ascontiguousarray(rel[P - 1])
    a["near_mask_q"] = np.where(near > at + P, MASKED, 0.0).astype(np.float32)
    a["near_mask_k"] = np.where(at > near, MASKED, 0.0).astype(np.float32)

    L = "L3_xattn_"
    for i in "123":
        norm("L3_n" + i, L + f"ln{i}_g", L + f"ln{i}_b")
    swap = (np.arange(D) // DK) * DK + (np.arange(D) % DK + DK // 2) % DK
    for part in ("sa", "ca"):
        for w in "qk":
            weight, bias = inp[L + f"{part}_w{w}"], inp[L + f"{part}_b{w}"]
            a[f"L3{part}_w{w}"] = weight
            a[f"L3{part}_w{w}_turned"] = np.ascontiguousarray(weight[:, swap])
            columns(f"L3{part}_b{w}", bias)
            columns(f"L3{part}_b{w}_turned", bias[swap])
        a[f"L3{part}_wv"], a[f"L3{part}_bv"] = inp[L + part + "_wv"], inp[L + part + "_bv"].reshape(1, D)
        a[f"L3{part}_wo"], a[f"L3{part}_bo"] = inp[L + part + "_wo"], inp[L + part + "_bo"].reshape(1, D)
    frequency = np.float32(1.0) / np.float32(10000.0) ** (np.arange(0, DK, 2, dtype=np.float32) / np.float32(DK))
    angle = np.outer(np.arange(SQ, dtype=np.float32), frequency).astype(np.float32)
    cos = np.tile(np.cos(angle).T, (2 * HT, 1)).astype(np.float32)
    sin = np.tile(np.concatenate([-np.sin(angle), np.sin(angle)], axis=1).T, (HT, 1)).astype(np.float32)
    a["turn_k_cos"], a["turn_k_sin"] = cos, sin
    a["turn_q_cos"], a["turn_q_sin"] = cos * np.float32(SCALE), sin * np.float32(SCALE)
    feed_forward("L3", inp[L + "fc1_w"][None], inp[L + "fc1_b"], inp[L + "fc2_w"][None], inp[L + "fc2_b"])
    a["columns"] = np.ascontiguousarray(np.concatenate(packed, axis=1))
    return a, places


def kernel(**inputs):
    import concourse.bacc as bacc
    from concourse.bass_utils import run_bass_kernel_spmd

    nc = bacc.Bacc("TRN2", target_bir_lowering=False, num_devices=1)
    arrays, places = lay_out({k: np.asarray(v) for k, v in inputs.items()})
    d = {}
    for name, a in arrays.items():
        d[name] = nc.dram_tensor("in_" + name, a.shape, mybir.dt.from_np(a.dtype), kind="ExternalInput").ap()
    out = nc.dram_tensor("out", (B, SQ, D), F32, kind="ExternalOutput").ap()
    build(nc, d, places, out)
    r = run_bass_kernel_spmd(nc, [{"in_" + k: v for k, v in arrays.items()}], core_ids=[0])
    return r.results[0]["out"]
```

```python
from contextlib import ExitStack

import numpy as np
import concourse.bass as bass
from concourse import mybir

F32 = mybir.dt.float32
BF16 = mybir.dt.bfloat16
F16 = mybir.dt.float16
U32 = mybir.dt.uint32
I32 = mybir.dt.int32
ALU = mybir.AluOpType
ACT = mybir.ActivationFunctionType
AX = mybir.AxisListType

P = 128
D = 256
KT = D // P
H = 16
DK = D // H
HT = P // DK
B = 4
SQ = 1024
SC = 64
NT = B * SQ // P
TB = SQ // P
FF = 1024
FT = FF // P
E = 8
CH = 512
BS = 256
NB = 2 * NT * P // BS + E
SCALE = DK ** -0.5
PIECES = 6
KS = PIECES * DK
Q_PART = (0, 0, 0, 1, 1, 2)
K_PART = (0, 1, 2, 0, 1, 0)
VW = 3 * DK + 1
PW = 2 * (DK + 1)
NEG = -3.0e38
MASKED = -1.0e30
ZERO = 1376


class Signal:

    def __init__(self, sem):
        self.sem, self.base, self.total = sem, 0, 0

    def at(self, n):
        return self.base + n


class Signals:

    def __init__(self, nc, ctx):
        self.nc, self.ctx, self.known = nc, ctx, {}

    def __call__(self, name, total):
        if name not in self.known:
            self.known[name] = Signal(self.ctx.enter_context(self.nc.semaphore(name)))
        s = self.known[name]
        assert s.total == 0, name
        s.total = total
        return s

    def phase_over(self):
        for s in self.known.values():
            s.base, s.total = s.base + s.total, 0


class Phase:

    def __init__(self, nc, signals, name):
        self.nc, self.signals, self.name = nc, signals, name
        self.ctx = ExitStack()

    def __enter__(self):
        return self

    def __exit__(self, *a):
        self.ctx.close()
        self.signals.phase_over()
        return False

    def sb(self, name, shape, dt=F32):
        return self.ctx.enter_context(self.nc.sbuf_tensor(f"{self.name}_{name}", shape, dt))

    def ps(self, name, shape, dt=F32):
        return self.ctx.enter_context(self.nc.psum_tensor(f"{self.name}_{name}", shape, dt))

    def sig(self, name, total):
        return self.signals(name, total)


def load_all(eng, pairs, loaded):
    for dst, src in pairs:
        eng.dma_start(dst, src).then_inc(loaded.sem, 16)


MOMENT_STEPS = 6
GROUP = 8
QUAD = 4


class Statistics:

    def __init__(self, ph, x, rows, tiles, eps, minus_half, moments=None):
        self.x, self.rows, self.eps, self.minus_half = x, rows, eps, minus_half
        self.group = min(GROUP, tiles)
        self.groups = tiles // self.group
        self.raw = ph.sb("raw", [P, tiles, 6])
        self.mean = moments[0] if moments else ph.sb("mean", [P, tiles])
        self.spread = ph.sb("spread", [P, tiles])
        self.rstd = moments[1] if moments else ph.sb("rstd", [P, tiles])
        self.stats_done = ph.sig("stats_done", self.groups)
        self.moments_step = ph.sig("moments_step", MOMENT_STEPS * self.groups)
        self.rstd_done = ph.sig("rstd_done", 2 * self.groups)

    def columns(self, tensor, q):
        return tensor[0:self.rows, bass.ds(q * self.group, self.group)]

    def on_vector(self, eng, q):
        rows, step, s = self.rows, self.moments_step, q * MOMENT_STEPS
        for i in range(self.group):
            t = q * self.group + i
            op = eng.bn_stats(self.raw[0:rows, bass.ds(t, 1), :].rearrange("p t c -> p (t c)"), self.x[0:rows, t, :])
        op.then_inc(self.stats_done.sem, 1)
        mean_e, sq_e, mean_o, sq_o = (self.raw[0:rows, bass.ds(q * self.group, self.group), c] for c in (1, 2, 4, 5))
        mean, spread = self.columns(self.mean, q), self.columns(self.spread, q)
        eng.wait_ge(self.stats_done.sem, self.stats_done.at(q + 1))
        eng.tensor_tensor(mean, mean_e, mean_o, ALU.add).then_inc(step.sem, 1)
        eng.tensor_tensor(spread, mean_e, mean_o, ALU.subtract).then_inc(step.sem, 1)
        eng.wait_ge(step.sem, step.at(s + 2))
        eng.tensor_scalar(mean, mean, 0.5, None, ALU.mult).then_inc(step.sem, 1)
        eng.scalar_tensor_tensor(spread, spread, D / 4.0, spread, ALU.mult, ALU.mult).then_inc(step.sem, 1)
        eng.wait_ge(step.sem, step.at(s + 4))
        eng.tensor_tensor(spread, spread, sq_e, ALU.add).then_inc(step.sem, 1)
        eng.wait_ge(step.sem, step.at(s + 5))
        eng.tensor_tensor(spread, spread, sq_o, ALU.add).then_inc(step.sem, 1)

    def on_gpsimd(self, eng):
        for q in range(self.groups):
            rstd = self.columns(self.rstd, q)
            eng.wait_ge(self.moments_step.sem, self.moments_step.at(q * MOMENT_STEPS + MOMENT_STEPS))
            eng.tensor_scalar(rstd, self.columns(self.spread, q), 1.0 / D, self.eps, ALU.mult, ALU.add)\
               .then_inc(self.rstd_done.sem, 1)
            eng.wait_ge(self.rstd_done.sem, self.rstd_done.at(q * 2 + 1))
            eng.tensor_tensor(rstd, rstd, self.minus_half[0:self.rows, 0:self.group], ALU.pow)\
               .then_inc(self.rstd_done.sem, 1)

    def each_group(self, eng, use):
        def ready(q):
            eng.wait_ge(self.rstd_done.sem, self.rstd_done.at(q * 2 + 2))
            use(q)

        self.on_vector(eng, 0)
        if self.groups > 1:
            with eng.Fori(0, self.groups - 1) as q:
                self.on_vector(eng, q + 1)
                ready(q)
        ready(self.groups - 1)


def transpose_phase(nc, signals, name, x, hT, consts, rows, tiles, cols=None, eps=1e-5, moments=None):
    ident = consts["ident"]
    G = min(GROUP, tiles)
    groups = tiles // G
    QG = G // QUAD
    with Phase(nc, signals, name) as ph:
        norm = cols is not None
        nrm = [ph.sb(f"nrm{i}", [P, D]) for i in range(G)]
        psT = [[ph.ps(f"psT{u}{k}", [P, 512]) for k in range(KT)] for u in range(2)]
        stats = Statistics(ph, x, rows, tiles, eps, consts["minus_half"], moments) if norm else None
        ready = ph.sig("normalized", tiles)
        turned = ph.sig("transposed", QG + tiles // QUAD)
        stored = ph.sig("transpose_stored", 2 + tiles // QUAD)

        def each_group(eng, body):
            if groups == 1:
                body(0)
            else:
                with eng.Fori(0, groups) as q:
                    body(q)

        with nc.Block() as block:
            if norm:
                @block.gpsimd
                def _(eng):
                    stats.on_gpsimd(eng)

            @block.vector
            def _(eng):
                def normalize(q):
                    for i in range(G):
                        if i % QUAD == 0:
                            eng.wait_ge(turned.sem, turned.at(q * QG + (i // QUAD + 1)))
                        t = q * G + i
                        if norm:
                            eng.tensor_scalar(nrm[i][0:rows, :], x[0:rows, t, :],
                                              stats.mean[0:rows, bass.ds(t, 1)], stats.rstd[0:rows, bass.ds(t, 1)],
                                              ALU.subtract, ALU.mult).then_inc(ready.sem, 1)
                        else:
                            eng.tensor_copy(nrm[i][0:rows, :], x[0:rows, t, :]).then_inc(ready.sem, 1)

                if norm:
                    stats.each_group(eng, normalize)
                else:
                    each_group(eng, normalize)

            @block.tensor
            def _(eng):
                eng.sem_inc(turned.sem, QG)
                def body(q):
                    for i in range(G):
                        if i % QUAD == 0:
                            eng.wait_ge(stored.sem, stored.at(q * QG + (i // QUAD + 1)))
                        eng.wait_ge(ready.sem, ready.at(q * G + (i + 1)))
                        for k in range(KT):
                            at = (i % QUAD) * rows
                            mm = eng.transpose(psT[i // QUAD][k][:, at:at + rows], nrm[i][0:rows, k * P:(k + 1) * P],
                                               ident[0:rows, 0:rows])
                        if i % QUAD == QUAD - 1:
                            mm.then_inc(turned.sem, 1)

                each_group(eng, body)

            @block.scalar
            def _(eng):
                eng.sem_inc(stored.sem, 2)
                def body(q):
                    for u in range(QG):
                        eng.wait_ge(turned.sem, turned.at(q * QG + (u + 1 + QG)))
                        for k in range(KT):
                            dst = hT[:, k, bass.ds((q * QG + u) * (QUAD * rows), QUAD * rows)]
                            if norm:
                                act = eng.activation(dst, psT[u][k][:, 0:QUAD * rows], ACT.Identity,
                                                     bias=cols[1][:, k:k + 1], scale=cols[0][:, k:k + 1])
                            else:
                                act = eng.activation(dst, psT[u][k][:, 0:QUAD * rows], ACT.Copy)
                        act.then_inc(stored.sem, 1)

                each_group(eng, body)


def output_norm_phase(nc, signals, name, x, consts, gain_row, shift_row, eps):
    with Phase(nc, signals, name) as ph:
        stats = Statistics(ph, x, P, NT, eps, consts["minus_half"])
        gain = ph.sb("gain", [P, D])
        shift = ph.sb("shift", [P, D])
        loaded = ph.sig("weights_loaded", 32)
        centered = ph.sig("centered", NT)
        with nc.Block() as block:
            @block.sync
            def _(eng):
                eng.dma_start(gain[:], gain_row.partition_broadcast(P)).then_inc(loaded.sem, 16)
                eng.dma_start(shift[:], shift_row.partition_broadcast(P)).then_inc(loaded.sem, 16)

            @block.gpsimd
            def _(eng):
                stats.on_gpsimd(eng)

            @block.vector
            def _(eng):
                eng.wait_ge(loaded.sem, loaded.at(32))

                def scale(q):
                    for i in range(GROUP):
                        xt = x[:, q * GROUP + i, :]
                        eng.scalar_tensor_tensor(xt, xt, stats.mean[:, bass.ds(q * GROUP + i, 1)], gain[:],
                                                 ALU.subtract, ALU.mult).then_inc(centered.sem, 1)
                    for i in range(GROUP):
                        xt = x[:, q * GROUP + i, :]
                        eng.wait_ge(centered.sem, centered.at(q * GROUP + (i + 1)))
                        eng.scalar_tensor_tensor(xt, xt, stats.rstd[:, bass.ds(q * GROUP + i, 1)], shift[:],
                                                 ALU.mult, ALU.add)

                stats.each_group(eng, scale)


def context_heads_phase(nc, signals, name, sT, w_k, w_v, b_k, b_v, consts, Kbd, Vbd, rope=None):
    n_k = KT * (2 if rope else 1)
    with Phase(nc, signals, name) as ph:
        wk = ph.sb("wk", [P, KT, D])
        wk2 = ph.sb("wk2", [P, KT, D]) if rope else None
        wv = ph.sb("wv", [P, KT, D])
        bv = ph.sb("bv", [1, D])
        sT2 = ph.sb("sT2", [P, KT, B, 2, SC])
        kT = [ph.sb(f"kT{t}", [P, B, SC]) for t in range(KT)]
        kS = [ph.sb(f"kS{t}", [P, B, SC]) for t in range(KT)] if rope else None
        psK = [ph.ps(f"psK{i}", [P, B * SC]) for i in range(n_k)]
        psV = [ph.ps(f"psV{b}", [P, D]) for b in range(B)]
        loaded = ph.sig("weights_loaded", 16 * (4 if rope else 3))
        doubled = ph.sig("context_doubled", 1)
        cleared = ph.sig("cleared", 1)
        k_ready = ph.sig("keys_in_psum", 1)
        v_ready = ph.sig("values_in_psum", 1)
        kT_ready = ph.sig("keys_biased", KT)
        turned = ph.sig("keys_turned", 2 * KT)
        with nc.Block() as block:
            @block.sync
            def _(eng):
                eng.dma_start(wk[:], w_k[0]).then_inc(loaded.sem, 16)
                if rope:
                    eng.dma_start(wk2[:], w_k[1]).then_inc(loaded.sem, 16)
                eng.dma_start(wv[:], w_v).then_inc(loaded.sem, 16)
                eng.dma_start(bv[:], b_v).then_inc(loaded.sem, 16)

            @block.gpsimd
            def _(eng):
                src = sT[:, :, :].rearrange("p k (b c) -> p (k b) c", c=SC)
                for s in range(2):
                    op = eng.tensor_copy(sT2[:, :, :, s, :].rearrange("p k b c -> p (k b) c"), src)
                op.then_inc(doubled.sem, 1)

            @block.tensor
            def _(eng):
                eng.wait_ge(loaded.sem, loaded.at(loaded.total))
                for t in range(KT):
                    for r in range(2 if rope else 1):
                        for k in range(KT):
                            mm = eng.matmul(psK[r * KT + t][:], (wk2 if r else wk)[:, k, t * P:(t + 1) * P],
                                            sT[:, k, :], start=(k == 0), stop=(k == KT - 1))
                mm.then_inc(k_ready.sem, 1)
                eng.wait_ge(doubled.sem, doubled.at(1))
                for b in range(B):
                    eng.matmul(psV[b][:], consts["ones"][0:1, 0:P], bv[:], start=True, stop=False)
                    for k in range(KT):
                        mm = eng.matmul(psV[b][:], sT2[:, k, b, :, :].rearrange("p s c -> p (s c)"),
                                        wv[:, k, :], start=False, stop=(k == KT - 1))
                mm.then_inc(v_ready.sem, 1)

            @block.scalar
            def _(eng):
                eng.wait_ge(k_ready.sem, k_ready.at(1))
                if not rope:
                    for t in range(KT):
                        eng.activation(kT[t][:].rearrange("p b c -> p (b c)"), psK[t][:], ACT.Identity,
                                       bias=b_k[0][:, t:t + 1], scale=1.0).then_inc(kT_ready.sem, 1)
                eng.wait_ge(v_ready.sem, v_ready.at(1))
                eng.wait_ge(cleared.sem, cleared.at(1))
                for b in range(B):
                    for s in range(2):
                        rows = slice(s * SC, (s + 1) * SC)
                        src = psV[b][rows, :].rearrange("p (j s d) -> p j s d", s=2, d=DK)[:, :, s, :]
                        eng.activation(Vbd[rows, b, :, s * (DK + 1):s * (DK + 1) + DK], src, ACT.Copy)

            @block.vector
            def _(eng):
                eng.memset(Vbd[:], 0.0).then_inc(turned.sem, 1)
                eng.wait_ge(turned.sem, turned.at(1))
                eng.memset(Vbd[0:SC, :, :, DK:DK + 1], 1.0)
                eng.memset(Vbd[SC:P, :, :, PW - 1:PW], 1.0).then_inc(cleared.sem, 1)
                if rope:
                    cos, sin = rope
                    eng.wait_ge(k_ready.sem, k_ready.at(1))
                    for t in range(KT):
                        for b in range(B):
                            cols = slice(b * SC, (b + 1) * SC)
                            eng.scalar_tensor_tensor(kT[t][:, b, :], psK[t][:, cols], b_k[0][:, t:t + 1],
                                                     cos[:, 0:SC], ALU.add, ALU.mult)
                            op = eng.scalar_tensor_tensor(kS[t][:, b, :], psK[KT + t][:, cols],
                                                          b_k[1][:, t:t + 1], sin[:, 0:SC], ALU.add, ALU.mult)
                    op.then_inc(turned.sem, 1)
                    eng.wait_ge(turned.sem, turned.at(2))
                    for t in range(KT):
                        eng.tensor_tensor(kT[t][:], kT[t][:], kS[t][:], ALU.add).then_inc(kT_ready.sem, 1)
                else:
                    eng.sem_inc(turned.sem, 1)
                for t in range(KT):
                    eng.wait_ge(kT_ready.sem, kT_ready.at(t + 1))
                    for b in range(B):
                        op = eng.tensor_tensor(Kbd[:, b, t, :].rearrange("p (h c) -> p h c", c=SC),
                                               kT[t][:, b, :].unsqueeze(1).to_broadcast([P, HT, SC]),
                                               consts["head_rows"][:].unsqueeze(2).to_broadcast([P, HT, SC]),
                                               ALU.mult)
                    op.then_inc(turned.sem, 1)


def cross_attention_phase(nc, signals, name, hT, x, rows, tiles, w_q, b_q, w_o, b_o, Kbd, Vbd, consts,
                          bias=None, rope=None, meanwhile=None, on_gpsimd=None):
    chunks = max(1, tiles * rows // CH)
    tpc = tiles // chunks
    cw = tpc * rows
    n_r = 2 if rope else 1
    with Phase(nc, signals, name) as ph:
        wq = [ph.sb(f"wq{r}", [P, KT, D]) for r in range(n_r)]
        wo = ph.sb("wo", [P, KT, D])
        bo = ph.sb("bo", [P, D])
        bq_scaled = ph.sb("bq_scaled", [P, KT])
        table = ph.sb("table", [P, bias[1], H * SC]) if bias else None
        qT = [[ph.sb(f"qT{u}{t}", [P, CH]) for t in range(KT)] for u in range(2)]
        qS = ph.sb("qS", [P, CH]) if rope else None
        sc = [ph.sb(f"sc{u}", [P, H, SC]) for u in range(2)]
        top = [ph.sb(f"top{u}", [P, H]) for u in range(2)]
        pT = [ph.sb(f"pT{u}", [P, H // 2, P]) for u in range(2)]
        rden = [ph.sb(f"rden{u}", [P, H]) for u in range(2)]
        cx = [ph.sb(f"cx{u}", [P, D]) for u in range(2)]
        cT = [ph.sb(f"cT{u}", [P, KT, P]) for u in range(2)]
        psS = ph.ps("psS", [P, H, SC])
        psT = ph.ps("psT", [P, H // 4, P])
        psQ = [ph.ps(f"psQ{i}", [P, CH]) for i in range(2)]
        psO = ph.ps("psO", [P, 512])
        psC = ph.ps("psC", [P, KT, P])
        psY = ph.ps("psY", [P, 512])
        n = B * tiles
        n_load = 16 * (n_r + 2 + bool(bias))
        loaded = ph.sig("weights_loaded", n_load)
        scaled = ph.sig("bias_scaled", 1)
        q_psum = ph.sig("query_in_psum", B * chunks * KT)
        q_halves = ph.sig("query_halves", B * chunks * KT if rope else 0)
        q_ready = ph.sig("query_ready", B * chunks * KT)
        s_psum = ph.sig("scores_in_psum", n)
        s_biased = ph.sig("scores_biased", n if bias else 0)
        s_top = ph.sig("scores_top", n)
        s_less = ph.sig("scores_less_top", n)
        p_ready = ph.sig("probs_ready", n)
        p_psum = ph.sig("probs_transposed", 2 * n)
        p_turned = ph.sig("probs_turned", 2 * n)
        c_psum = ph.sig("context_in_psum", n)
        c_inv = ph.sig("context_inverse", n)
        c_ready = ph.sig("context_ready", n)
        ct_psum = ph.sig("context_transposed", n)
        ct_ready = ph.sig("context_turned", n)
        y_psum = ph.sig("output_in_psum", n)
        x_biased = ph.sig("bias_added", n)
        y_added = ph.sig("output_added", n)

        LAST = 4

        def each_step(eng, step):
            for b in range(B if tiles == 1 else 1):
                for s in range(tiles):
                    step(b, s)
            if tiles > 1:
                with eng.Fori(0, B - 1) as b:
                    for s in range(tiles):
                        step(b + 1, s)
            for s in range(LAST):
                step(B, s)

        def entered(b, s, back):
            if isinstance(b, int):
                t = b * tiles + s - back
                return (t, t % 2, t // tiles, t % tiles) if 0 <= t < n else None
            return b * tiles + (s - back), (s - back) % 2, b if s >= back else b - 1, (s - back) % tiles

        gpsimd_program = on_gpsimd(ph) if on_gpsimd else None

        def after(count):
            return not isinstance(count, int) or count > 0

        def chunk_due(b, s):
            for c in range(chunks):
                if s == max(0, c * tpc - 2) and entered(b, s, 0):
                    return c
            return None

        with nc.Block() as block:
            @block.sync
            def _(eng):
                for r in range(n_r):
                    eng.dma_start(wq[r][:], w_q[r]).then_inc(loaded.sem, 16)
                eng.dma_start(wo[:], w_o).then_inc(loaded.sem, 16)
                eng.dma_start(bo[:], b_o.partition_broadcast(P)).then_inc(loaded.sem, 16)
                if bias:
                    eng.dma_start(table[0:rows], bias[0]).then_inc(loaded.sem, 16)
                if meanwhile:
                    meanwhile(eng)

            @block.tensor
            def _(eng):
                def transpose_probs(t, u, half):
                    if after(t * 2 + half):
                        eng.wait_ge(p_turned.sem, p_turned.at(t * 2 + half))
                    for j in range(H // 4):
                        h = half * (H // 2) + 2 * j
                        mm = eng.transpose(psT[:, j, 0:rows],
                                           sc[u][0:rows, h:h + 2, :].rearrange("p h c -> p (h c)"),
                                           consts["ident"][0:rows, 0:rows])
                    mm.then_inc(p_psum.sem, 1)

                def step(b, s):
                    c = chunk_due(b, s)
                    if c is not None:
                        for k_out in range(KT):
                            q = b * (chunks * KT) + (c * KT + k_out)
                            q_read = q if rope else q - 1
                            if after(q_read):
                                eng.wait_ge(q_ready.sem, q_ready.at(q_read))
                            for r in range(n_r):
                                for k in range(KT):
                                    mm = eng.matmul(psQ[r if rope else k_out][:, 0:cw], wq[r][:, k, k_out * P:(k_out + 1) * P],
                                                    hT[:, k, bass.ds(b * (tiles * rows) + c * cw, cw)],
                                                    start=(k == 0), stop=(k == KT - 1))
                            mm.then_inc(q_psum.sem, 1)
                    if entered(b, s, 0):
                        t, _, batch, local = entered(b, s, 0)
                        c = local // tpc
                        eng.wait_ge(q_ready.sem, q_ready.at(batch * (chunks * KT) + (c + 1) * KT))
                        if after(t):
                            eng.wait_ge(s_less.sem, s_less.at(t))
                        for k in range(KT):
                            mm = eng.matmul(psS[0:rows, k * HT:(k + 1) * HT, :].rearrange("p h c -> p (h c)"),
                                            qT[c % 2][k][:, (local % tpc) * rows:(local % tpc + 1) * rows],
                                            Kbd[:, batch, k, :], start=True, stop=True)
                        mm.then_inc(s_psum.sem, 1)
                    if entered(b, s, 1):
                        t, u, _, _ = entered(b, s, 1)
                        eng.wait_ge(p_ready.sem, p_ready.at(t + 1))
                        transpose_probs(t, u, 0)
                    if entered(b, s, 2):
                        t, u, batch, _ = entered(b, s, 2)
                        eng.wait_ge(p_turned.sem, p_turned.at(t * 2 + 2))
                        if after(t):
                            eng.wait_ge(c_ready.sem, c_ready.at(t))
                        for j in range(H // 2):
                            mm = eng.matmul(psO[0:rows, j * PW:(j + 1) * PW], pT[u][:, j, 0:rows],
                                            Vbd[:, batch, j, :], start=True, stop=True)
                        mm.then_inc(c_psum.sem, 1)
                    if entered(b, s, 3):
                        t, u, _, _ = entered(b, s, 3)
                        eng.wait_ge(c_ready.sem, c_ready.at(t + 1))
                        if after(t):
                            eng.wait_ge(ct_ready.sem, ct_ready.at(t))
                        for k in range(KT):
                            mm = eng.transpose(psC[:, k, 0:rows], cx[u][0:rows, k * P:(k + 1) * P],
                                               consts["ident"][0:rows, 0:rows])
                        mm.then_inc(ct_psum.sem, 1)
                    if entered(b, s, 4):
                        t, u, _, _ = entered(b, s, 4)
                        eng.wait_ge(ct_ready.sem, ct_ready.at(t + 1))
                        if after(t):
                            eng.wait_ge(y_added.sem, y_added.at(t))
                        for k in range(KT):
                            mm = eng.matmul(psY[0:rows, 0:D], cT[u][:, k, 0:rows], wo[:, k, :],
                                            start=(k == 0), stop=(k == KT - 1))
                        mm.then_inc(y_psum.sem, 1)
                    if entered(b, s, 1):
                        t, u, _, _ = entered(b, s, 1)
                        transpose_probs(t, u, 1)

                eng.wait_ge(loaded.sem, loaded.at(n_load))
                each_step(eng, step)

            @block.scalar
            def _(eng):
                def turn_probs(t, u, half):
                    eng.wait_ge(p_psum.sem, p_psum.at(t * 2 + half + 1))
                    eng.activation(pT[u][:, half * 4:half * 4 + 4, 0:rows], psT[:, :, 0:rows], ACT.Copy)\
                       .then_inc(p_turned.sem, 1)

                eng.wait_ge(loaded.sem, loaded.at(n_load))
                if not rope:
                    eng.mul(bq_scaled[:], b_q[0], SCALE).then_inc(scaled.sem, 1)
                    eng.wait_ge(scaled.sem, scaled.at(1))

                def step(b, s):
                    c = chunk_due(b, s)
                    if c is not None and not rope:
                        for k in range(KT):
                            q = b * (chunks * KT) + (c * KT + k)
                            eng.wait_ge(q_psum.sem, q_psum.at(q + 1))
                            eng.activation(qT[c % 2][k][:, 0:cw], psQ[k][:, 0:cw], ACT.Identity,
                                           bias=bq_scaled[:, k:k + 1], scale=SCALE).then_inc(q_ready.sem, 1)
                    if entered(b, s, 1):
                        t, u, _, _ = entered(b, s, 1)
                        if after(t - 1):
                            eng.wait_ge(c_psum.sem, c_psum.at(t - 1))
                        turn_probs(t, u, 0)
                    if entered(b, s, 0):
                        t, u, _, _ = entered(b, s, 0)
                        eng.wait_ge(s_less.sem, s_less.at(t + 1))
                        eng.activation(sc[u][0:rows], sc[u][0:rows], ACT.Exp).then_inc(p_ready.sem, 1)
                    if entered(b, s, 3):
                        t, u, _, _ = entered(b, s, 3)
                        eng.wait_ge(ct_psum.sem, ct_psum.at(t + 1))
                        if after(t - 1):
                            eng.wait_ge(y_psum.sem, y_psum.at(t - 1))
                        eng.activation(cT[u][:, :, 0:rows], psC[:, :, 0:rows], ACT.Copy).then_inc(ct_ready.sem, 1)
                    if entered(b, s, 1):
                        t, u, _, _ = entered(b, s, 1)
                        turn_probs(t, u, 1)

                each_step(eng, step)

            @block.gpsimd
            def _(eng):
                eng.wait_ge(loaded.sem, loaded.at(n_load))
                with eng.Fori(0, n // 4) as quad:
                    for i in range(4):
                        xt = x[0:rows, quad * 4 + i, :]
                        eng.tensor_tensor(xt, xt, bo[0:rows, :], ALU.add).then_inc(x_biased.sem, 1)
                if gpsimd_program:
                    gpsimd_program(eng)

            @block.vector
            def _(eng):
                eng.wait_ge(loaded.sem, loaded.at(n_load))

                def step(b, s):
                    c = chunk_due(b, s)
                    if c is not None and rope:
                        cos, sin = rope
                        for k in range(KT):
                            q = b * (chunks * KT) + (c * KT + k)
                            eng.wait_ge(q_psum.sem, q_psum.at(q + 1))
                            eng.scalar_tensor_tensor(qT[c % 2][k][:, 0:cw], psQ[0][:, 0:cw], b_q[0][:, k:k + 1],
                                                     cos[:, c * cw:(c + 1) * cw], ALU.add, ALU.mult)
                            eng.scalar_tensor_tensor(qS[:, 0:cw], psQ[1][:, 0:cw], b_q[1][:, k:k + 1],
                                                     sin[:, c * cw:(c + 1) * cw], ALU.add, ALU.mult)\
                               .then_inc(q_halves.sem, 1)
                            eng.wait_ge(q_halves.sem, q_halves.at(q + 1))
                            eng.tensor_tensor(qT[c % 2][k][:, 0:cw], qT[c % 2][k][:, 0:cw], qS[:, 0:cw],
                                              ALU.add).then_inc(q_ready.sem, 1)
                            eng.wait_ge(q_ready.sem, q_ready.at(q + 1))
                    if entered(b, s, 0):
                        t, u, _, local = entered(b, s, 0)
                        eng.wait_ge(s_psum.sem, s_psum.at(t + 1))
                        if after(t - 1):
                            eng.wait_ge(p_psum.sem, p_psum.at((t - 1) * 2))
                        src = psS
                        if bias:
                            j = min(local, bias[1] - 1)
                            eng.tensor_tensor(sc[u][0:rows], psS[0:rows],
                                              table[0:rows, j, :].rearrange("p (h c) -> p h c", c=SC),
                                              ALU.add).then_inc(s_biased.sem, 1)
                            eng.wait_ge(s_biased.sem, s_biased.at(t + 1))
                            src = sc[u]
                        eng.tensor_reduce(top[u][0:rows], src[0:rows], AX.X, ALU.max).then_inc(s_top.sem, 1)
                        eng.wait_ge(s_top.sem, s_top.at(t + 1))
                        eng.tensor_tensor(sc[u][0:rows], src[0:rows],
                                          top[u][0:rows].unsqueeze(2).to_broadcast([rows, H, SC]),
                                          ALU.subtract).then_inc(s_less.sem, 1)
                    if entered(b, s, 2):
                        t, u, _, _ = entered(b, s, 2)
                        got = psO[0:rows, 0:H * (DK + 1)].rearrange("p (h d) -> p h d", d=DK + 1)
                        eng.wait_ge(c_psum.sem, c_psum.at(t + 1))
                        eng.reciprocal(rden[u][0:rows], got[:, :, DK]).then_inc(c_inv.sem, 1)
                        eng.wait_ge(c_inv.sem, c_inv.at(t + 1))
                        if after(t - 1):
                            eng.wait_ge(ct_psum.sem, ct_psum.at(t - 1))
                        eng.tensor_tensor(cx[u][0:rows].rearrange("p (h d) -> p h d", d=DK), got[:, :, 0:DK],
                                          rden[u][0:rows].unsqueeze(2).to_broadcast([rows, H, DK]),
                                          ALU.mult).then_inc(c_ready.sem, 1)
                    if entered(b, s, 4):
                        t, _, _, _ = entered(b, s, 4)
                        xt = x[0:rows, t, :]
                        eng.wait_ge(y_psum.sem, y_psum.at(t + 1))
                        eng.wait_ge(x_biased.sem, x_biased.at(t + 1))
                        eng.tensor_tensor(xt, xt, psY[0:rows, 0:D], ALU.add).then_inc(y_added.sem, 1)

                each_step(eng, step)


def self_heads_phase(nc, signals, name, hT, w_q, w_k, w_v, b_q, b_k, b_v, consts, Qd, Kd, Vd, rope=None):
    n_r = 2 if rope else 1
    ITEMS = []
    for half in range(2):
        ITEMS += [("qk", half, t, kind) for t in range(KT) for kind in range(2)]
        ITEMS += [("v", half, j, 0) for j in range(4)]
    n_qk, n_v = 8, 8
    index, seen = [], {"qk": 0, "v": 0}
    for item in ITEMS:
        index.append(seen[item[0]])
        seen[item[0]] += 1
    with Phase(nc, signals, name) as ph:
        w = [[ph.sb(f"w{kind}{r}", [P, KT, D]) for r in range(n_r)] for kind in range(2)]
        wv = ph.sb("wv", [P, KT, D])
        bv = ph.sb("bv", [1, D])
        Vst = ph.sb("Vst", [P, B * H, 3 * DK, TB], BF16)
        bq_scaled = ph.sb("bq_scaled", [P, KT])
        hS = [ph.sb(f"hS{u}", [P, KT, CH]) for u in range(2)]
        y = [ph.sb(f"y{u}", [P, CH]) for u in range(2)]
        y2 = [ph.sb(f"y2{u}", [P, CH]) for u in range(2)] if rope else None
        rest = [ph.sb(f"rest{u}", [P, CH]) for u in range(2)]
        piece = [ph.sb(f"piece{u}", [P, 3, CH], BF16) for u in range(4)]
        vrest = [ph.sb(f"vrest{u}", [P, H, DK]) for u in range(2)]
        psQ = [[ph.ps(f"psQ{u}{r}", [P, CH]) for r in range(n_r)] for u in range(2)]
        psV = [ph.ps(f"psV{u}", [P, 512]) for u in range(2)]
        n_load = 16 * (2 * n_r + 2)
        loaded = ph.sig("weights_loaded", n_load)
        scaled = ph.sig("bias_scaled", 1)
        staged = [ph.sig(f"chunk_staged{u}", 16 * B) for u in range(2)]
        qk_psum = ph.sig("projection_in_psum", n_qk * B)
        qk_read = ph.sig("projection_read", n_qk * B)
        y_ready = ph.sig("projection_ready", n_qk * B if rope else 0)
        high = ph.sig("high_ready", n_qk * B)
        rested = ph.sig("rest_ready", n_qk * B)
        mid = ph.sig("mid_ready", n_qk * B)
        low = ph.sig("low_ready", n_qk * B)
        written = [ph.sig(f"pieces_written{u}", 16 * n_qk * B // 4) for u in range(4)]
        v_written = ph.sig("values_written", 16 * B)
        v_psum = ph.sig("value_in_psum", n_v * B)
        v_high = ph.sig("value_high_ready", n_v * B)
        v_rest = ph.sig("value_rest_ready", n_v * B)
        v_mid = ph.sig("value_mid_ready", n_v * B)
        v_low = ph.sig("value_low_ready", n_v * B)

        def each_batch(eng, batch):
            batch(0)
            with eng.Fori(0, B - 1) as b:
                batch(b + 1)

        def wait_past(eng, s, count):
            if not isinstance(count, int) or count > 0:
                eng.wait_ge(s.sem, s.at(count))

        def vst(b, j, part):
            return Vst[:, bass.ds(b * H, H), part * DK:(part + 1) * DK, j]

        with nc.Block() as block:
            @block.sync
            def _(eng):
                for dst, src in ((w[0], w_q), (w[1], w_k)):
                    for r in range(n_r):
                        eng.dma_start(dst[r][:], src[r]).then_inc(loaded.sem, 16)
                eng.dma_start(wv[:], w_v).then_inc(loaded.sem, 16)
                eng.dma_start(bv[:], b_v).then_inc(loaded.sem, 16)

                def store_values(b):
                    heads = bass.ds(b * H, H)
                    eng.dma_start(Vd[heads].rearrange("g p c j -> p g (c j)"),
                                  Vst[:, heads].rearrange("p g c j -> p g (c j)")).then_inc(v_written.sem, 16)

                def batch(b):
                    for half in range(2):
                        wait_past(eng, v_psum, b * n_v - 4 * (1 - half) if not isinstance(b, int) else 0)
                        eng.dma_start(hS[half][:], hT[:, :, bass.ds(b * SQ + half * CH, CH)])\
                           .then_inc(staged[half].sem, 16)
                    if not isinstance(b, int):
                        eng.wait_ge(v_low.sem, v_low.at(b * n_v))
                        eng.wait_ge(v_mid.sem, v_mid.at(b * n_v))
                        store_values(b - 1)
                    for n, (what, half, t, kind) in enumerate(ITEMS):
                        if what == "qk":
                            g = b * n_qk + index[n]
                            eng.wait_ge(low.sem, low.at(g + 1))
                            eng.wait_ge(mid.sem, mid.at(g + 1))
                            eng.wait_ge(high.sem, high.at(g + 1))
                            dst = (Kd if kind else Qd)[:, bass.ds(b * D + t * P, P), half * CH:(half + 1) * CH]
                            eng.dma_start(dst.rearrange("r p c -> p r c"), piece[index[n] % 4][:])\
                               .then_inc(written[index[n] % 4].sem, 16)

                each_batch(eng, batch)
                eng.wait_ge(v_low.sem, v_low.at(B * n_v))
                store_values(B - 1)
                for s in written:
                    eng.wait_ge(s.sem, s.at(s.total))
                eng.wait_ge(v_written.sem, v_written.at(16 * B))

            @block.tensor
            def _(eng):
                eng.wait_ge(loaded.sem, loaded.at(n_load))
                def batch(b):
                    for n, (what, half, t, kind) in enumerate(ITEMS):
                        i = index[n]
                        if n % 8 == 0:
                            eng.wait_ge(staged[half].sem, staged[half].at(b * 16 + 16))
                        if what == "qk":
                            wait_past(eng, qk_read, b * n_qk + (i - 1))
                            for r in range(n_r):
                                for k in range(KT):
                                    mm = eng.matmul(psQ[i % 2][r][:], w[kind][r][:, k, t * P:(t + 1) * P],
                                                    hS[half][:, k, :], start=(k == 0), stop=(k == KT - 1))
                            mm.then_inc(qk_psum.sem, 1)
                        else:
                            wait_past(eng, v_rest, b * n_v + (i - 1))
                            eng.matmul(psV[i % 2][:, 0:D], consts["ones"][0:1, 0:P], bv[:], start=True, stop=False)
                            for k in range(KT):
                                mm = eng.matmul(psV[i % 2][:, 0:D], hS[half][:, k, t * P:(t + 1) * P], wv[:, k, :],
                                                start=False, stop=(k == KT - 1))
                            mm.then_inc(v_psum.sem, 1)

                each_batch(eng, batch)

            @block.scalar
            def _(eng):
                if not rope:
                    eng.mul(bq_scaled[:], b_q[0], SCALE).then_inc(scaled.sem, 1)
                    eng.wait_ge(scaled.sem, scaled.at(1))
                def batch(b):
                    for n in range(len(ITEMS) + 1):
                        if n < len(ITEMS):
                            what, half, t, kind = ITEMS[n]
                            i = index[n]
                            if what == "qk" and not rope:
                                eng.wait_ge(qk_psum.sem, qk_psum.at(b * n_qk + (i + 1)))
                                wait_past(eng, rested, b * n_qk + (i - 1))
                                bias = (b_k[0] if kind else bq_scaled)[:, t:t + 1]
                                eng.activation(y[i % 2][:], psQ[i % 2][0][:], ACT.Identity, bias=bias,
                                               scale=1.0 if kind else SCALE).then_inc(qk_read.sem, 1)
                            if what == "v":
                                eng.wait_ge(v_psum.sem, v_psum.at(b * n_v + (i + 1)))
                                src = psV[i % 2][:, 0:D].rearrange("p (h d) -> p h d", d=DK)
                                eng.activation(vst(b, i, 0), src, ACT.Copy).then_inc(v_high.sem, 1)
                        if n >= 1:
                            what, half, t, kind = ITEMS[n - 1]
                            i = index[n - 1]
                            if what == "qk":
                                eng.wait_ge(rested.sem, rested.at(b * n_qk + (i + 1)))
                                wait_past(eng, written[i % 4], b * (4 * n_qk) + 16 * (i // 4))
                                eng.activation(piece[i % 4][:, 1, :], rest[i % 2][:], ACT.Copy).then_inc(mid.sem, 1)
                            else:
                                eng.wait_ge(v_rest.sem, v_rest.at(b * n_v + (i + 1)))
                                eng.activation(vst(b, i, 1), vrest[i % 2][:], ACT.Copy).then_inc(v_mid.sem, 1)

                each_batch(eng, batch)

            @block.vector
            def _(eng):
                def batch(b):
                    for n, (what, half, t, kind) in enumerate(ITEMS):
                        i = index[n]
                        u = i % 2
                        if what == "qk":
                            g = b * n_qk + i
                            if rope:
                                cos, sin = rope[kind]
                                bias = b_k if kind else b_q
                                cs = slice(half * CH, (half + 1) * CH)
                                eng.wait_ge(qk_psum.sem, qk_psum.at(g + 1))
                                wait_past(eng, y_ready, b * n_qk + (i - 1))
                                eng.scalar_tensor_tensor(y[u][:], psQ[u][0][:], bias[0][:, t:t + 1], cos[:, cs],
                                                         ALU.add, ALU.mult)
                                eng.scalar_tensor_tensor(y2[u][:], psQ[u][1][:], bias[1][:, t:t + 1], sin[:, cs],
                                                         ALU.add, ALU.mult).then_inc(qk_read.sem, 1)
                                eng.wait_ge(y_ready.sem, y_ready.at(g + 1))
                            else:
                                eng.wait_ge(qk_read.sem, qk_read.at(g + 1))
                            wait_past(eng, written[i % 4], b * (4 * n_qk) + 16 * (i // 4))
                            wait_past(eng, low, b * n_qk + (i - 1))
                            eng.tensor_copy(piece[i % 4][:, 0, :], y[u][:]).then_inc(high.sem, 1)
                            eng.wait_ge(high.sem, high.at(g + 1))
                            eng.tensor_tensor(rest[u][:], y[u][:], piece[i % 4][:, 0, :], ALU.subtract)\
                               .then_inc(rested.sem, 1)
                        else:
                            eng.wait_ge(v_high.sem, v_high.at(b * n_v + (i + 1)))
                            wait_past(eng, v_low, b * n_v + (i - 1))
                            eng.tensor_tensor(vrest[u][:], psV[u][:, 0:D].rearrange("p (h d) -> p h d", d=DK),
                                              vst(b, i, 0), ALU.subtract).then_inc(v_rest.sem, 1)

                each_batch(eng, batch)

            @block.gpsimd
            def _(eng):
                def batch(b):
                    for n in range(len(ITEMS) + 1):
                        if n < len(ITEMS) and ITEMS[n][0] == "qk" and rope:
                            i = index[n]
                            eng.wait_ge(qk_read.sem, qk_read.at(b * n_qk + (i + 1)))
                            eng.tensor_tensor(y[i % 2][:], y[i % 2][:], y2[i % 2][:], ALU.add).then_inc(y_ready.sem, 1)
                        if n >= 1:
                            i = index[n - 1]
                            u = i % 2
                            if ITEMS[n - 1][0] == "qk":
                                eng.wait_ge(mid.sem, mid.at(b * n_qk + (i + 1)))
                                wait_past(eng, written[i % 4], b * (4 * n_qk) + 16 * (i // 4))
                                eng.tensor_tensor(piece[i % 4][:, 2, :], rest[u][:], piece[i % 4][:, 1, :], ALU.subtract)\
                                   .then_inc(low.sem, 1)
                            else:
                                eng.wait_ge(v_mid.sem, v_mid.at(b * n_v + (i + 1)))
                                eng.tensor_tensor(vst(b, i, 2), vrest[u][:], vst(b, i, 1), ALU.subtract)\
                                   .then_inc(v_low.sem, 1)

                each_batch(eng, batch)


def near_blocks(ph, q_rel, k_rel, far, mask_q, mask_k, q_near, k_near):
    HN = H + 1
    rel = ph.sb("rel", [P, HN, 2 * P])
    rest = ph.sb("rest", [P, HN, 2 * P])
    far_sb = ph.sb("far", [P, HN])
    mask = ph.sb("mask", [P, 2 * P])
    loaded = ph.sig("tables_loaded", 16 * 5)
    step = ph.sig("near_step", 10)
    done = 0

    def program(eng):
        def then(op):
            nonlocal done
            op.then_inc(step.sem, 1)
            done += 1
            eng.wait_ge(step.sem, step.at(done))

        far_b = far_sb[:].unsqueeze(2).to_broadcast([P, HN, 2 * P])
        mask_b = mask[:].unsqueeze(1).to_broadcast([P, HN, 2 * P])
        eng.dma_start(far_sb[:], far.partition_broadcast(P)).then_inc(loaded.sem, 16)
        for side, (table, causal) in enumerate(((q_rel, mask_q), (k_rel, mask_k))):
            eng.dma_start(rel[:], table).then_inc(loaded.sem, 16)
            eng.dma_start(mask[:], causal).then_inc(loaded.sem, 16)
            eng.wait_ge(loaded.sem, loaded.at(80 if side else 48))
            then(eng.tensor_tensor(rel[:], rel[:], far_b, ALU.subtract))
            then(eng.tensor_tensor(rel[:], rel[:], mask_b, ALU.add))
            then(eng.tensor_copy((k_near[0] if side else q_near)[:], rel[:]))
        for piece in range(2):
            then(eng.tensor_tensor(rest[:], (rest if piece else rel)[:], k_near[piece][:], ALU.subtract))
            then(eng.tensor_copy(k_near[piece + 1][:], rest[:]))

    return program


def self_attention_phase(nc, signals, name, Qd, Kd, Vd, Od, Dd, consts, causal, near=None):
    KB = SQ // P
    LOAD_AHEAD = 2
    RING = 4

    def max_units(qt):
        end = (qt + 1) * P if causal else SQ
        return [("A", qt, hf, min(CH, end - hf * CH)) for hf in range(2) if end > hf * CH]

    units = [m for qt in range(KB) for m in max_units(qt)]
    ON_VECTOR = (1, 4, 6) if causal else (1, 5)
    ON_POOL = tuple(kt for kt in range(KB) if kt not in ON_VECTOR)
    MAXIMA_AT = 5 if causal else 6
    steps = (2, 3, 2, 3, 2) if causal else (3, 2, 3, 3, 3, 2)
    plan = [[] for _ in range(KB)]
    queue = list(units)
    for s in range(MAXIMA_AT):
        plan[s] += queue[:steps[s]]
        queue = queue[steps[s]:]
    assert not queue
    plan[MAXIMA_AT] = [("M", 0), ("M", 1)]
    flat = [m for s in plan for m in s]
    NU = len(flat)
    assert NU % 2 == 0
    nA = len(units)

    def q_from(kt):
        return kt * P if causal else 0

    def banks(lo, hi):
        return [(max(lo, c * CH), min(hi, (c + 1) * CH)) for c in range(2) if min(hi, (c + 1) * CH) > max(lo, c * CH)]

    with Phase(nc, signals, name) as ph:
        Qs = [ph.sb(f"Qs{r}", [KS + 1, SQ], BF16) for r in range(RING)]
        Ks = [ph.sb(f"Ks{r}", [KS + 1, SQ], BF16) for r in range(RING)]
        Pf = [ph.sb(f"Pf{r}", [P, SQ]) for r in range(4)]
        Pl = [ph.sb(f"Pl{r}", [P, SQ], F16) for r in range(4)]
        Vs = [ph.sb(f"Vs{r}", [P, VW, TB], BF16) for r in range(RING)]
        oT = [ph.sb(f"oT{u}", [VW, SQ]) for u in range(2)]
        mxp = ph.sb("mxp", [P, KB, 2])
        mx = ph.sb("mx", [P, KB], BF16)
        psA = [ph.ps(f"psA{u}", [P, CH]) for u in range(2)]
        psB = [ph.ps(f"psB{u}", [P, SQ]) for u in range(2)]
        psO = ph.ps("psO", [P, SQ])
        HEADS = B * H
        padded = ph.sig("heads_padded", 48)
        cleared = ph.sig("cleared", 1)
        prep = ph.sig("prepared", 3)
        q_loaded = [ph.sig(f"head_loaded{r}", 16 * 13 * ((HEADS + LOAD_AHEAD - r + RING - 1) // RING)) for r in range(RING)]
        a_psum = ph.sig("unit_in_psum", nA + 2 + HEADS * NU)
        a_read = ph.sig("unit_read", 2 + nA + 2 + HEADS * NU)
        maxed = ph.sig("maxima_ready", HEADS + 1)
        b_psum = ph.sig("scores_in_psum", LOAD_AHEAD * KB + HEADS * KB)
        p_ready = ph.sig("probs_ready", 2 + HEADS * KB)
        l_vec = ph.sig("low_probs_vector", 1 + HEADS * len(ON_VECTOR))
        l_pool = ph.sig("low_probs_pool", 1 + HEADS * len(ON_POOL))
        o_read = ph.sig("context_read", 1 + HEADS + 1)
        o_written = [ph.sig(f"context_written{u}", 16 * u + 64 * (HEADS // 2 + 1)) for u in range(2)]
        pv_done = ph.sig("key_tile_used", 2 + 2 + HEADS * KB)

        def hi(t, lo, hi_):
            return Pf[t][:].bitcast(BF16).rearrange("p (q two) -> p q two", two=2)[:, lo:hi_, 1]

        def each_head(eng, body):
            with eng.Fori(0, B) as b:
                with eng.Fori(0, H // RING) as quarter:
                    hq = quarter * RING
                    for r in range(RING):
                        body(b * H + hq + r, hq + r, r)

        with nc.Block() as block:
            @block.sync
            def _(eng):
                def load(g, r):
                    for dst, src, parts in ((Qs, Qd, Q_PART), (Ks, Kd, K_PART)):
                        for n, part in enumerate(parts):
                            eng.dma_start(dst[r][n * DK:(n + 1) * DK, :], src[part, bass.ds(g * DK, DK), :])\
                               .then_inc(q_loaded[r].sem, 16)
                    eng.dma_start(Vs[r][:, 0:3 * DK, :], Vd[bass.ds(g, 1)].rearrange("g p c j -> (g p) c j"))\
                       .then_inc(q_loaded[r].sem, 16)

                def write_context(g, r):
                    for part in range(3):
                        eng.dma_start(Od[part, bass.ds(g * DK, DK), :], oT[r % 2][part * DK:(part + 1) * DK, :])\
                           .then_inc(o_written[r % 2].sem, 16)
                    eng.dma_start(Dd[bass.ds(g, 1), :], oT[r % 2][3 * DK:VW, :]).then_inc(o_written[r % 2].sem, 16)

                for dram in (Qd, Kd):
                    eng.dma_start(dram[:, B * D:B * D + LOAD_AHEAD * DK, :], dram[:, 0:LOAD_AHEAD * DK, :])\
                       .then_inc(padded.sem, 16)
                eng.dma_start(Vd[B * H:B * H + LOAD_AHEAD], Vd[0:LOAD_AHEAD]).then_inc(padded.sem, 16)
                for g in range(LOAD_AHEAD):
                    load(g, g)
                eng.wait_ge(padded.sem, padded.at(48))
                eng.wait_ge(cleared.sem, cleared.at(1))

                def body(g, h, r):
                    eng.wait_ge(o_read.sem, o_read.at(g + 1))
                    eng.wait_ge(b_psum.sem, b_psum.at(g * KB + (KB + 3)))
                    load(g + LOAD_AHEAD, (r + LOAD_AHEAD) % RING)
                    write_context(g, r)

                each_head(eng, body)
                for g in range(HEADS, HEADS + 2):
                    eng.wait_ge(o_read.sem, o_read.at(g + 1))
                    write_context(g, g % RING)
                for u in range(2):
                    eng.wait_ge(o_written[u].sem, o_written[u].at(o_written[u].total))
                for r in range(RING):
                    eng.wait_ge(q_loaded[r].sem, q_loaded[r].at(q_loaded[r].total))

            @block.tensor
            def _(eng):
                def unit(m, n, count, r_next, h_next):
                    bank = psA[n % 2]
                    eng.wait_ge(a_read.sem, a_read.at(count + 1))
                    if m[0] == "A":
                        _, qt, hf, width = m
                        add = []
                        if near:
                            q_near, _, wide, per_head = near
                            for blk in ((qt - 1, qt) if wide else (qt,)):
                                if blk >= 0 and hf * CH <= blk * P < hf * CH + width:
                                    add.append(blk)
                        mm = eng.matmul(bank[:, 0:width], Qs[r_next][0:KS, qt * P:(qt + 1) * P],
                                        Ks[r_next][0:KS, hf * CH:hf * CH + width], start=True, stop=not add)
                        for blk in add:
                            at = (blk - qt + 1) * P if wide else 0
                            src = q_near[:, bass.ds(h_next, 1), at:at + P].rearrange("p h c -> p (h c)") \
                                if per_head else q_near[:, at:at + P]
                            mm = eng.matmul(bank[:, blk * P - hf * CH:blk * P - hf * CH + P], consts["identb"][:],
                                            src, start=False, stop=(blk == add[-1]))
                    else:
                        for j in range(4):
                            q = m[1] * 4 + j
                            mm = eng.matmul(bank[0:1, j * P:(j + 1) * P], mx[:, q:q + 1], consts["identb"][:],
                                            start=True, stop=True)
                    mm.then_inc(a_psum.sem, 1)

                def values(g, r, kt, part):
                    v = (kt - 2) % KB
                    if part:
                        l_ready, tiles = (l_vec, ON_VECTOR) if v in ON_VECTOR else (l_pool, ON_POOL)
                        before = (0 if kt >= 2 else -len(tiles)) + tiles.index(v)
                        eng.wait_ge(l_ready.sem, l_ready.at(g * len(tiles) + (before + 2)))
                    elif kt == 2:
                        eng.wait_ge(o_read.sem, o_read.at(g + 2))
                    lhs = Vs[r if kt >= 2 else (r - 1) % RING][:, :, v]
                    for lo, up in banks(q_from(v), SQ):
                        src = Pl[v % 4][:, lo:up] if part else hi(v % 4, lo, up)
                        final = KB - 1 if (not causal or lo >= CH) else CH // P - 1
                        mm = eng.matmul(psO[0:VW, lo:up], lhs, src, start=(v == 0 and part == 0),
                                        stop=(v == final and part == 1))
                    if part:
                        mm.then_inc(pv_done.sem, 1)

                eng.sem_inc(b_psum.sem, LOAD_AHEAD * KB)
                eng.sem_inc(pv_done.sem, 2)
                eng.wait_ge(prep.sem, prep.at(3))
                eng.wait_ge(cleared.sem, cleared.at(1))
                for c in range(2):
                    eng.matmul(psO[0:VW, c * CH:(c + 1) * CH], Vs[RING - 1][:, :, KB - 1],
                               hi(KB // 2 - 1, c * CH, (c + 1) * CH), start=True, stop=(causal and c == 0))
                eng.wait_ge(q_loaded[0].sem, q_loaded[0].at(16 * 13))
                for n, m in enumerate(units):
                    unit(m, n, n, 0, 0)
                eng.wait_ge(maxed.sem, maxed.at(1))
                for n in range(2):
                    unit(("M", n), nA + n, nA + n, 0, 0)

                def body(g, h, r):
                    nxt = (r + 1) % RING
                    it = (g - r) if r < RING - 1 else (g + 1)
                    eng.wait_ge(q_loaded[nxt].sem,
                                q_loaded[nxt].at(it * (16 * 13 // RING) + 16 * 13))
                    n = 0
                    for kt in range(KB):
                        if kt == 0:
                            eng.wait_ge(a_read.sem, a_read.at(g * NU + (nA + 2 + 2)))
                        eng.wait_ge(p_ready.sem, p_ready.at(g * KB + (kt + 1)))
                        k_near, wide, per_head = (near[1], near[2], near[3]) if near else ([], False, False)
                        for lo, up in banks(q_from(kt), SQ):
                            near_end = (kt + 2) * P if wide else (kt + 1) * P
                            adds = banks(max(lo, kt * P), min(up, near_end)) if k_near else []
                            mm = eng.matmul(psB[kt % 2][:, lo:up], Ks[r][:, kt * P:(kt + 1) * P], Qs[r][:, lo:up],
                                            start=True, stop=not adds)
                            for lo2, up2 in adds:
                                for piece in k_near:
                                    at = lo2 - kt * P
                                    src = piece[:, bass.ds(h, 1), at:at + up2 - lo2].rearrange("p h c -> p (h c)") \
                                        if per_head else piece[:, at:at + up2 - lo2]
                                    mm = eng.matmul(psB[kt % 2][:, lo2:up2], consts["identb"][:], src,
                                                    start=False, stop=(piece is k_near[-1]))
                        mm.then_inc(b_psum.sem, 1)
                        todo = plan[kt] if kt < MAXIMA_AT else []
                        for at in range(3):
                            for m in todo[at:at + 1]:
                                unit(m, nA + 2 + n, g * NU + (nA + 2 + n), nxt, h + 1)
                                n += 1
                            if at < 2:
                                values(g, r, kt, at)
                        if kt == MAXIMA_AT:
                            eng.wait_ge(maxed.sem, maxed.at(g + 2))
                            for m in plan[kt]:
                                unit(m, nA + 2 + n, g * NU + (nA + 2 + n), nxt, h + 1)
                                n += 1

                each_head(eng, body)
                for kt in range(2):
                    eng.wait_ge(p_ready.sem, p_ready.at(HEADS * KB + (kt + 1)))
                    for part in range(2):
                        values(HEADS, 0, kt, part)

            @block.scalar
            def _(eng):
                eng.sem_inc(p_ready.sem, 2)
                eng.sem_inc(o_written[1].sem, 16)
                eng.sem_inc(o_read.sem, 1)
                eng.wait_ge(cleared.sem, cleared.at(1))

                def copy_context(g, r):
                    eng.wait_ge(pv_done.sem, pv_done.at(g * KB + 4))
                    u = (r + 1) % 2
                    eng.wait_ge(o_written[u].sem, o_written[u].at(g * 32 + (32 if r % 2 else 16)))
                    eng.activation(oT[u][:], psO[0:VW, :], ACT.Copy).then_inc(o_read.sem, 1)

                def shift_row(count, half, r_next):
                    eng.wait_ge(a_psum.sem, a_psum.at(count + 1))
                    eng.activation(Qs[r_next][KS:KS + 1, half * CH:(half + 1) * CH], psA[half][0:1, :], ACT.Copy)\
                       .then_inc(a_read.sem, 1)

                for half in range(2):
                    shift_row(nA + half, half, 0)

                def body(g, h, r):
                    for kt in range(KB):
                        if kt == 2:
                            copy_context(g, r)
                        eng.wait_ge(b_psum.sem, b_psum.at(g * KB + (kt + 1 + LOAD_AHEAD * KB)))
                        eng.wait_ge(pv_done.sem, pv_done.at(g * KB + (kt + 1)))
                        lo = q_from(kt)
                        eng.activation(Pf[kt % 4][:, lo:SQ], psB[kt % 2][:, lo:SQ], ACT.Exp).then_inc(p_ready.sem, 1)
                        if kt == MAXIMA_AT:
                            for half in range(2):
                                shift_row(g * NU + (nA + 2 + nA + half), half, (r + 1) % RING)

                each_head(eng, body)
                copy_context(HEADS, 0)

            def rests(eng, g, kt, done):
                eng.wait_ge(p_ready.sem, p_ready.at(g * KB + (kt + 3)))
                eng.wait_ge(pv_done.sem, pv_done.at(g * KB + (kt + 1)))
                lo = q_from(kt)
                eng.tensor_tensor(Pl[kt % 4][:, lo:SQ], Pf[kt % 4][:, lo:SQ], hi(kt % 4, lo, SQ),
                                  ALU.subtract).then_inc(done.sem, 1)

            @block.gpsimd
            def _(eng):
                for t in (2, 3):
                    eng.memset(Pf[t][:], 1.0)
                    eng.memset(Pl[t][:], 1.0)
                for u in range(2):
                    eng.memset(oT[u][:], 1.0)
                for r in range(RING - 1):
                    eng.memset(Vs[r][:, 3 * DK:VW, :], 1.0)
                eng.memset(Vs[RING - 1][:], 1.0).then_inc(cleared.sem, 1)
                eng.sem_inc(l_pool.sem, 1)

                def body(g, h, r):
                    for kt in ON_POOL:
                        rests(eng, g, kt, l_pool)

                each_head(eng, body)

            @block.vector
            def _(eng):
                for r in range(RING):
                    eng.memset(Ks[r][KS:KS + 1, :], 1.0)
                eng.memset(mxp[:], NEG).then_inc(prep.sem, 1)
                eng.wait_ge(prep.sem, prep.at(1))
                eng.sem_inc(a_read.sem, 2)
                eng.sem_inc(prep.sem, 2)
                eng.sem_inc(l_vec.sem, 1)

                def unit(m, n, count):
                    _, qt, hf, width = m
                    eng.wait_ge(a_psum.sem, a_psum.at(count + 1))
                    eng.tensor_reduce(mxp[:, qt, hf:hf + 1], psA[n % 2][:, 0:width], AX.X, ALU.max)\
                       .then_inc(a_read.sem, 1)

                def maxima(count, g_next):
                    eng.wait_ge(a_read.sem, a_read.at(count))
                    eng.tensor_reduce(mx[:], mxp[:], AX.X, ALU.max, negate=True).then_inc(maxed.sem, 1)
                    eng.wait_ge(maxed.sem, maxed.at(g_next + 1))

                for n, m in enumerate(units):
                    unit(m, n, n)
                maxima(nA + 2, 0)

                def body(g, h, r):
                    n = 0
                    for kt in range(KB):
                        if kt == MAXIMA_AT:
                            maxima(g * NU + (nA + 2 + nA + 2), g + 1)
                        else:
                            for m in plan[kt]:
                                unit(m, nA + 2 + n, g * NU + (nA + 2 + n))
                                n += 1
                        if kt in ON_VECTOR:
                            rests(eng, g, kt, l_vec)

                each_head(eng, body)


def output_phase(nc, signals, name, Od, Dd, x, w_o, b_o, consts):
    chunks = NT * P // CH
    TC = CH // P
    ROWS = H * DK
    with Phase(nc, signals, name) as ph:
        wo = ph.sb("wo", [P, KT, D])
        bo = ph.sb("bo", [P, D])
        den = ph.sb("den", [B * H, SQ])
        parts = [ph.sb(f"parts{u}", [P, 3, CH]) for u in range(4)]
        cT = [ph.sb(f"cT{u}", [P, CH]) for u in range(4)]
        psY = [ph.ps(f"psY{u}", [P, 512]) for u in range(4)]
        psR = [ph.ps(f"psR{u}", [P, CH]) for u in range(4)]
        loaded = ph.sig("weights_loaded", 32)
        den_loaded = ph.sig("denominators_loaded", 16)
        r_psum = ph.sig("inverse_spread", chunks * KT)
        n = chunks * KT
        parts_loaded = [ph.sig(f"context_loaded{u}", 16 * n // 4) for u in range(4)]
        added = ph.sig("pieces_added", n)
        inverse = ph.sig("denominators_inverse", 1)
        summed = ph.sig("pieces_summed", n)
        c_ready = ph.sig("context_ready", n)
        x_biased = ph.sig("bias_added", NT)
        y_psum = ph.sig("output_in_psum", NT)
        y_added = ph.sig("output_added", NT)

        with nc.Block() as block:
            @block.sync
            def _(eng):
                eng.dma_start(den[:], Dd[2:2 + B * H, :]).then_inc(den_loaded.sem, 16)
                eng.dma_start(wo[:], w_o).then_inc(loaded.sem, 16)
                eng.dma_start(bo[:], b_o.partition_broadcast(P)).then_inc(loaded.sem, 16)
                for i in range(n):
                    c, k = i // KT, i % KT
                    row = 2 * DK + (c // 2) * ROWS + k * P
                    if i >= 4:
                        eng.wait_ge(c_ready.sem, c_ready.at(i - 3))
                    eng.dma_start(parts[i % 4][:], Od[:, row:row + P, (c % 2) * CH:(c % 2 + 1) * CH]
                                  .rearrange("r p c -> p r c")).then_inc(parts_loaded[i % 4].sem, 16)

            @block.gpsimd
            def _(eng):
                eng.wait_ge(loaded.sem, loaded.at(32))
                for i in range(n):
                    eng.wait_ge(parts_loaded[i % 4].sem, parts_loaded[i % 4].at(16 * (i // 4) + 16))
                    eng.tensor_tensor(parts[i % 4][:, 1, :], parts[i % 4][:, 1, :], parts[i % 4][:, 2, :], ALU.add)\
                       .then_inc(added.sem, 1)
                    for t in range(i * 2, i * 2 + 2):
                        eng.tensor_tensor(x[:, t, :], x[:, t, :], bo[:], ALU.add).then_inc(x_biased.sem, 1)

            @block.tensor
            def _(eng):
                def spread_inverse(i):
                    c, k = i // KT, i % KT
                    if i >= 4:
                        eng.wait_ge(c_ready.sem, c_ready.at(i - 3))
                    eng.matmul(psR[i % 4][:], consts["spread"][:, (c // 2) * KT + k, :],
                               den[:, (c % 2) * CH:(c % 2 + 1) * CH], start=True, stop=True).then_inc(r_psum.sem, 1)

                eng.wait_ge(inverse.sem, inverse.at(1))
                for i in range(4):
                    spread_inverse(i)
                eng.wait_ge(loaded.sem, loaded.at(32))
                for c in range(chunks):
                    for j in range(TC):
                        t = c * TC + j
                        if j >= KT and c * KT + 4 + j - KT < n:
                            spread_inverse(c * KT + 4 + j - KT)
                        if t >= 4:
                            eng.wait_ge(y_added.sem, y_added.at(t - 3))
                        for k in range(KT):
                            i = c * KT + k
                            eng.wait_ge(c_ready.sem, c_ready.at(i + 1))
                            mm = eng.matmul(psY[t % 4][:, 0:D], cT[i % 4][:, j * P:(j + 1) * P], wo[:, k, :],
                                            start=(k == 0), stop=(k == KT - 1))
                        mm.then_inc(y_psum.sem, 1)

            @block.vector
            def _(eng):
                eng.wait_ge(den_loaded.sem, den_loaded.at(16))
                eng.reciprocal(den[:], den[:]).then_inc(inverse.sem, 1)
                for c in range(chunks + 1):
                    for k in range(KT):
                        i = c * KT + k
                        if c < chunks:
                            src = parts[i % 4]
                            eng.wait_ge(parts_loaded[i % 4].sem, parts_loaded[i % 4].at(16 * (i // 4) + 16))
                            eng.wait_ge(added.sem, added.at(i + 1))
                            eng.tensor_tensor(src[:, 0, :], src[:, 0, :], src[:, 1, :], ALU.add)\
                               .then_inc(summed.sem, 1)
                            eng.wait_ge(summed.sem, summed.at(i + 1))
                            eng.wait_ge(r_psum.sem, r_psum.at(i + 1))
                            if i >= 4:
                                eng.wait_ge(y_psum.sem, y_psum.at((c - 1) * TC))
                            eng.tensor_tensor(cT[i % 4][:], src[:, 0, :], psR[i % 4][:], ALU.mult)\
                               .then_inc(c_ready.sem, 1)
                        if c >= 1:
                            for t in range((c - 1) * TC + 2 * k, (c - 1) * TC + 2 * k + 2):
                                eng.wait_ge(y_psum.sem, y_psum.at(t + 1))
                                eng.wait_ge(x_biased.sem, x_biased.at(t + 1))
                                eng.tensor_tensor(x[:, t, :], x[:, t, :], psY[t % 4][:, 0:D], ALU.add)\
                                   .then_inc(y_added.sem, 1)


def router_phase(nc, signals, name, hT, gates, slots, block_expert, w_r, b_r, consts):
    chunks = NT * P // CH
    TIMES = NT * P // BS
    SCAN = 5
    assert 1 << SCAN == NT
    with Phase(nc, signals, name) as ph:
        wr = ph.sb("wr", [P, KT, E])
        br = ph.sb("br", [E, 1])
        lT = [ph.sb(f"lT{u}", [E, CH]) for u in range(2)]
        lg = ph.sb("logits", [P, NT, E])
        rank = ph.sb("rank", [P, E])
        one = [ph.sb(f"onehot{i}", [P, NT, E]) for i in range(2)]
        wt = ph.sb("weighted", [P, NT, E])
        m = [ph.sb(f"m{i}", [P, NT]) for i in range(5)]
        before = ph.sb("before", [P, P])
        every = ph.sb("every", [P, P])
        sizes = ph.sb("sizes", [P, E, TIMES])
        behind = ph.sb("behind", [P, E, E])
        number = ph.sb("number", [P, NB, E])
        chosen = ph.sb("chosen", [P, NT, E])
        seen = [ph.sb(f"seen{i}", [P, NT, E]) for i in range(2)]
        place = ph.sb("place", [P, NT, E])
        size_over = ph.sb("size_over", [P, E, TIMES])
        blocks_of = ph.sb("blocks_of", [P, E])
        earlier = ph.sb("earlier", [P, E, E])
        first = ph.sb("first", [P, E])
        last = ph.sb("last", [P, E])
        past = ph.sb("past", [P, NB, E])
        owner = ph.sb("owner", [P, NB])
        dest = ph.sb("dest", [P, 2, NT])
        psN = ph.ps("psN", [P, NT * E])
        psA = ph.ps("psA", [P, NT * E])
        psL = [ph.ps(f"psL{u}", [P, CH]) for u in range(2)]
        psT = [ph.ps(f"psT{u}", [P, 4, E]) for u in range(2)]
        n_load = 16 * 8
        loaded = ph.sig("weights_loaded", n_load)
        l_psum = ph.sig("logits_in_psum", chunks)
        l_ready = ph.sig("logits_biased", chunks)
        t_psum = ph.sig("logits_transposed", chunks)
        t_read = ph.sig("logits_read", chunks)
        step = ph.sig("gate_step", 14 + 2 * SCAN + 19)
        is_chosen = ph.sig("experts_chosen", 1)
        counted = ph.sig("chosen_counted", 1)
        exped = ph.sig("gate_exp", 1)
        with nc.Block() as block:
            @block.sync
            def _(eng):
                eng.dma_start(wr[:], w_r).then_inc(loaded.sem, 16)
                eng.dma_start(br[:], b_r).then_inc(loaded.sem, 16)
                eng.dma_start(rank[:], consts["rank"]).then_inc(loaded.sem, 16)
                for dst, src in ((before, "before"), (every, "every"), (sizes, "sizes"), (behind, "behind"),
                                 (number, "number")):
                    eng.dma_start(dst[:], consts[src]).then_inc(loaded.sem, 16)

            @block.tensor
            def _(eng):
                eng.wait_ge(loaded.sem, loaded.at(n_load))
                for c in range(chunks + 1):
                    if c < chunks:
                        if c >= 2:
                            eng.wait_ge(l_ready.sem, l_ready.at(c - 1))
                        for k in range(KT):
                            mm = eng.matmul(psL[c % 2][0:E, :], wr[:, k, :], hT[:, k, c * CH:(c + 1) * CH],
                                            start=(k == 0), stop=(k == KT - 1))
                        mm.then_inc(l_psum.sem, 1)
                    if c >= 1:
                        u = (c - 1) % 2
                        eng.wait_ge(l_ready.sem, l_ready.at(c))
                        if c >= 3:
                            eng.wait_ge(t_read.sem, t_read.at(c - 2))
                        for j in range(4):
                            mm = eng.transpose(psT[u][:, j, :], lT[u][:, j * P:(j + 1) * P], consts["ident"][0:E, 0:E])
                        mm.then_inc(t_psum.sem, 1)
                eng.wait_ge(is_chosen.sem, is_chosen.at(1))
                sel = chosen[:].rearrange("p t e -> p (t e)")
                eng.matmul(psN[:], before[:], sel, start=True, stop=True)
                eng.matmul(psA[:], every[:], sel, start=True, stop=True).then_inc(counted.sem, 1)

            @block.scalar
            def _(eng):
                eng.wait_ge(loaded.sem, loaded.at(n_load))
                for c in range(chunks):
                    eng.wait_ge(l_psum.sem, l_psum.at(c + 1))
                    if c >= 2:
                        eng.wait_ge(t_psum.sem, t_psum.at(c - 1))
                    eng.activation(lT[c % 2][:], psL[c % 2][0:E, :], ACT.Identity, bias=br[:], scale=1.0)\
                       .then_inc(l_ready.sem, 1)
                eng.wait_ge(step.sem, step.at(12))
                eng.activation(m[2][:], m[2][:], ACT.Exp).then_inc(exped.sem, 1)

            @block.vector
            def _(eng):
                for c in range(chunks):
                    eng.wait_ge(t_psum.sem, t_psum.at(c + 1))
                    eng.tensor_copy(lg[:, c * 4:(c + 1) * 4, :], psT[c % 2][:]).then_inc(t_read.sem, 1)
                eng.wait_ge(t_read.sem, t_read.at(chunks))
                eng.wait_ge(loaded.sem, loaded.at(n_load))
                ranks = rank[:].unsqueeze(1).to_broadcast([P, NT, E])

                def wide(v):
                    return v[:].unsqueeze(2).to_broadcast([P, NT, E])

                n = 0
                for i in range(2):
                    eng.tensor_reduce(m[i][:], lg[:], AX.X, ALU.max).then_inc(step.sem, 1)
                    eng.wait_ge(step.sem, step.at(n + 1))
                    eng.tensor_tensor(wt[:], lg[:], wide(m[i]), ALU.is_equal).then_inc(step.sem, 1)
                    eng.wait_ge(step.sem, step.at(n + 2))
                    eng.tensor_tensor(wt[:], wt[:], ranks, ALU.mult).then_inc(step.sem, 1)
                    eng.wait_ge(step.sem, step.at(n + 3))
                    eng.tensor_reduce(m[4][:], wt[:], AX.X, ALU.max).then_inc(step.sem, 1)
                    eng.wait_ge(step.sem, step.at(n + 4))
                    eng.tensor_tensor(one[i][:], wt[:], wide(m[4]), ALU.is_equal).then_inc(step.sem, 1)
                    eng.wait_ge(step.sem, step.at(n + 5))
                    n += 5
                    if i == 0:
                        eng.scalar_tensor_tensor(lg[:], one[0][:], NEG, lg[:], ALU.mult, ALU.add).then_inc(step.sem, 1)
                        n += 1
                        eng.wait_ge(step.sem, step.at(n))
                eng.tensor_tensor(chosen[:], one[0][:], one[1][:], ALU.add).then_inc(is_chosen.sem, 1)
                eng.tensor_tensor(m[2][:], m[1][:], m[0][:], ALU.subtract).then_inc(step.sem, 1)
                eng.wait_ge(exped.sem, exped.at(1))
                eng.tensor_scalar(m[3][:], m[2][:], 1.0, None, ALU.add).then_inc(step.sem, 1)
                eng.wait_ge(step.sem, step.at(13))
                eng.reciprocal(gates[0][:], m[3][:]).then_inc(step.sem, 1)
                eng.wait_ge(step.sem, step.at(14))
                eng.tensor_tensor(gates[1][:], m[2][:], gates[0][:], ALU.mult)

                n = 14

                def then(op):
                    nonlocal n
                    op.then_inc(step.sem, 1)
                    n += 1
                    eng.wait_ge(step.sem, step.at(n))

                eng.wait_ge(counted.sem, counted.at(1))
                psA_v = psA[:].rearrange("p (t e) -> p t e", e=E)
                then(eng.tensor_copy(seen[0][:], psA_v))
                for k in range(SCAN):
                    old, new, far = seen[k % 2], seen[(k + 1) % 2], 1 << k
                    then(eng.tensor_copy(new[:, 0:far, :], old[:, 0:far, :]))
                    then(eng.tensor_tensor(new[:, far:NT, :], old[:, far:NT, :], old[:, 0:NT - far, :], ALU.add))
                total = seen[SCAN % 2]
                then(eng.tensor_tensor(place[:], total[:], psA_v, ALU.subtract))
                then(eng.tensor_tensor(place[:], place[:], psN[:].rearrange("p (t e) -> p t e", e=E), ALU.add))
                then(eng.tensor_tensor(size_over[:], total[:, NT - 1, :].unsqueeze(2).to_broadcast([P, E, TIMES]),
                                       sizes[:], ALU.is_gt))
                then(eng.tensor_reduce(blocks_of[:], size_over[:], AX.X, ALU.add))
                then(eng.tensor_tensor(earlier[:], blocks_of[:].unsqueeze(1).to_broadcast([P, E, E]), behind[:],
                                       ALU.mult))
                then(eng.tensor_reduce(first[:], earlier[:], AX.X, ALU.add))
                then(eng.tensor_tensor(last[:], first[:], blocks_of[:], ALU.add))
                then(eng.tensor_tensor(past[:], number[:], last[:].unsqueeze(1).to_broadcast([P, NB, E]), ALU.is_ge))
                then(eng.tensor_reduce(owner[:], past[:], AX.X, ALU.add))
                then(eng.tensor_scalar(owner[:], owner[:], float(E - 1), None, ALU.min))
                then(eng.tensor_copy(block_expert[:], owner[0:1, :]))
                then(eng.tensor_scalar(first[:], first[:], float(BS), 2.0 * BS, ALU.mult, ALU.add))
                then(eng.tensor_tensor(place[:], place[:], first[:].unsqueeze(1).to_broadcast([P, NT, E]), ALU.add))
                for i in range(2):
                    then(eng.tensor_tensor(one[i][:], one[i][:], place[:], ALU.mult))
                    then(eng.tensor_reduce(dest[:, i, :], one[i][:], AX.X, ALU.add))
                then(eng.tensor_copy(slots[:], dest[:]))
                assert n == step.total


def dispatch_phase(nc, signals, name, x, moments, slots, Xs):
    SET = 4
    mean, rstd = moments
    with Phase(nc, signals, name) as ph:
        rows = [[ph.sb(f"row{u}_{j}", [P, D]) for j in range(SET)] for u in range(2)]
        index = [ph.sb(f"index{u}", [P, 2, SET], U32) for u in range(2)]
        ready = ph.sig("rows_ready", NT // SET)
        begun = ph.sig("set_begun", NT // SET)
        sent = [ph.sig(f"rows_sent{u}", 16 * 2 * SET * (NT // SET // 2)) for u in range(2)]
        ALL = 16 * 2 * SET
        with nc.Block() as block:
            @block.vector
            def _(eng):
                def fill(pair, u):
                    eng.tensor_copy(index[u][:], slots[:, :, bass.ds((pair * 2 + u) * SET, SET)])
                    for j in range(SET):
                        t = (pair * 2 + u) * SET + j
                        op = eng.tensor_scalar(rows[u][j][:], x[:, t, :], mean[:, bass.ds(t, 1)],
                                               rstd[:, bass.ds(t, 1)], ALU.subtract, ALU.mult)
                    op.then_inc(ready.sem, 1)

                for u in range(2):
                    fill(0, u)
                with eng.Fori(0, NT // SET // 2 - 1) as pair:
                    for u in range(2):
                        eng.wait_ge(sent[u].sem, sent[u].at(pair * ALL + ALL))
                        fill(pair + 1, u)

            @block.gpsimd
            def _(eng):
                with eng.Fori(0, NT // SET // 2) as pair:
                    for u in range(2):
                        eng.wait_ge(ready.sem, ready.at(pair * 2 + (u + 1)))
                        eng.sem_inc(begun.sem, 1)
                        for j in range(SET):
                            for i in range(2):
                                eng.indirect_dma_start(Xs[:], bass.IndirectOffsetOnAxis(index[u][:, i, j:j + 1], 0),
                                                       rows[u][j][:], None).then_inc(sent[u].sem, 16)
                for u in range(2):
                    eng.wait_ge(sent[u].sem, sent[u].at(sent[u].total))


def expert_blocks_phase(nc, signals, name, Xs, Ys, block_expert, cols, w_1, w_2, b_1, b_2, func, consts):
    TS = BS // P
    UNROLL = 2
    with Phase(nc, signals, name) as ph:
        w1 = [ph.sb(f"w1{v}", [P, KT, FF]) for v in range(2)]
        w2 = [ph.sb(f"w2{v}", [P, FT, D]) for v in range(2)]
        b1 = [ph.sb(f"b1{v}", [P, FT]) for v in range(2)]
        b2 = [ph.sb(f"b2{v}", [P, D]) for v in range(2)]
        rows = [ph.sb(f"rows{v}", [P, TS, D]) for v in range(2)]
        h = [ph.sb(f"h{v}", [P, KT, BS]) for v in range(2)]
        h1 = [ph.sb(f"h1{v}", [P, FT, BS]) for v in range(2)]
        y = [ph.sb(f"y{v}", [P, TS, D]) for v in range(2)]
        psX = ph.ps("psX", [P, KT, BS])
        ps1 = [ph.ps(f"ps1{i}", [P, 512]) for i in range(4)]
        ps2 = [ph.ps(f"ps2{i}", [P, 512]) for i in range(TS)]
        loaded = [ph.sig(f"expert_loaded{v}", 64 * NB // 2) for v in range(2)]
        x_loaded = [ph.sig(f"rows_loaded{v}", 16 * (NB // 2 + 1 - v)) for v in range(2)]
        y_clear = ph.sig("outputs_cleared", 1)
        x_psum = ph.sig("rows_turned", 1 + NB + 1)
        h_ready = ph.sig("rows_scaled", NB + 1)
        h_psum = ph.sig("hidden_in_psum", NB * FT)
        h1_ready = ph.sig("hidden_ready", 4 + NB * FT)
        y_psum = ph.sig("output_in_psum", 2 * TS + NB * TS)
        y_ready = ph.sig("output_ready", 2 * TS + NB * TS)
        y_stored = [ph.sig(f"output_stored{v}", 16 * (NB // 2 + 1)) for v in range(2)]

        def each_block(eng, body):
            with eng.Fori(0, NB // UNROLL) as group:
                for v in range(UNROLL):
                    body(group * UNROLL + v, v)

        def load_rows(eng, b, v):
            eng.dma_start(rows[v][:], Xs[bass.ds((b + 2) * BS, BS), :].rearrange("(j p) d -> p j d", p=P))\
               .then_inc(x_loaded[v].sem, 16)

        def store_output(eng, b, v):
            eng.dma_start(Ys[bass.ds(b * BS, BS), :].rearrange("(j p) d -> p j d", p=P), y[v][:])\
               .then_inc(y_stored[v].sem, 16)

        with nc.Block() as block:
            @block.sync
            def _(eng):
                load_rows(eng, 0, 0)
                eng.wait_ge(y_clear.sem, y_clear.at(1))

                def body(b, v):
                    e = eng.value_load(block_expert[0:1, bass.ds(b, 1)], min_val=0, max_val=E - 1)
                    eng.wait_ge(x_psum.sem, x_psum.at(b + 1))
                    eng.wait_ge(y_ready.sem, y_ready.at(b * TS + TS))
                    sel = bass.ds(e, 1)
                    eng.dma_start(w1[v][:], w_1[sel].rearrange("e (k p) n -> p (e k) n", p=P)).then_inc(loaded[v].sem, 16)
                    eng.dma_start(w2[v][:], w_2[sel].rearrange("e (k p) n -> p (e k) n", p=P)).then_inc(loaded[v].sem, 16)
                    eng.dma_start(b1[v][:], b_1[sel].rearrange("e p m -> p (e m)")).then_inc(loaded[v].sem, 16)
                    eng.dma_start(b2[v][:], b_2[sel, :].to_broadcast([P, D])).then_inc(loaded[v].sem, 16)
                    load_rows(eng, b + 1, (v + 1) % 2)
                    store_output(eng, b, v)

                each_block(eng, body)
                for v in range(2):
                    eng.wait_ge(y_ready.sem, y_ready.at((NB + v) * TS + TS))
                    store_output(eng, NB + v, v)
                for v in range(2):
                    eng.wait_ge(y_stored[v].sem, y_stored[v].at(y_stored[v].total))

            @block.gpsimd
            def _(eng):
                eng.memset(y[0][:], 0.0)
                eng.memset(y[1][:], 0.0).then_inc(y_clear.sem, 1)

            @block.tensor
            def _(eng):
                def turn_rows(b, v):
                    eng.wait_ge(x_loaded[v].sem, x_loaded[v].at((b - v) * (16 // UNROLL) + 16))
                    for k in range(KT):
                        for j in range(TS):
                            mm = eng.transpose(psX[:, k, j * P:(j + 1) * P], rows[v][:, j, k * P:(k + 1) * P],
                                               consts["ident"][:])
                    mm.then_inc(x_psum.sem, 1)

                eng.sem_inc(y_psum.sem, 2 * TS)
                eng.sem_inc(x_psum.sem, 1)
                turn_rows(0, 0)

                def body(b, v):
                    eng.wait_ge(loaded[v].sem, loaded[v].at((b - v) * (64 // UNROLL) + 64))
                    eng.wait_ge(h_ready.sem, h_ready.at(b + 1))
                    for m in range(FT):
                        eng.wait_ge(h1_ready.sem, h1_ready.at(b * FT + (m + 1)))
                        for k in range(KT):
                            mm = eng.matmul(ps1[m % 4][:, 0:BS], w1[v][:, k, m * P:(m + 1) * P], h[v][:, k, :],
                                            start=(k == 0), stop=(k == KT - 1))
                        mm.then_inc(h_psum.sem, 1)
                    turn_rows(b + 1, (v + 1) % 2)
                    for j in range(TS):
                        eng.wait_ge(y_ready.sem, y_ready.at(b * TS + (j + 1 + TS)))
                        for m in range(FT):
                            if j == 0:
                                eng.wait_ge(h1_ready.sem, h1_ready.at(b * FT + (m + 1 + 4)))
                            mm = eng.matmul(ps2[j][:, 0:D], h1[v][:, m, j * P:(j + 1) * P], w2[v][:, m, :],
                                            start=(m == 0), stop=(m == FT - 1))
                        mm.then_inc(y_psum.sem, 1)

                each_block(eng, body)

            @block.scalar
            def _(eng):
                eng.sem_inc(h1_ready.sem, 4)

                def body(b, v):
                    eng.wait_ge(y_psum.sem, y_psum.at(b * TS + TS))
                    for m in range(FT):
                        eng.wait_ge(h_psum.sem, h_psum.at(b * FT + (m + 1)))
                        eng.activation(h1[v][:, m, :], ps1[m % 4][:, 0:BS], func, bias=b1[v][:, m:m + 1], scale=1.0)\
                           .then_inc(h1_ready.sem, 1)

                each_block(eng, body)

            @block.vector
            def _(eng):
                def scale_rows(b, v):
                    eng.wait_ge(x_psum.sem, x_psum.at(b + 2))
                    for k in range(KT):
                        op = eng.tensor_scalar(h[v][:, k, :], psX[:, k, :], cols[0][:, k:k + 1], cols[1][:, k:k + 1],
                                               ALU.mult, ALU.add)
                    op.then_inc(h_ready.sem, 1)

                eng.sem_inc(y_ready.sem, 2 * TS)
                for v in range(2):
                    eng.wait_ge(y_clear.sem, y_clear.at(1))
                scale_rows(0, 0)

                def body(b, v):
                    scale_rows(b + 1, (v + 1) % 2)
                    eng.wait_ge(y_stored[v].sem, y_stored[v].at((b - v) * (16 // UNROLL) + 16))
                    for j in range(TS):
                        eng.wait_ge(y_psum.sem, y_psum.at(b * TS + (j + 1 + 2 * TS)))
                        eng.tensor_tensor(y[v][:, j, :], ps2[j][:, 0:D], b2[v][:], ALU.add).then_inc(y_ready.sem, 1)

                each_block(eng, body)


def combine_phase(nc, signals, name, x, gates, slots, Ys):
    SET = 4
    with Phase(nc, signals, name) as ph:
        rows = [[[ph.sb(f"row{u}_{i}_{j}", [P, D]) for j in range(SET)] for i in range(2)] for u in range(2)]
        index = [ph.sb(f"index{u}", [P, 2, SET], U32) for u in range(2)]
        ALL = 16 * 2 * SET
        pairs = NT // SET // 2
        indexed = ph.sig("index_ready", NT // SET)
        begun = ph.sig("set_begun", NT // SET)
        fetched = [ph.sig(f"rows_fetched{u}", ALL * pairs) for u in range(2)]
        added = ph.sig("first_expert_added", NT)
        used = ph.sig("rows_used", 2 + NT // SET)
        with nc.Block() as block:
            @block.vector
            def _(eng):
                eng.sem_inc(used.sem, 2)

                def indices(pair, u):
                    eng.tensor_copy(index[u][:], slots[:, :, bass.ds((pair * 2 + u) * SET, SET)])\
                       .then_inc(indexed.sem, 1)

                def add(pair, u):
                    eng.wait_ge(fetched[u].sem, fetched[u].at(pair * ALL + ALL))
                    for i in range(2):
                        for j in range(SET):
                            t = (pair * 2 + u) * SET + j
                            if i:
                                eng.wait_ge(added.sem, added.at(t + 1))
                            op = eng.scalar_tensor_tensor(x[:, t, :], rows[u][i][j][:], gates[i][:, bass.ds(t, 1)],
                                                          x[:, t, :], ALU.mult, ALU.add)
                            if i == 0:
                                op.then_inc(added.sem, 1)
                    op.then_inc(used.sem, 1)

                for u in range(2):
                    indices(0, u)
                with eng.Fori(0, pairs - 1) as pair:
                    for u in range(2):
                        add(pair, u)
                        indices(pair + 1, u)
                for u in range(2):
                    add(pairs - 1, u)

            @block.gpsimd
            def _(eng):
                with eng.Fori(0, pairs) as pair:
                    for u in range(2):
                        eng.wait_ge(used.sem, used.at(pair * 2 + (u + 1)))
                        eng.wait_ge(indexed.sem, indexed.at(pair * 2 + (u + 1)))
                        eng.sem_inc(begun.sem, 1)
                        for j in range(SET):
                            for i in range(2):
                                eng.indirect_dma_start(rows[u][i][j][:], None, Ys[:],
                                                       bass.IndirectOffsetOnAxis(index[u][:, i, j:j + 1], 0))\
                                   .then_inc(fetched[u].sem, 16)


def feed_forward_phase(nc, signals, name, hT, x, rows, tokens, w_1, w_2, b_1, b_2, func):
    cw = min(CH, tokens)
    chunks = tokens // cw
    tpc = cw // rows
    UC = min(2, chunks)
    tiles = tokens // rows
    with Phase(nc, signals, name) as ph:
        w1 = ph.sb("w1", [P, KT, FF])
        w2 = ph.sb("w2", [P, FT, D])
        b1 = ph.sb("b1", [P, FT])
        b2 = ph.sb("b2", [P, D])
        h1 = [ph.sb(f"h1{u}", [P, FT, cw]) for u in range(UC)]
        ps1 = [ph.ps(f"ps1{i}", [P, CH]) for i in range(4)]
        ps2 = [ph.ps(f"ps2{i}", [P, 512]) for i in range(2)]
        loaded = ph.sig("weights_loaded", 32)
        w2_loaded = ph.sig("output_weights_loaded", 32)
        H_FREE, Y_FREE, OUT_FREE = 4, 2, UC * tpc
        h_psum = ph.sig("hidden_in_psum", chunks * FT)
        h_ready = ph.sig("hidden_ready", H_FREE + chunks * FT)
        x_biased = ph.sig("bias_added", tiles)
        y_psum = ph.sig("output_in_psum", OUT_FREE + tiles)
        y_added = ph.sig("output_added", Y_FREE + tiles)

        def each_chunk(eng, body):
            if chunks == UC:
                for u in range(UC):
                    body(u, u)
            else:
                with eng.Fori(0, chunks // UC) as pair:
                    for u in range(UC):
                        body(pair * UC + u, u)

        with nc.Block() as block:
            @block.sync
            def _(eng):
                eng.dma_start(w1[:], w_1[0].rearrange("(k p) n -> p k n", p=P)).then_inc(loaded.sem, 16)
                eng.dma_start(b1[:], b_1[0]).then_inc(loaded.sem, 16)
                eng.dma_start(w2[:], w_2[0].rearrange("(k p) n -> p k n", p=P)).then_inc(w2_loaded.sem, 16)
                eng.dma_start(b2[:], b_2.partition_broadcast(P)).then_inc(w2_loaded.sem, 16)

            @block.tensor
            def _(eng):
                eng.sem_inc(y_psum.sem, OUT_FREE)
                eng.wait_ge(loaded.sem, loaded.at(32))

                def body(c, u):
                    for m in range(FT):
                        eng.wait_ge(h_ready.sem, h_ready.at(c * FT + (m + 1)))
                        for k in range(KT):
                            mm = eng.matmul(ps1[m % 4][:, 0:cw], w1[:, k, m * P:(m + 1) * P],
                                            hT[:, k, bass.ds(c * cw, cw)], start=(k == 0), stop=(k == KT - 1))
                        mm.then_inc(h_psum.sem, 1)
                    eng.wait_ge(w2_loaded.sem, w2_loaded.at(32))
                    for j in range(tpc):
                        eng.wait_ge(y_added.sem, y_added.at(c * tpc + (j + 1)))
                        for m in range(FT):
                            if j == 0:
                                eng.wait_ge(h_ready.sem, h_ready.at(c * FT + (m + 1 + H_FREE)))
                            mm = eng.matmul(ps2[j % 2][0:rows, 0:D], h1[u][:, m, j * rows:(j + 1) * rows],
                                            w2[:, m, :], start=(m == 0), stop=(m == FT - 1))
                        mm.then_inc(y_psum.sem, 1)

                each_chunk(eng, body)

            @block.scalar
            def _(eng):
                eng.sem_inc(h_ready.sem, H_FREE)

                def body(c, u):
                    eng.wait_ge(y_psum.sem, y_psum.at(c * tpc + tpc))
                    for m in range(FT):
                        eng.wait_ge(h_psum.sem, h_psum.at(c * FT + (m + 1)))
                        eng.activation(h1[u][:, m, :], ps1[m % 4][:, 0:cw], func, bias=b1[:, m:m + 1], scale=1.0)\
                           .then_inc(h_ready.sem, 1)

                each_chunk(eng, body)

            @block.gpsimd
            def _(eng):
                eng.wait_ge(w2_loaded.sem, w2_loaded.at(32))
                with eng.Fori(0, tiles // 4) as quad:
                    for i in range(4):
                        xt = x[0:rows, quad * 4 + i, :]
                        eng.tensor_tensor(xt, xt, b2[0:rows, :], ALU.add).then_inc(x_biased.sem, 1)

            @block.vector
            def _(eng):
                eng.sem_inc(y_added.sem, Y_FREE)

                def body(c, u):
                    for j in range(tpc):
                        eng.wait_ge(x_biased.sem, x_biased.at(c * tpc + (j + 1)))
                        eng.wait_ge(y_psum.sem, y_psum.at(c * tpc + (j + 1 + OUT_FREE)))
                        xt = x[0:rows, c * tpc + j, :]
                        eng.tensor_tensor(xt, xt, ps2[j % 2][0:rows, 0:D], ALU.add).then_inc(y_added.sem, 1)

                each_chunk(eng, body)


def build(nc, d, places, out):
    with ExitStack() as ctx:
        def sb(name, shape, dt=F32):
            return ctx.enter_context(nc.sbuf_tensor(name, shape, dt))

        signals = Signals(nc, ctx)
        x = sb("x_res", [P, NT, D])
        hT = sb("activationsT", [P, KT, NT * P])
        zeros = sb("zeros", [P, ZERO])
        Qd = nc.dram_tensor("q_pieces", [3, B * D + 2 * DK, SQ], BF16)
        Kd = nc.dram_tensor("k_pieces", [3, B * D + 2 * DK, SQ], BF16)
        Vd = nc.dram_tensor("v_pieces", [B * H + 2, P, 3 * DK, TB], BF16)
        Od = nc.dram_tensor("context_pieces", [3, 2 * DK + B * D, SQ], F32)
        SLOTS = (NB + 3) * BS
        Xs = nc.dram_tensor("tokens_by_expert", [SLOTS, D], F32)
        Ys = nc.dram_tensor("outputs_by_expert", [SLOTS - BS, D], F32)
        Dd = nc.dram_tensor("denominators", [2 + B * H, SQ], F32)
        cT = sb("contextT", [P, KT, B * SC])
        consts = {"ident": sb("ident", [P, P]), "ones": sb("ones", [1, P]), "head_rows": sb("head_rows", [P, HT]),
                  "minus_half": sb("minus_half", [P, NT]),
                  "identb": sb("identb", [P, P], BF16), "spread": sb("spread", [B * H, B * KT, P])}
        xe = sb("encoder", [SC, B, D])
        xd = d["x"].rearrange("b s d -> (b s) d").rearrange("(t p) d -> p t d", p=P)
        packed = sb("packed_columns", [P, d["columns"].shape[1]])
        start_loaded = signals("start_loaded", 16 * 10)
        with nc.Block() as block:
            @block.sync
            def _(eng):
                eng.dma_start(packed[:], d["columns"]).then_inc(start_loaded.sem, 16)
                eng.dma_start(consts["ident"][:], d["ident"]).then_inc(start_loaded.sem, 16)
                eng.dma_start(consts["minus_half"][:], d["minus_half"]).then_inc(start_loaded.sem, 16)
                eng.dma_start(consts["ones"][:], d["ones"]).then_inc(start_loaded.sem, 16)
                eng.dma_start(consts["head_rows"][:], d["head_rows"]).then_inc(start_loaded.sem, 16)
                eng.dma_start(cT[:], d["ctxT"].rearrange("(k p) c -> p k c", p=P)).then_inc(start_loaded.sem, 16)
                eng.dma_start(hT[:], d["xT"].rearrange("(k p) t -> p k t", p=P)).then_inc(start_loaded.sem, 16)
                eng.dma_start(x[:], xd).then_inc(start_loaded.sem, 16)
                eng.dma_start(consts["spread"][:], d["spread"]).then_inc(start_loaded.sem, 16)
                eng.dma_start(xe[:], d["ctx"].rearrange("b c d -> c b d")).then_inc(start_loaded.sem, 16)
                eng.wait_ge(start_loaded.sem, start_loaded.at(16 * 10))

            @block.vector
            def _(eng):
                eng.wait_ge(start_loaded.sem, start_loaded.at(16 * 10))
                eng.tensor_copy(consts["identb"][:], consts["ident"][:])
                eng.memset(zeros[:], 0.0)
        signals.phase_over()

        def cols(name):
            at, n = places[name]
            return packed[:, at:at + n]

        def weights(name):
            return d[name].rearrange("(k p) n -> p k n", p=P)

        for table in ("rank", "before", "every", "sizes", "behind", "number"):
            consts[table] = d[table]

        def cross(name, sT, x_to, rows, tiles, hT_from, bias=None, rope=None, meanwhile=None,
                  on_gpsimd=None):
            pair = range(2) if rope else range(1)
            tag = ("", "_turned")
            with ExitStack() as heads:
                Kbd = heads.enter_context(nc.sbuf_tensor(name + "_Kbd", [P, B, KT, HT * SC], F32))
                Vbd = heads.enter_context(nc.sbuf_tensor(name + "_Vbd", [P, B, H // 2, PW], F32))
                context_heads_phase(nc, signals, name + "kv", sT, [weights(name + "_wk" + tag[r]) for r in pair],
                                    weights(name + "_wv"), [cols(name + "_bk" + tag[r]) for r in pair],
                                    d[name + "_bv"], consts, Kbd, Vbd, rope=rope and rope[1])
                cross_attention_phase(nc, signals, name + "at", hT_from, x_to, rows, tiles,
                                      [weights(name + "_wq" + tag[r]) for r in pair],
                                      [cols(name + "_bq" + tag[r]) for r in pair], weights(name + "_wo"),
                                      d[name + "_bo"], Kbd, Vbd, consts, bias=bias, rope=rope and rope[0],
                                      meanwhile=meanwhile, on_gpsimd=on_gpsimd)

        def self_attention(name, causal, near=None, rope=None):
            pair = range(2) if rope else range(1)
            tag = ("", "_turned")
            self_heads_phase(nc, signals, name + "qkv", hT, [weights(name + "_wq" + tag[r]) for r in pair],
                             [weights(name + "_wk" + tag[r]) for r in pair], weights(name + "_wv"),
                             [cols(name + "_bq" + tag[r]) for r in pair],
                             [cols(name + "_bk" + tag[r]) for r in pair], d[name + "_bv"], consts,
                             Qd, Kd, Vd, rope=rope)
            self_attention_phase(nc, signals, name + "at", Qd, Kd, Vd, Od, Dd, consts, causal, near)
            output_phase(nc, signals, name + "out", Od, Dd, x, weights(name + "_wo"), d[name + "_bo"], consts)

        def norm(name):
            return cols(name + "_g"), cols(name + "_b")

        def clear_slots(eng):
            runs = SLOTS * D // P // ZERO
            slots_cleared = signals("slots_cleared", 16)
            eng.dma_start(Xs.rearrange("(p r) d -> p (r d)", p=P).rearrange("p (n c) -> p n c", c=ZERO),
                          zeros[:].unsqueeze(1).to_broadcast([P, runs, ZERO])).then_inc(slots_cleared.sem, 16)
            eng.wait_ge(slots_cleared.sem, slots_cleared.at(16))

        cross("L0", cT, x, P, TB, hT, meanwhile=clear_slots)
        output_norm_phase(nc, signals, "L0ln", x, consts, d["L0_gamma"], d["L0_beta"], 1e-5)

        transpose_phase(nc, signals, "L1t1", x, hT, consts, P, NT, norm("L1_n1"))
        self_attention("L1sa", False)
        transpose_phase(nc, signals, "L1t2", x, hT, consts, P, NT, norm("L1_n2"))
        tables = ctx.enter_context(ExitStack())
        q_near = tables.enter_context(nc.sbuf_tensor("q_near", [P, H + 1, 2 * P], BF16))
        k_near = [tables.enter_context(nc.sbuf_tensor(f"k_near{i}", [P, H + 1, 2 * P], BF16)) for i in range(3)]
        with ExitStack() as normed:
            nT = normed.enter_context(nc.sbuf_tensor("L1_contextT", [P, KT, B * SC], F32))
            transpose_phase(nc, signals, "L1t3", xe, nT, consts, SC, B, norm("L1_nc"))
            cross("L1ca", nT, x, P, TB, hT,
                  on_gpsimd=lambda ph: near_blocks(ph, d["L2_rel_q"], d["L2_rel_k"], d["L2_rel_far"],
                                                   d["near_mask_q"], d["near_mask_k"], q_near, k_near))
        with ExitStack() as mixture:
            def kept(name, shape, dt=F32):
                return mixture.enter_context(nc.sbuf_tensor(name, shape, dt))

            moments = (kept("L1_mean", [P, NT]), kept("L1_rstd", [P, NT]))
            gates = [kept(f"gate{i}", [P, NT]) for i in range(2)]
            slots = kept("slots", [P, 2, NT], U32)
            block_expert = kept("block_expert", [1, NB], I32)
            transpose_phase(nc, signals, "L1t4", x, hT, consts, P, NT, norm("L1_n3"), moments=moments)
            router_phase(nc, signals, "L1r", hT, gates, slots, block_expert, weights("L1_wr"), d["L1_br"], consts)
            dispatch_phase(nc, signals, "L1d", x, moments, slots, Xs)
            expert_blocks_phase(nc, signals, "L1ff", Xs, Ys, block_expert, norm("L1_n3"), d["L1_w1"], d["L1_w2"],
                                d["L1_b1"], d["L1_b2"], ACT.Gelu, consts)
            combine_phase(nc, signals, "L1c", x, gates, slots, Ys)

        with ExitStack() as encoder:
            nT = encoder.enter_context(nc.sbuf_tensor("L2_contextT", [P, KT, B * SC], F32))
            transpose_phase(nc, signals, "L2e1", xe, nT, consts, SC, B, norm("L2_e1"), 1e-6)
            cross("L2e", nT, xe, SC, 1, nT, bias=(d["L2_enc_bias"], 1))
            transpose_phase(nc, signals, "L2e2", xe, nT, consts, SC, B, norm("L2_e2"), 1e-6)
            feed_forward_phase(nc, signals, "L2ef", nT, xe, SC, B * SC, d["L2e_w1"], d["L2e_w2"], d["L2e_b1"],
                               d["L2e_b2"], ACT.Relu)
            transpose_phase(nc, signals, "L2e3", xe, nT, consts, SC, B)
            transpose_phase(nc, signals, "L2t1", x, hT, consts, P, NT, norm("L2_n1"), 1e-6)
            self_attention("L2sa", True, near=(q_near, k_near, True, True))
            transpose_phase(nc, signals, "L2t2", x, hT, consts, P, NT, norm("L2_n2"), 1e-6)
            cross("L2ca", nT, x, P, TB, hT, bias=(d["L2_cross_bias"], 3))
        tables.close()
        transpose_phase(nc, signals, "L2t3", x, hT, consts, P, NT, norm("L2_n3"), 1e-6)
        feed_forward_phase(nc, signals, "L2ff", hT, x, P, NT * P, d["L2_w1"], d["L2_w2"], d["L2_b1"],
                           d["L2_b2"], ACT.Relu)

        with ExitStack() as rotary:
            turn = {}
            for part in ("q_cos", "q_sin", "k_cos", "k_sin"):
                turn[part] = rotary.enter_context(nc.sbuf_tensor("turn_" + part, [P, SQ], F32))
            mask = [rotary.enter_context(nc.sbuf_tensor("diagonal_" + part, [P, P], BF16)) for part in "qk"]
            with Phase(nc, signals, "L3l") as ph:
                mask_f = [ph.sb("mask_" + part, [P, P]) for part in "qk"]
                loaded = ph.sig("weights_loaded", 16 * 6)
                with nc.Block() as block:
                    @block.sync
                    def _(eng):
                        for part, tile in turn.items():
                            eng.dma_start(tile[:], d["turn_" + part]).then_inc(loaded.sem, 16)
                        eng.dma_start(mask_f[0][:], d["near_mask_q"][:, P:2 * P]).then_inc(loaded.sem, 16)
                        eng.dma_start(mask_f[1][:], d["near_mask_k"][:, 0:P]).then_inc(loaded.sem, 16)

                    @block.vector
                    def _(eng):
                        eng.wait_ge(loaded.sem, loaded.at(16 * 6))
                        for i in range(2):
                            eng.tensor_copy(mask[i][:], mask_f[i][:])
            rope = ((turn["q_cos"], turn["q_sin"]), (turn["k_cos"], turn["k_sin"]))
            transpose_phase(nc, signals, "L3t1", x, hT, consts, P, NT, norm("L3_n1"))
            self_attention("L3sa", True, near=(mask[0], [mask[1]], False, False), rope=rope)
            transpose_phase(nc, signals, "L3t2", x, hT, consts, P, NT, norm("L3_n2"))
            cross("L3ca", cT, x, P, TB, hT, rope=rope)
        transpose_phase(nc, signals, "L3t3", x, hT, consts, P, NT, norm("L3_n3"))
        feed_forward_phase(nc, signals, "L3ff", hT, x, P, NT * P, d["L3_w1"], d["L3_w2"], d["L3_b1"],
                           d["L3_b2"], ACT.Gelu_apprx_tanh)

        written = signals("output_written", 16)
        with nc.Block() as block:
            @block.sync
            def _(eng):
                eng.dma_start(out.rearrange("b s d -> (b s) d").rearrange("(t p) d -> p t d", p=P), x[:])\
                   .then_inc(written.sem, 16)
                eng.wait_ge(written.sem, written.at(16))


def lay_out(inp):
    a, places, packed = {}, {}, []

    def columns(name, v):
        v = v.reshape(-1, P).T
        places[name] = (sum(c.shape[1] for c in packed), v.shape[1])
        packed.append(v)

    a["x"] = inp["x"]
    a["xT"] = np.ascontiguousarray(inp["x"].reshape(B * SQ, D).T)
    a["ctxT"] = np.ascontiguousarray(inp["ctx_1024"].reshape(B * SC, D).T)
    a["ident"] = np.eye(P, dtype=np.float32)
    a["minus_half"] = np.full((P, NT), -0.5, np.float32)
    a["ones"] = np.ones((1, P), np.float32)
    a["head_rows"] = np.repeat(np.eye(HT, dtype=np.float32), DK, axis=0)

    def packed_attention(name, w, b, wo, bo):
        for i, part in enumerate("qkv"):
            a[f"{name}_w{part}"] = np.ascontiguousarray(w[i * D:(i + 1) * D].T)
            rows = b[i * D:(i + 1) * D]
            if part == "v":
                a[f"{name}_bv"] = rows.reshape(1, D)
            else:
                columns(f"{name}_b{part}", rows)
        a[f"{name}_wo"] = np.ascontiguousarray(wo.T)
        a[f"{name}_bo"] = bo.reshape(1, D)

    packed_attention("L0", inp["L0_xattn_W_qkv"], inp["L0_xattn_b_qkv"], inp["L0_xattn_W_o"], inp["L0_xattn_b_o"])
    a["L0_gamma"] = inp["L0_xattn_ln_gamma"]
    a["L0_beta"] = inp["L0_xattn_ln_beta"]
    a["ctx"] = inp["ctx_1024"]
    a["spread"] = np.repeat(np.eye(B * H, dtype=np.float32), DK, axis=1).reshape(B * H, B * KT, P)
    a["rank"] = np.tile(np.arange(E, 0, -1, dtype=np.float32), (P, 1))

    a["before"] = np.triu(np.ones((P, P), np.float32), 1)
    a["every"] = np.ones((P, P), np.float32)
    a["sizes"] = np.tile(np.arange(NT * P // BS, dtype=np.float32) * BS, (P, E, 1))
    a["behind"] = np.tile(np.tril(np.ones((E, E), np.float32), -1), (P, 1, 1))
    a["number"] = np.tile(np.arange(NB, dtype=np.float32)[:, None], (P, 1, E))

    def norm(name, g, b):
        columns(name + "_g", inp[g])
        columns(name + "_b", inp[b])

    def feed_forward(name, w1, b1, w2, b2):
        a[name + "_w1"], a[name + "_w2"] = np.ascontiguousarray(w1), np.ascontiguousarray(w2)
        a[name + "_b1"] = np.ascontiguousarray(b1.reshape(-1, FT, P).transpose(0, 2, 1))
        a[name + "_b2"] = b2.reshape(-1, D)

    L = "L1_xattn_"
    norm("L1_n1", L + "sa_ln_g", L + "sa_ln_b")
    norm("L1_n2", L + "ca_q_ln_g", L + "ca_q_ln_b")
    norm("L1_nc", L + "ca_kv_ln_g", L + "ca_kv_ln_b")
    norm("L1_n3", L + "moe_ln_g", L + "moe_ln_b")
    packed_attention("L1sa", *(inp[L + n] for n in ("sa_in_w", "sa_in_b", "sa_out_w", "sa_out_b")))
    packed_attention("L1ca", *(inp[L + n] for n in ("ca_in_w", "ca_in_b", "ca_out_w", "ca_out_b")))
    a["L1_wr"] = np.ascontiguousarray(inp[L + "router_w"].T)
    a["L1_br"] = inp[L + "router_b"].reshape(E, 1)
    feed_forward("L1", inp[L + "e_fc1_w"].transpose(0, 2, 1), inp[L + "e_fc1_b"], inp[L + "e_fc2_w"].transpose(0, 2, 1),
                 inp[L + "e_fc2_b"])

    L = "L2_xattn_"
    norm("L2_e1", L + "enc_n1_s", L + "enc_n1_b")
    norm("L2_e2", L + "enc_n2_s", L + "enc_n2_b")
    for i in "123":
        norm("L2_n" + i, L + f"dec_n{i}_s", L + f"dec_n{i}_b")
    packed_attention("L2e", *(inp[L + n] for n in ("enc_in_w", "enc_in_b", "enc_out_w", "enc_out_b")))
    packed_attention("L2sa", *(inp[L + n] for n in ("dec_sa_in_w", "dec_sa_in_b", "dec_sa_out_w", "dec_sa_out_b")))
    packed_attention("L2ca", *(inp[L + n] for n in ("dec_ca_in_w", "dec_ca_in_b", "dec_ca_out_w", "dec_ca_out_b")))
    for name, part in (("L2e", "enc"), ("L2", "dec")):
        feed_forward(name, inp[L + part + "_ff1_w"].T[None], inp[L + part + "_ff1_b"],
                     inp[L + part + "_ff2_w"].T[None], inp[L + part + "_ff2_b"])

    def rows_of(queries, keys):
        ahead = keys - queries
        return np.where(ahead < 0, np.minimum(-ahead, P - 1), np.minimum(ahead, P - 1) + P)

    def laid(table, queries, keys):
        return np.ascontiguousarray(table[rows_of(queries, keys)].transpose(0, 2, 1))

    at, to, near = np.arange(P)[:, None], np.arange(SC)[None, :], np.arange(2 * P)[None, :]
    a["L2_enc_bias"] = laid(inp[L + "enc_rel"], at[0:SC], to).reshape(SC, 1, H * SC)
    a["L2_cross_bias"] = np.ascontiguousarray(np.stack(
        [laid(inp[L + "dec_rel_cross"], at + P * j, to).reshape(P, H * SC) for j in range(3)], axis=1))
    rel = inp[L + "dec_rel_self"][:, list(range(H)) + [0]]
    a["L2_rel_q"] = laid(rel, at + P, near)
    a["L2_rel_k"] = laid(rel, near, at)
    a["L2_rel_far"] = np.ascontiguousarray(rel[P - 1])
    a["near_mask_q"] = np.where(near > at + P, MASKED, 0.0).astype(np.float32)
    a["near_mask_k"] = np.where(at > near, MASKED, 0.0).astype(np.float32)

    L = "L3_xattn_"
    for i in "123":
        norm("L3_n" + i, L + f"ln{i}_g", L + f"ln{i}_b")
    swap = (np.arange(D) // DK) * DK + (np.arange(D) % DK + DK // 2) % DK
    for part in ("sa", "ca"):
        for w in "qk":
            weight, bias = inp[L + f"{part}_w{w}"], inp[L + f"{part}_b{w}"]
            a[f"L3{part}_w{w}"] = weight
            a[f"L3{part}_w{w}_turned"] = np.ascontiguousarray(weight[:, swap])
            columns(f"L3{part}_b{w}", bias)
            columns(f"L3{part}_b{w}_turned", bias[swap])
        a[f"L3{part}_wv"], a[f"L3{part}_bv"] = inp[L + part + "_wv"], inp[L + part + "_bv"].reshape(1, D)
        a[f"L3{part}_wo"], a[f"L3{part}_bo"] = inp[L + part + "_wo"], inp[L + part + "_bo"].reshape(1, D)
    frequency = np.float32(1.0) / np.float32(10000.0) ** (np.arange(0, DK, 2, dtype=np.float32) / np.float32(DK))
    angle = np.outer(np.arange(SQ, dtype=np.float32), frequency).astype(np.float32)
    cos = np.tile(np.cos(angle).T, (2 * HT, 1)).astype(np.float32)
    sin = np.tile(np.concatenate([-np.sin(angle), np.sin(angle)], axis=1).T, (HT, 1)).astype(np.float32)
    a["turn_k_cos"], a["turn_k_sin"] = cos, sin
    a["turn_q_cos"], a["turn_q_sin"] = cos * np.float32(SCALE), sin * np.float32(SCALE)
    feed_forward("L3", inp[L + "fc1_w"][None], inp[L + "fc1_b"], inp[L + "fc2_w"][None], inp[L + "fc2_b"])
    a["columns"] = np.ascontiguousarray(np.concatenate(packed, axis=1))
    return a, places


def kernel(**inputs):
    import concourse.bacc as bacc
    from concourse.bass_utils import run_bass_kernel_spmd

    nc = bacc.Bacc("TRN2", target_bir_lowering=False, num_devices=1)
    arrays, places = lay_out({k: np.asarray(v) for k, v in inputs.items()})
    d = {}
    for name, a in arrays.items():
        d[name] = nc.dram_tensor("in_" + name, a.shape, mybir.dt.from_np(a.dtype), kind="ExternalInput").ap()
    out = nc.dram_tensor("out", (B, SQ, D), F32, kind="ExternalOutput").ap()
    build(nc, d, places, out)
    r = run_bass_kernel_spmd(nc, [{"in_" + k: v for k, v in arrays.items()}], core_ids=[0])
    return r.results[0]["out"]
```
